# Optimizing a Trainium2 kernel written in Bass

```python
import numpy as np
import jax
import jax.numpy as jnp

def _softmax(x, axis=-1):
    return jax.nn.softmax(x, axis=axis)

def _gelu(x):
    return jax.nn.gelu(x, approximate=True)

def _silu(x):
    return jax.nn.silu(x)

def _sigmoid(x):
    return jax.nn.sigmoid(x)

def _layernorm(x, axis=-1, eps=1e-05):
    m = jnp.mean(x, axis=axis, keepdims=True)
    v = jnp.var(x, axis=axis, keepdims=True)
    return (x - m) / jnp.sqrt(v + eps)

def _scatter_add(tgt, idx, src, axis=0):
    return tgt.at[idx].add(src)

def _segment_sum(src, seg, n):
    return jax.ops.segment_sum(src, seg, n)
kernel_name = 'mk_sandwich_d4_jaxref_r8_18dee2'

def setup_inputs(seed: int=0):
    np.random.seed(seed)
    _w = jnp.asarray

    def _L0_attn_setup():
        import jax, jax.numpy as jnp
        import numpy as np
        import math
        HIDDEN = 128
        N_HEADS = 16
        HEAD = HIDDEN // N_HEADS
        NEG_INF = -10000.0
        key = jax.random.key(seed)
        ks = jax.random.split(key, 5)
        B, S = (4, 256)
        x = jax.random.normal(ks[0], (B, S, HIDDEN), dtype=jnp.float32)
        sc = 1.0 / math.sqrt(HIDDEN)
        qkv_w = jax.random.normal(ks[1], (HIDDEN, 3 * HIDDEN), dtype=jnp.float32) * sc
        qkv_b = jnp.zeros((3 * HIDDEN,), dtype=jnp.float32)
        out_w = jax.random.normal(ks[2], (HIDDEN, HIDDEN), dtype=jnp.float32) * sc
        out_b = jnp.zeros((HIDDEN,), dtype=jnp.float32)
        return {'x': x, 'qkv_w': qkv_w, 'qkv_b': qkv_b, 'out_w': out_w, 'out_b': out_b}
    _L0_attn_in = _L0_attn_setup()

    def _L0_ffn_setup():
        import jax, jax.numpy as jnp
        import numpy as np
        H, I, E_ROUTED, TOP_K = (128, 352, 7, 2)
        B, S = (4, 256)

        def _expert(h, g, u, d):
            return jnp.einsum('...i,hi->...h', jax.nn.silu(h @ g.T) * (h @ u.T), d)
        key = jax.random.key(seed)
        ks = jax.random.split(key, 10)
        sc = 0.02
        return {'x': jax.random.normal(ks[0], (B, S, H), dtype=jnp.float32), 'sg': jax.random.normal(ks[1], (I, H), dtype=jnp.float32) * sc, 'su': jax.random.normal(ks[2], (I, H), dtype=jnp.float32) * sc, 'sd': jax.random.normal(ks[3], (H, I), dtype=jnp.float32) * sc, 'rg': jax.random.normal(ks[4], (E_ROUTED, I, H), dtype=jnp.float32) * sc, 'ru': jax.random.normal(ks[5], (E_ROUTED, I, H), dtype=jnp.float32) * sc, 'rd': jax.random.normal(ks[6], (E_ROUTED, H, I), dtype=jnp.float32) * sc, 'wr': jax.random.normal(ks[7], (E_ROUTED, H), dtype=jnp.float32) * sc, 'rb': jnp.zeros((E_ROUTED,), dtype=jnp.float32)}
    _L0_ffn_in = _L0_ffn_setup()

    def _L1_attn_setup():
        import jax, jax.numpy as jnp
        import numpy as np
        import math
        B, T, D = (2, 256, 128)
        N_HEADS = 16
        D_HEAD = D // N_HEADS

        def _rope_tables(t, d_head, dtype=jnp.float32):
            theta = 1.0 / 10000.0 ** (jnp.arange(0, d_head, 2, dtype=jnp.float32) / d_head)
            angles = jnp.outer(jnp.arange(t, dtype=jnp.float32), theta)
            angles = jnp.concatenate([angles, angles], axis=-1)
            return (jnp.cos(angles).astype(dtype), jnp.sin(angles).astype(dtype))

        def _rotate_half(x):
            half = x.shape[-1] // 2
            return jnp.concatenate([-x[..., half:], x[..., :half]], axis=-1)

        def _apply_rope(x, cos, sin):
            return x * cos[None, None] + _rotate_half(x) * sin[None, None]
        key = jax.random.key(seed)
        k1, k2, k3, k4 = jax.random.split(key, 4)
        s_in = 1.0 / math.sqrt(D)
        return {'x': jax.random.normal(k1, (B, T, D), dtype=jnp.float32), 'w_qkv': jax.random.normal(k2, (D, 3 * D), dtype=jnp.float32) * s_in, 'w_out': jax.random.normal(k3, (D, D), dtype=jnp.float32) * s_in, 'b_out': jax.random.normal(k4, (D,), dtype=jnp.float32) * 0.01}
    _L1_attn_in = _L1_attn_setup()

    def _L1_ffn_setup():
        import jax, jax.numpy as jnp
        import numpy as np
        B, S, H = (8, 512, 128)
        NAV = 128
        E = 8
        F = 2 * H
        key = jax.random.key(seed)
        ks = jax.random.split(key, 12)

        def w(k, shape, fan_in):
            return jax.random.normal(k, shape, dtype=jnp.float32) / np.sqrt(fan_in)
        return {'hidden_states': jax.random.normal(ks[0], (B, S, H), dtype=jnp.float32), 'Wp1': w(ks[1], (H, NAV), H), 'bp1': jnp.zeros((NAV,), jnp.float32), 'Wp2': w(ks[2], (NAV, E), NAV), 'bp2': jnp.zeros((E,), jnp.float32), 'W1': w(ks[3], (E, H, F), H), 'b1': jnp.zeros((E, F), jnp.float32), 'W2': w(ks[4], (E, F, H), F), 'b2': jnp.zeros((E, H), jnp.float32), 'Wo': w(ks[5], (H, H), H), 'bo': jnp.zeros((H,), jnp.float32)}
    _L1_ffn_in = _L1_ffn_setup()

    def _L2_attn_setup():
        import jax, jax.numpy as jnp
        import numpy as np
        import math
        INPUT_WIDTH = 128
        KEY_WIDTH = 64
        VALUE_WIDTH = 64
        NUM_HEADS = 16
        NUM_GROUPS = 4
        HEADS_PER_GROUP = NUM_HEADS // NUM_GROUPS
        key = jax.random.key(seed)
        k_x, k_q, k_k, k_v, k_p = jax.random.split(key, 5)
        n, s = (2, 256)

        def lin(k, fan_in, fan_out):
            bound = 1.0 / math.sqrt(fan_in)
            return jax.random.uniform(k, (fan_in, fan_out), minval=-bound, maxval=bound, dtype=jnp.float32)
        return {'X': jax.random.normal(k_x, (n, s, INPUT_WIDTH), dtype=jnp.float32), 'Wq': lin(k_q, INPUT_WIDTH, NUM_HEADS * KEY_WIDTH), 'Wk': lin(k_k, INPUT_WIDTH, NUM_GROUPS * KEY_WIDTH), 'Wv': lin(k_v, INPUT_WIDTH, NUM_GROUPS * VALUE_WIDTH), 'Wpost': lin(k_p, NUM_HEADS * VALUE_WIDTH, INPUT_WIDTH)}
    _L2_attn_in = _L2_attn_setup()

    def _L2_ffn_setup():
        import jax, jax.numpy as jnp
        import numpy as np
        B, S, H = (8, 512, 128)
        NAV = 128
        E = 8
        F = 2 * H
        key = jax.random.key(seed)
        ks = jax.random.split(key, 12)

        def w(k, shape, fan_in):
            return jax.random.normal(k, shape, dtype=jnp.float32) / np.sqrt(fan_in)
        return {'hidden_states': jax.random.normal(ks[0], (B, S, H), dtype=jnp.float32), 'Wp1': w(ks[1], (H, NAV), H), 'bp1': jnp.zeros((NAV,), jnp.float32), 'Wp2': w(ks[2], (NAV, E), NAV), 'bp2': jnp.zeros((E,), jnp.float32), 'W1': w(ks[3], (E, H, F), H), 'b1': jnp.zeros((E, F), jnp.float32), 'W2': w(ks[4], (E, F, H), F), 'b2': jnp.zeros((E, H), jnp.float32), 'Wo': w(ks[5], (H, H), H), 'bo': jnp.zeros((H,), jnp.float32)}
    _L2_ffn_in = _L2_ffn_setup()

    def _L3_attn_setup():
        import jax, jax.numpy as jnp
        import numpy as np
        HEADS = 16

        def _split_heads(t, h):
            b, y, hd = t.shape
            d = hd // h
            return t.reshape(b, y, h, d).transpose(0, 2, 1, 3).reshape(b * h, y, d)

        def _merge_heads(t, b, h):
            bh, y, d = t.shape
            return t.reshape(b, h, y, d).transpose(0, 2, 1, 3).reshape(b, y, h * d)
        key = jax.random.key(seed)
        ks = jax.random.split(key, 5)
        B, S, D = (8, 512, 128)
        scale = 1.0 / np.sqrt(D)
        x = jax.random.normal(ks[0], (B, S, D), dtype=jnp.float32)
        Wq = jax.random.normal(ks[1], (D, D), dtype=jnp.float32) * scale
        Wk = jax.random.normal(ks[2], (D, D), dtype=jnp.float32) * scale
        Wv = jax.random.normal(ks[3], (D, D), dtype=jnp.float32) * scale
        Wo = jax.random.normal(ks[4], (D, D), dtype=jnp.float32) * scale
        return {'x': x, 'Wq': Wq, 'Wk': Wk, 'Wv': Wv, 'Wo': Wo}
    _L3_attn_in = _L3_attn_setup()

    def _L3_ffn_setup():
        import jax, jax.numpy as jnp
        import numpy as np
        E = 8
        K = 2
        D = 128
        H = 342
        B, S = (2, 256)

        def _moe_forward(x, centroid, Wg, bg, W1, b1, W2, b2):
            T = x.shape[0] * x.shape[1]
            xs = x.reshape(T, D)
            d2 = jnp.sum(xs * xs, axis=-1, keepdims=True) + jnp.sum(centroid * centroid, axis=-1)[None, :] - 2.0 * (xs @ centroid.T)
            dist = jnp.sqrt(jnp.maximum(d2, 1e-12))
            w, sel = jax.lax.top_k(dist, K)
            w = jax.nn.softmax(w.astype(jnp.float32), axis=1).astype(x.dtype)
            we = jnp.zeros((T, E), dtype=x.dtype).at[jnp.arange(T)[:, None], sel].add(w)
            out = jnp.zeros_like(xs)
            for e in range(E):
                h = jax.nn.silu(xs @ Wg[e] + bg[e]) * (xs @ W1[e] + b1[e])
                out = out + we[:, e:e + 1] * (h @ W2[e] + b2[e])
            return out.reshape(x.shape)
        key = jax.random.key(seed)
        ks = jax.random.split(key, 9)
        scale = 0.02
        return {'x': jax.random.normal(ks[0], (B, S, D), dtype=jnp.float32), 'centroid': jax.random.normal(ks[1], (E, D), dtype=jnp.float32), 'Wg': jax.random.normal(ks[2], (E, D, H), dtype=jnp.float32) * scale, 'bg': jnp.zeros((E, H), dtype=jnp.float32), 'W1': jax.random.normal(ks[3], (E, D, H), dtype=jnp.float32) * scale, 'b1': jnp.zeros((E, H), dtype=jnp.float32), 'W2': jax.random.normal(ks[4], (E, H, D), dtype=jnp.float32) * scale, 'b2': jnp.zeros((E, D), dtype=jnp.float32)}
    _L3_ffn_in = _L3_ffn_setup()
    _d = {'L0_attn_x': _L0_attn_in['x'], 'L0_attn_qkv_w': _L0_attn_in['qkv_w'], 'L0_attn_qkv_b': _L0_attn_in['qkv_b'], 'L0_attn_out_w': _L0_attn_in['out_w'], 'L0_attn_out_b': _L0_attn_in['out_b'], 'L0_ffn_sg': _L0_ffn_in['sg'], 'L0_ffn_su': _L0_ffn_in['su'], 'L0_ffn_sd': _L0_ffn_in['sd'], 'L0_ffn_rg': _L0_ffn_in['rg'], 'L0_ffn_ru': _L0_ffn_in['ru'], 'L0_ffn_rd': _L0_ffn_in['rd'], 'L0_ffn_wr': _L0_ffn_in['wr'], 'L0_ffn_rb': _L0_ffn_in['rb'], 'L1_attn_w_qkv': _L1_attn_in['w_qkv'], 'L1_attn_w_out': _L1_attn_in['w_out'], 'L1_attn_b_out': _L1_attn_in['b_out'], 'L1_ffn_Wp1': _L1_ffn_in['Wp1'], 'L1_ffn_bp1': _L1_ffn_in['bp1'], 'L1_ffn_Wp2': _L1_ffn_in['Wp2'], 'L1_ffn_bp2': _L1_ffn_in['bp2'], 'L1_ffn_W1': _L1_ffn_in['W1'], 'L1_ffn_b1': _L1_ffn_in['b1'], 'L1_ffn_W2': _L1_ffn_in['W2'], 'L1_ffn_b2': _L1_ffn_in['b2'], 'L1_ffn_Wo': _L1_ffn_in['Wo'], 'L1_ffn_bo': _L1_ffn_in['bo'], 'L2_attn_Wq': _L2_attn_in['Wq'], 'L2_attn_Wk': _L2_attn_in['Wk'], 'L2_attn_Wv': _L2_attn_in['Wv'], 'L2_attn_Wpost': _L2_attn_in['Wpost'], 'L2_ffn_Wp1': _L2_ffn_in['Wp1'], 'L2_ffn_bp1': _L2_ffn_in['bp1'], 'L2_ffn_Wp2': _L2_ffn_in['Wp2'], 'L2_ffn_bp2': _L2_ffn_in['bp2'], 'L2_ffn_W1': _L2_ffn_in['W1'], 'L2_ffn_b1': _L2_ffn_in['b1'], 'L2_ffn_W2': _L2_ffn_in['W2'], 'L2_ffn_b2': _L2_ffn_in['b2'], 'L2_ffn_Wo': _L2_ffn_in['Wo'], 'L2_ffn_bo': _L2_ffn_in['bo'], 'L3_attn_Wq': _L3_attn_in['Wq'], 'L3_attn_Wk': _L3_attn_in['Wk'], 'L3_attn_Wv': _L3_attn_in['Wv'], 'L3_attn_Wo': _L3_attn_in['Wo'], 'L3_ffn_centroid': _L3_ffn_in['centroid'], 'L3_ffn_Wg': _L3_ffn_in['Wg'], 'L3_ffn_bg': _L3_ffn_in['bg'], 'L3_ffn_W1': _L3_ffn_in['W1'], 'L3_ffn_b1': _L3_ffn_in['b1'], 'L3_ffn_W2': _L3_ffn_in['W2'], 'L3_ffn_b2': _L3_ffn_in['b2']}
    _x0 = _d['L0_attn_x']
    _d['L0_attn_x'] = jax.random.normal(jax.random.fold_in(jax.random.key(seed), 1), (8, 256, 128), dtype=_x0.dtype)
    del _x0
    return _d

def reference(L0_attn_x, L0_attn_qkv_w, L0_attn_qkv_b, L0_attn_out_w, L0_attn_out_b, L0_ffn_sg, L0_ffn_su, L0_ffn_sd, L0_ffn_rg, L0_ffn_ru, L0_ffn_rd, L0_ffn_wr, L0_ffn_rb, L1_attn_w_qkv, L1_attn_w_out, L1_attn_b_out, L1_ffn_Wp1, L1_ffn_bp1, L1_ffn_Wp2, L1_ffn_bp2, L1_ffn_W1, L1_ffn_b1, L1_ffn_W2, L1_ffn_b2, L1_ffn_Wo, L1_ffn_bo, L2_attn_Wq, L2_attn_Wk, L2_attn_Wv, L2_attn_Wpost, L2_ffn_Wp1, L2_ffn_bp1, L2_ffn_Wp2, L2_ffn_bp2, L2_ffn_W1, L2_ffn_b1, L2_ffn_W2, L2_ffn_b2, L2_ffn_Wo, L2_ffn_bo, L3_attn_Wq, L3_attn_Wk, L3_attn_Wv, L3_attn_Wo, L3_ffn_centroid, L3_ffn_Wg, L3_ffn_bg, L3_ffn_W1, L3_ffn_b1, L3_ffn_W2, L3_ffn_b2):

    def _L0_attn_ref(x, qkv_w, qkv_b, out_w, out_b):
        import jax, jax.numpy as jnp
        import numpy as np
        import math
        HIDDEN = 128
        N_HEADS = 16
        HEAD = HIDDEN // N_HEADS
        NEG_INF = -10000.0
        B, S, H = x.shape
        qkv = x @ qkv_w + qkv_b
        q, k, v = jnp.split(qkv, 3, axis=-1)

        def heads(t):
            return t.reshape(B, S, N_HEADS, HEAD).transpose(0, 2, 1, 3)
        q, k, v = (heads(q), heads(k), heads(v))
        scores = jnp.einsum('bhql,bhkl->bhqk', q, k) / math.sqrt(HEAD)
        q_ind = jnp.arange(S)[:, None]
        k_ind = jnp.arange(S)[None, :]
        mask = q_ind < k_ind
        scores = jnp.where(mask, NEG_INF, scores)
        attn = jax.nn.softmax(scores, axis=-1)
        ctx = jnp.einsum('bhqk,bhkl->bhql', attn, v)
        ctx = ctx.transpose(0, 2, 1, 3).reshape(B, S, H)
        return ctx @ out_w + out_b

    def _L0_ffn_ref(x, sg, su, sd, rg, ru, rd, wr, rb):
        import jax, jax.numpy as jnp
        import numpy as np
        H, I, E_ROUTED, TOP_K = (128, 352, 7, 2)
        B, S = (4, 256)

        def _expert(h, g, u, d):
            return jnp.einsum('...i,hi->...h', jax.nn.silu(h @ g.T) * (h @ u.T), d)
        shared_out = _expert(x, sg, su, sd)
        logits = x @ wr.T + rb
        probs = jax.nn.softmax(logits, axis=-1)
        scores, idx = jax.lax.top_k(probs, TOP_K)
        scores = scores / scores.sum(axis=-1, keepdims=True)
        w = jnp.sum(scores[..., None] * jax.nn.one_hot(idx, E_ROUTED, dtype=x.dtype), axis=-2)
        out = shared_out
        for e in range(E_ROUTED):
            out = out + w[..., e:e + 1] * _expert(x, rg[e], ru[e], rd[e])
        return out

    def _L1_attn_ref(x, w_qkv, w_out, b_out):
        import jax, jax.numpy as jnp
        import numpy as np
        import math
        B, T, D = (2, 256, 128)
        N_HEADS = 16
        D_HEAD = D // N_HEADS

        def _rope_tables(t, d_head, dtype=jnp.float32):
            theta = 1.0 / 10000.0 ** (jnp.arange(0, d_head, 2, dtype=jnp.float32) / d_head)
            angles = jnp.outer(jnp.arange(t, dtype=jnp.float32), theta)
            angles = jnp.concatenate([angles, angles], axis=-1)
            return (jnp.cos(angles).astype(dtype), jnp.sin(angles).astype(dtype))

        def _rotate_half(x):
            half = x.shape[-1] // 2
            return jnp.concatenate([-x[..., half:], x[..., :half]], axis=-1)

        def _apply_rope(x, cos, sin):
            return x * cos[None, None] + _rotate_half(x) * sin[None, None]
        b, t, d = x.shape
        qkv = x @ w_qkv
        qkv = qkv.reshape(b, t, 3, N_HEADS, D_HEAD)
        q = jnp.transpose(qkv[:, :, 0], (0, 2, 1, 3))
        k = jnp.transpose(qkv[:, :, 1], (0, 2, 1, 3))
        v = jnp.transpose(qkv[:, :, 2], (0, 2, 1, 3))
        cos, sin = _rope_tables(t, D_HEAD, x.dtype)
        q = _apply_rope(q, cos, sin)
        k = _apply_rope(k, cos, sin)
        scores = jnp.einsum('bhqd,bhkd->bhqk', q, k) / math.sqrt(D_HEAD)
        probs = jax.nn.softmax(scores, axis=-1)
        out = jnp.einsum('bhqk,bhkd->bhqd', probs, v)
        out = jnp.transpose(out, (0, 2, 1, 3)).reshape(b, t, d)
        return out @ w_out + b_out

    def _L1_ffn_ref(hidden_states, Wp1, bp1, Wp2, bp2, W1, b1, W2, b2, Wo, bo):
        import jax, jax.numpy as jnp
        import numpy as np
        B, S, H = (8, 512, 128)
        NAV = 128
        E = 8
        F = 2 * H
        last = hidden_states[:, -1, :]
        logits = jax.nn.gelu(last @ Wp1 + bp1, approximate=False) @ Wp2 + bp2
        action_probs = jax.nn.softmax(logits, axis=-1)
        sel = jnp.argmax(action_probs, axis=-1)
        w1 = W1[sel]
        w2 = W2[sel]
        h = jax.nn.gelu(jnp.einsum('bsh,bhf->bsf', hidden_states, w1) + b1[sel][:, None, :], approximate=False)
        reasoned = jnp.einsum('bsf,bfh->bsh', h, w2) + b2[sel][:, None, :]
        out = reasoned @ Wo + bo
        return hidden_states + 0.3 * out

    def _L2_attn_ref(X, Wq, Wk, Wv, Wpost):
        import jax, jax.numpy as jnp
        import numpy as np
        import math
        INPUT_WIDTH = 128
        KEY_WIDTH = 64
        VALUE_WIDTH = 64
        NUM_HEADS = 16
        NUM_GROUPS = 4
        HEADS_PER_GROUP = NUM_HEADS // NUM_GROUPS
        n, s, _ = X.shape
        Q = (X @ Wq).reshape(n, s, NUM_GROUPS, HEADS_PER_GROUP, KEY_WIDTH)
        K = (X @ Wk).reshape(n, s, NUM_GROUPS, KEY_WIDTH)
        V = (X @ Wv).reshape(n, s, NUM_GROUPS, VALUE_WIDTH)
        scale = 1.0 / math.sqrt(KEY_WIDTH)
        raw = jnp.einsum('bsgwe,btge->bstgw', Q, K * scale)
        attn = jax.nn.softmax(raw, axis=2)
        A = jnp.einsum('bstgw,btge->bsgwe', attn, V).reshape(n, s, NUM_HEADS * VALUE_WIDTH)
        P = A @ Wpost
        return X + P

    def _L2_ffn_ref(hidden_states, Wp1, bp1, Wp2, bp2, W1, b1, W2, b2, Wo, bo):
        import jax, jax.numpy as jnp
        import numpy as np
        B, S, H = (8, 512, 128)
        NAV = 128
        E = 8
        F = 2 * H
        last = hidden_states[:, -1, :]
        logits = jax.nn.gelu(last @ Wp1 + bp1, approximate=False) @ Wp2 + bp2
        action_probs = jax.nn.softmax(logits, axis=-1)
        sel = jnp.argmax(action_probs, axis=-1)
        w1 = W1[sel]
        w2 = W2[sel]
        h = jax.nn.gelu(jnp.einsum('bsh,bhf->bsf', hidden_states, w1) + b1[sel][:, None, :], approximate=False)
        reasoned = jnp.einsum('bsf,bfh->bsh', h, w2) + b2[sel][:, None, :]
        out = reasoned @ Wo + bo
        return hidden_states + 0.3 * out

    def _L3_attn_ref(x, Wq, Wk, Wv, Wo):
        import jax, jax.numpy as jnp
        import numpy as np
        HEADS = 16

        def _split_heads(t, h):
            b, y, hd = t.shape
            d = hd // h
            return t.reshape(b, y, h, d).transpose(0, 2, 1, 3).reshape(b * h, y, d)

        def _merge_heads(t, b, h):
            bh, y, d = t.shape
            return t.reshape(b, h, y, d).transpose(0, 2, 1, 3).reshape(b, y, h * d)
        b = x.shape[0]
        h = HEADS
        q = _split_heads(x @ Wq.T, h)
        k = _split_heads(x @ Wk.T, h)
        v = _split_heads(x @ Wv.T, h)
        d = q.shape[-1]
        z = jnp.einsum('byq,byk->bkq', q, k) / jnp.sqrt(jnp.asarray(d, x.dtype))
        z = jax.nn.softmax(z, axis=-1)
        z = jnp.einsum('byz,bvy->bvz', z, v)
        z = _merge_heads(z, b, h)
        return z @ Wo.T

    def _L3_ffn_ref(x, centroid, Wg, bg, W1, b1, W2, b2):
        import jax, jax.numpy as jnp
        import numpy as np
        E = 8
        K = 2
        D = 128
        H = 342
        B, S = (2, 256)

        def _moe_forward(x, centroid, Wg, bg, W1, b1, W2, b2):
            T = x.shape[0] * x.shape[1]
            xs = x.reshape(T, D)
            d2 = jnp.sum(xs * xs, axis=-1, keepdims=True) + jnp.sum(centroid * centroid, axis=-1)[None, :] - 2.0 * (xs @ centroid.T)
            dist = jnp.sqrt(jnp.maximum(d2, 1e-12))
            w, sel = jax.lax.top_k(dist, K)
            w = jax.nn.softmax(w.astype(jnp.float32), axis=1).astype(x.dtype)
            we = jnp.zeros((T, E), dtype=x.dtype).at[jnp.arange(T)[:, None], sel].add(w)
            out = jnp.zeros_like(xs)
            for e in range(E):
                h = jax.nn.silu(xs @ Wg[e] + bg[e]) * (xs @ W1[e] + b1[e])
                out = out + we[:, e:e + 1] * (h @ W2[e] + b2[e])
            return out.reshape(x.shape)
        return _moe_forward(x, centroid, Wg, bg, W1, b1, W2, b2)
    x = L0_attn_x
    x = x + _layernorm(_L0_attn_ref(_layernorm(x, axis=-1), L0_attn_qkv_w, L0_attn_qkv_b, L0_attn_out_w, L0_attn_out_b), axis=-1)
    x = x + _layernorm(_L0_ffn_ref(_layernorm(x, axis=-1), L0_ffn_sg, L0_ffn_su, L0_ffn_sd, L0_ffn_rg, L0_ffn_ru, L0_ffn_rd, L0_ffn_wr, L0_ffn_rb), axis=-1)
    x = x + _layernorm(_L1_attn_ref(_layernorm(x, axis=-1), L1_attn_w_qkv, L1_attn_w_out, L1_attn_b_out), axis=-1)
    x = x + _layernorm(_L1_ffn_ref(_layernorm(x, axis=-1), L1_ffn_Wp1, L1_ffn_bp1, L1_ffn_Wp2, L1_ffn_bp2, L1_ffn_W1, L1_ffn_b1, L1_ffn_W2, L1_ffn_b2, L1_ffn_Wo, L1_ffn_bo), axis=-1)
    x = x + _layernorm(_L2_attn_ref(_layernorm(x, axis=-1), L2_attn_Wq, L2_attn_Wk, L2_attn_Wv, L2_attn_Wpost), axis=-1)
    x = x + _layernorm(_L2_ffn_ref(_layernorm(x, axis=-1), L2_ffn_Wp1, L2_ffn_bp1, L2_ffn_Wp2, L2_ffn_bp2, L2_ffn_W1, L2_ffn_b1, L2_ffn_W2, L2_ffn_b2, L2_ffn_Wo, L2_ffn_bo), axis=-1)
    x = x + _layernorm(_L3_attn_ref(_layernorm(x, axis=-1), L3_attn_Wq, L3_attn_Wk, L3_attn_Wv, L3_attn_Wo), axis=-1)
    x = x + _layernorm(_L3_ffn_ref(_layernorm(x, axis=-1), L3_ffn_centroid, L3_ffn_Wg, L3_ffn_bg, L3_ffn_W1, L3_ffn_b1, L3_ffn_W2, L3_ffn_b2), axis=-1)
    return x

_drawn_inputs = setup_inputs


def setup_inputs(seed=0):
    import zlib

    import numpy as np

    out = dict(_drawn_inputs(seed))
    spreads = {'L0_attn_qkv_b': (0.0, 0.1),
     'L0_attn_out_b': (0.0, 0.1),
     'L0_ffn_rb': (0.0, 0.1),
     'L1_ffn_bp1': (0.0, 0.1),
     'L1_ffn_bp2': (0.0, 0.1),
     'L1_ffn_b1': (0.0, 0.364),
     'L1_ffn_b2': (0.0, 0.271),
     'L1_ffn_bo': (0.0, 0.323),
     'L2_ffn_bp1': (0.0, 0.1),
     'L2_ffn_bp2': (0.0, 0.1),
     'L2_ffn_b1': (0.0, 0.44),
     'L2_ffn_b2': (0.0, 0.412),
     'L2_ffn_bo': (0.0, 0.464),
     'L3_ffn_bg': (0.0, 0.8),
     'L3_ffn_b1': (0.0, 0.8),
     'L3_ffn_b2': (0.0, 0.1)}
    factors = {'L2_attn_Wq': 6.958, 'L2_attn_Wk': 6.906, 'L3_ffn_Wg': 2.864, 'L3_ffn_W1': 2.887}
    for name, (base, spread) in spreads.items():
        noise = np.random.default_rng([zlib.crc32(name.encode()), seed]).standard_normal(out[name].shape)
        drawn = base * np.exp(spread * noise) if base else spread * noise
        out[name] = jnp.asarray(drawn.astype(out[name].dtype))
    for name, factor in factors.items():
        out[name] = (out[name] * factor).astype(out[name].dtype)
    return out
```

```python
from contextlib import ExitStack

import numpy as np
import concourse.bass as bass
from concourse import mybir

F32 = mybir.dt.float32
F32R = mybir.dt.float32r
U32 = mybir.dt.uint32
BF16 = mybir.dt.bfloat16
ALU = mybir.AluOpType
ACT = mybir.ActivationFunctionType
AX = mybir.AxisListType.X

P = 128
SEQS = 8
SEQ = 256
T = SEQ // P
TILES = SEQS * T
NH = 16
NG = 4
HG = NH // NG
EPS = 1e-5
MASKED = -1e30
BANK = 512
D8 = 8
D64 = 64
ROWS = 24
NE = 8
F_EXP = {0: 352, 3: 342}
FC = 3
RT = 4
RUN = RT * P
RUNS = TILES // RT
DEPTH = 2


class Signal:

    def __init__(self, sem, per):
        self.sem, self.per = sem, per

    def credit(self, eng):
        eng.sem_inc(self.sem, DEPTH * self.per)

    def at(self, i, c, back=0):
        assert 1 <= c <= self.per and 0 <= back <= DEPTH
        return i * self.per + ((DEPTH - back) * self.per + c)


def own_wait(eng, sem):
    eng.sem_inc(sem, 1)


class Chain:

    def __init__(self, sem, per):
        self.sem, self.sig, self.per, self.n = sem, Signal(sem, per), per, 0

    def begin(self, i):
        self.i, self.n = i, 0

    def next(self):
        self.n += 1
        return self.sem

    def so_far(self):
        return self.sig.at(self.i, self.n)

    def end(self):
        assert self.n == self.per, f"{self.n} signals, not {self.per}"


def merge(first, second):
    parts = [first, second]
    while parts:
        for part in list(parts):
            if next(part, "end") == "end":
                parts.remove(part)


def issue(part):
    for _ in part:
        pass


def pipeline(eng, front, back):
    issue(front(0, 0))
    with eng.Fori(0, (SEQS - 2) // 2) as t:
        merge(back(t * 2, 0), front(t * 2 + 1, 1))
        merge(back(t * 2 + 1, 1), front(t * 2 + 2, 0))
    merge(back(SEQS - 2, 0), front(SEQS - 1, 1))
    issue(back(SEQS - 1, 1))


class Stage:

    def __init__(self, nc, ctx, name):
        self.nc, self.ctx, self.name = nc, ctx, name
        self.sems = []
        ctx.callback(self.release)
        self.dve_waited, self.sp_waited = self.sem("dve_waited"), self.sem("sp_waited")
        self.ps = ctx.enter_context(nc.psum_tensor(f"{name}_banks", [P, 8, BANK], F32))

    def sb(self, name, shape, dt=F32):
        return self.ctx.enter_context(self.nc.sbuf_tensor(f"{self.name}_{name}", shape, dt))

    def sem(self, name):
        self.sems.append(self.nc.alloc_semaphore(name=f"{self.name}_{name}"))
        return self.sems[-1]

    def release(self):
        self.nc.clear_and_free_semaphores(self.sems)
        self.nc.all_engine_barrier()

    def sig(self, name, per):
        return Signal(self.sem(name), per)



class Norm:

    def __init__(self, st, name, n):
        self.n = n
        self.waited = st.dve_waited
        self.stats = st.sb(f"{name}_stats", [P, n, 6])
        self.mean_var = st.sb(f"{name}_mean_var", [P, n, 2])
        self.var = st.sb(f"{name}_var", [P, n])
        self.rstd = st.sb(f"{name}_rstd", [P, n])
        self.var_ready = st.sig(f"{name}_var_ready", 1)
        self.rstd_ready = st.sig(f"{name}_rstd_ready", 1)

    CHAIN = 2

    def moments(self, nc, dve, chain, src):
        for j in range(self.n):
            last = nc.vector.bn_stats(self.stats[:, j, :], src(j))
        last.then_inc(chain.next(), 1)
        dve.wait_ge(chain.sem, chain.so_far())
        own_wait(dve, self.waited)
        for j in range(self.n):
            last = nc.vector.bn_aggr(self.mean_var[:, j, :], self.stats[:, j, :])
        last.then_inc(chain.next(), 1)
        dve.wait_ge(chain.sem, chain.so_far())
        nc.vector.tensor_scalar(self.var[:, :], self.mean_var[:, :, 1], EPS, None, ALU.add).then_inc(
            self.var_ready.sem, 1)

    def power(self, nc, pool, i, minus_half):
        pool.wait_ge(self.var_ready.sem, self.var_ready.at(i, 1))
        nc.gpsimd.tensor_tensor(self.rstd[:, :], self.var[:, :], minus_half[:, 0:self.n], ALU.pow).then_inc(
            self.rstd_ready.sem, 1)

    def apply(self, nc, j, out, src):
        return nc.vector.tensor_scalar(out, src, self.mean_var[:, j, 0:1], self.rstd[:, j:j + 1],
                                       ALU.subtract, ALU.mult)


def add_normed(nc, dve, chain, norm, i, x, tile0, f):
    dve.wait_ge(norm.rstd_ready.sem, norm.rstd_ready.at(i, 1))
    for j in range(norm.n):
        last = norm.apply(nc, j, f[:, j, :], f[:, j, :])
    last.then_inc(chain.next(), 1)
    dve.wait_ge(chain.sem, chain.so_far())
    for j in range(norm.n):
        last = nc.vector.tensor_tensor(x[:, tile0 + j, :], x[:, tile0 + j, :], f[:, j, :], ALU.add)
    last.then_inc(chain.next(), 1)



def attention8(nc, g, layer, blob):
    causal, rope = layer == 0, layer == 1
    FILLS = 3 if causal else 4
    SCALE = float(D8) ** -0.5
    DV = D8 + 1
    x = g.x
    with ExitStack() as ctx:
        st = Stage(nc, ctx, f"a{layer}")
        ps = st.ps
        n_w = blob.shape[1]
        w = st.sb("w", [P, n_w])
        at, off = {}, 0
        for name, width in ATT8[layer]:
            at[name] = w[:, off:off + width]
            off += width
        assert off == n_w
        spread_raw = st.sb("spread_raw", [P, 16, P])
        spread = st.sb("spread", [P, 16, P], F32R)
        if causal:
            masks = st.sb("masks", [P, 4, BANK], BF16)
            masks_raw = st.sb("masks_raw", [P, 4, BANK])
            ident16 = st.sb("ident16", [P, P], BF16)
        y = st.sb("y", [P, T, P])
        f = st.sb("f", [P, T, P])
        yT = st.sb("yT", [P, SEQ])
        qk = st.sb("qk", [P, 2 * SEQ])
        rot = st.sb("rot", [P, 2 * SEQ])
        hi = st.sb("hi", [P, 2 * SEQ], F32R)
        lo = st.sb("lo", [P, 2 * SEQ], F32R)
        QT = [st.sb(f"QT{k}", [P, NG, SEQ], F32R) for k in range(2)]
        KT = [st.sb(f"KT{k}", [P, NG, SEQ], F32R) for k in range(2)]
        V = [st.sb(f"V{k}", [P, T, NH, DV]) for k in range(2)]
        rowmax = st.sb("rowmax", [P, T, NH])
        mrow = [[st.sb(f"mrow{k}{j}", [NG, SEQ], F32R) for j in range(NG)] for k in range(2)]
        probs = [st.sb(f"probs{k}", [P, FILLS, BANK]) for k in range(2)]
        recip = st.sb("recip", [P, T, NH])
        cx = st.sb("cx", [P, T, P])
        cxT = st.sb("cxT", [P, SEQ])
        norm_in, norm_out = Norm(st, "in", T), Norm(st, "out", T)

        loaded = st.sem("weights_loaded")
        constants = st.sem("constants_ready")
        spread_ready = st.sem("spread_ready")
        y_ready, yT_ps, yT_ready = st.sig("y_ready", 1), st.sig("yT_ps", 1), st.sig("yT_ready", 1)
        qk_ps, qk_ready = st.sig("qk_ps", 1), st.sig("qk_ready", 1)
        hi_ready, lo_ready = st.sig("hi_ready", 1), st.sig("lo_ready", 1)
        v_ps, v_ready = st.sig("v_ps", 1), st.sig("v_ready", 1)
        stack_ps, stack_ready = st.sig("stack_ps", 4), st.sig("stack_ready", 4)
        score_ps, rowmax_ready = st.sig("score_ps", NG * FILLS), st.sig("rowmax_ready", NG * FILLS)
        max_ps, mrow_ready = st.sig("max_ps", NG), st.sig("mrow_ready", NG)
        mrow_placed = [st.sem(f"mrow_placed{j}") for j in range(NG)]
        sT_ps, exp_done = st.sig("sT_ps", NG * FILLS), st.sig("exp_done", NG * FILLS)
        pv_done, cx_ready = st.sig("pv_done", NG), st.sig("cx_ready", 1)
        cxT_ps, cxT_ready = st.sig("cxT_ps", 1), st.sig("cxT_ready", 1)
        out_ps, f_ready = st.sig("out_ps", 1), st.sig("f_ready", 1)
        front_chain = Chain(st.sem("dve_front"), Norm.CHAIN + (2 if rope else 0))
        back_chain = Chain(st.sem("dve_back"), Norm.CHAIN + 3)

        Q_HI, Q_LO, K_HI, K_LO = (4 * k for k in range(4))
        block = ctx.enter_context(nc.Block())

        @block.sync
        def _(sp):
            sp.dma_start(w[:, :], blob).then_inc(loaded, 16)
            sp.dma_start(spread_raw[:, :, :], g.spread).then_inc(loaded, 16)
            if causal:
                sp.dma_start(masks_raw[:, :, :], g.masks).then_inc(loaded, 16)

            def front(i, p):
                for _ in range(4):
                    yield
                for j in range(NG):
                    sp.wait_ge(mrow_ready.sem, mrow_ready.at(i, j + 1))
                    sp.dma_start(QT[p][32 * j + ROWS:32 * j + ROWS + 1, :, :].bitcast(F32),
                                 mrow[p][j][:, :].bitcast(F32)).then_inc(
                        mrow_placed[j], 16)
                    yield

            pipeline(sp, front, lambda i, p: iter(()))

        @block.gpsimd
        def _(pool):
            norm_in.rstd_ready.credit(pool)
            norm_out.rstd_ready.credit(pool)

            def front(i, p):
                norm_in.power(nc, pool, i, g.minus_half)
                yield

            def back(i, p):
                for _ in range(NG + 1):
                    yield
                norm_out.power(nc, pool, i, g.minus_half)
                yield

            pipeline(pool, front, back)

        @block.vector
        def _(dve):
            for s in (norm_in.var_ready, norm_out.var_ready, y_ready, qk_ready, lo_ready, v_ready,
                      rowmax_ready, cx_ready, f_ready, front_chain.sig, back_chain.sig):
                s.credit(dve)
            dve.wait_ge(loaded, 48 if causal else 32)
            if causal:
                nc.vector.tensor_copy(masks[:, :, :], masks_raw[:, :, :])
                nc.vector.tensor_copy(ident16[:, :], g.ident[:, :])
            nc.vector.tensor_copy(spread[:, :, :], spread_raw[:, :, :]).then_inc(spread_ready, 1)
            nc.vector.memset(V[0][:, :, :, D8:DV], 1.0)
            nc.vector.memset(V[1][:, :, :, D8:DV], 1.0).then_inc(constants, 1)
            dve.wait_ge(constants, 1)

            def front(i, p):
                front_chain.begin(i)
                norm_in.moments(nc, dve, front_chain, lambda j: x[:, i * T + j, :])
                dve.wait_ge(norm_in.rstd_ready.sem, norm_in.rstd_ready.at(i, 1))
                for j in range(T):
                    last = norm_in.apply(nc, j, y[:, j, :], x[:, i * T + j, :])
                last.then_inc(y_ready.sem, 1)
                yield
                dve.wait_ge(qk_ps.sem, qk_ps.at(i, 1))
                if rope:
                    nc.vector.tensor_tensor(qk[:, :], ps[:, 1, :], at["cos"], ALU.mult).then_inc(front_chain.next(), 1)
                    nc.vector.tensor_tensor(rot[:, :], ps[:, 0, :], at["sin"], ALU.mult).then_inc(front_chain.next(), 1)
                    dve.wait_ge(front_chain.sem, front_chain.so_far())
                    nc.vector.tensor_tensor(qk[:, :], qk[:, :], rot[:, :], ALU.add).then_inc(qk_ready.sem, 1)
                else:
                    for k in range(2):
                        last = nc.vector.tensor_scalar(qk[:, k * SEQ:(k + 1) * SEQ], ps[:, 1, k * SEQ:(k + 1) * SEQ],
                                                       at["qkb"][:, k:k + 1], None, ALU.add)
                    last.then_inc(qk_ready.sem, 1)
                yield
                dve.wait_ge(hi_ready.sem, hi_ready.at(i, 1))
                dve.wait_ge(qk_ready.sem, qk_ready.at(i, 1))
                nc.vector.tensor_tensor(lo[:, :], qk[:, :], hi[:, :].bitcast(F32), ALU.subtract).then_inc(
                    lo_ready.sem, 1)
                dve.wait_ge(v_ps.sem, v_ps.at(i, 1))
                v_bank = ps[:, 0 if causal else 1, 0:SEQ].rearrange("p (t h d) -> p t h d", t=T, h=NH)
                dve.wait_ge(pv_done.sem, pv_done.at(i, NG, 2))
                for t in range(T):
                    if causal:
                        last = nc.vector.tensor_tensor(V[p][:, t, :, 0:D8], v_bank[:, t],
                                                       at["vb"].rearrange("p (h d) -> p h d", h=NH), ALU.add)
                    else:
                        last = nc.vector.tensor_copy(V[p][:, t, :, 0:D8], v_bank[:, t])
                last.then_inc(v_ready.sem, 1)
                yield
                for j in range(NG):
                    if j == 0:
                        dve.wait_ge(max_ps.sem, max_ps.at(i, NG, 1))
                    for n in range(FILLS):
                        c = j * FILLS + n
                        dve.wait_ge(score_ps.sem, score_ps.at(i, c + 1))
                        bank = ps[:, 2 + c % 2, :]
                        if causal and n == 0:
                            o, src = rowmax[:, 0, 4 * j:4 * j + 4], bank.rearrange("p (h k) -> p h k", h=4)
                        else:
                            t, h = (1, 4 * j + 2 * (n - 1)) if causal else (n // 2, 4 * j + 2 * (n % 2))
                            o, src = rowmax[:, t, h:h + 2], bank.rearrange("p (h k) -> p h k", h=2)
                        nc.vector.reduce_max(o, src, AX).then_inc(rowmax_ready.sem, 1)
                    yield
                front_chain.end()

            def back(i, p):
                back_chain.begin(i)
                for _ in range(NG):
                    yield
                dve.wait_ge(pv_done.sem, pv_done.at(i, NG))
                c = ps[:, 6, 0:T * NH * DV].rearrange("p (t h d) -> p t h d", t=T, h=NH)
                nc.vector.reciprocal(recip[:, :, :], c[:, :, :, D8]).then_inc(back_chain.next(), 1)
                dve.wait_ge(back_chain.sem, back_chain.so_far())
                for t in range(T):
                    last = nc.vector.tensor_tensor(cx[:, t, :].rearrange("p (h d) -> p h d", h=NH), c[:, t, :, 0:D8],
                                                   recip[:, t, :].rearrange("p (h o) -> p h o", o=1).to_broadcast([P, NH, D8]), ALU.mult)
                last.then_inc(cx_ready.sem, 1)
                yield
                dve.wait_ge(out_ps.sem, out_ps.at(i, 1))
                for t in range(T):
                    last = nc.vector.tensor_tensor(f[:, t, :], ps[:, 7, t * P:(t + 1) * P], at["ob"], ALU.add)
                last.then_inc(f_ready.sem, 1)
                dve.wait_ge(f_ready.sem, f_ready.at(i, 1))
                norm_out.moments(nc, dve, back_chain, lambda j: f[:, j, :])
                yield
                add_normed(nc, dve, back_chain, norm_out, i, x, i * T, f)
                dve.wait_ge(back_chain.sem, back_chain.so_far())
                back_chain.end()

            pipeline(dve, front, back)

        @block.scalar
        def _(act):
            nc.scalar.preload_act_table(ACT.Exp)
            for s in (yT_ready, hi_ready, stack_ready, mrow_ready, exp_done, cxT_ready):
                s.credit(act)

            def front(i, p):
                yield
                act.wait_ge(yT_ps.sem, yT_ps.at(i, 1))
                nc.scalar.activation(yT[:, :], ps[:, 0, 0:SEQ], ACT.Copy).then_inc(yT_ready.sem, 1)
                yield
                act.wait_ge(qk_ready.sem, qk_ready.at(i, 1))
                act.wait_ge(stack_ps.sem, stack_ps.at(i, 4, 1))
                nc.scalar.activation(hi[:, :], qk[:, :], ACT.Copy).then_inc(hi_ready.sem, 1)
                act.wait_ge(sT_ps.sem, sT_ps.at(i, NG * FILLS, 2))
                for n in range(4):
                    act.wait_ge(stack_ps.sem, stack_ps.at(i, n + 1))
                    bank = ps[:, (1 if causal else 0) + (n % 2) * (-1 if causal else 1), :].rearrange(
                        "p (g t) -> p g t", g=2)
                    g2 = 2 * (n % 2)
                    if n < 2:
                        nc.scalar.activation(QT[p][:, g2:g2 + 2, :], bank, ACT.Copy).then_inc(stack_ready.sem, 1)
                    else:
                        nc.scalar.activation(KT[p][:, g2:g2 + 2, :], bank, ACT.Identity,
                                             bias=g.ones_rows[:, :]).then_inc(stack_ready.sem, 1)
                yield
                for j in range(NG):
                    yield
                    act.wait_ge(max_ps.sem, max_ps.at(i, j + 1))
                    bank = (j + 1) % 2 if causal else j % 2
                    nc.scalar.activation(mrow[p][j][:, :], ps[0:NG, bank, 0:SEQ], ACT.Copy, scale=-1.0).then_inc(
                        mrow_ready.sem, 1)

            def back(i, p):
                for j in range(NG):
                    if j < 2:
                        act.wait_ge(pv_done.sem, pv_done.at(i, j + 3, 1))
                    else:
                        act.wait_ge(pv_done.sem, pv_done.at(i, j - 1))
                    for n in range(FILLS):
                        c = j * FILLS + n
                        act.wait_ge(sT_ps.sem, sT_ps.at(i, c + 1))
                        nc.scalar.activation(probs[j % 2][:, n, :], ps[:, 4 + c % 2, :], ACT.Exp,
                                             scale=SCALE).then_inc(exp_done.sem, 1)
                    yield
                yield
                act.wait_ge(cxT_ps.sem, cxT_ps.at(i, 1))
                nc.scalar.activation(cxT[:, :], ps[:, 7, 0:SEQ], ACT.Copy).then_inc(cxT_ready.sem, 1)
                yield

            pipeline(act, front, back)

        @block.tensor
        def _(pe):
            mm = nc.tensor.matmul
            for s in (yT_ps, qk_ps, v_ps, stack_ps, score_ps, max_ps, sT_ps, pv_done, cxT_ps, out_ps):
                s.credit(pe)
            pe.wait_ge(loaded, 48 if causal else 32)
            pe.wait_ge(spread_ready, 1)
            pe.wait_ge(constants, 1)

            def front(i, p):
                yield
                pe.wait_ge(y_ready.sem, y_ready.at(i, 1))
                pe.wait_ge(mrow_ready.sem, mrow_ready.at(i, NG, 1))
                for t in range(T):
                    last = nc.tensor.transpose(ps[:, 0, t * P:(t + 1) * P], y[:, t, :], g.ident[:, :])
                last.then_inc(yT_ps.sem, 1)
                pe.wait_ge(yT_ready.sem, yT_ready.at(i, 1))
                for k in range(2):
                    last = mm(ps[:, 1, k * SEQ:(k + 1) * SEQ], at["wqk"][:, k * P:(k + 1) * P], yT[:, :],
                              start=True, stop=True)
                if rope:
                    for k in range(2):
                        last = mm(ps[:, 0, k * SEQ:(k + 1) * SEQ], at["wrot"][:, k * P:(k + 1) * P], yT[:, :],
                                  start=True, stop=True)
                last.then_inc(qk_ps.sem, 1)
                yield
                if rope:
                    pe.wait_ge(qk_ready.sem, qk_ready.at(i, 1))
                vb = 0 if causal else 1
                for t in range(T):
                    last = mm(ps[:, vb, t * P:(t + 1) * P], yT[:, t * P:(t + 1) * P], at["wv"], start=True, stop=True)
                last.then_inc(v_ps.sem, 1)
                pe.wait_ge(hi_ready.sem, hi_ready.at(i, 1))
                pe.wait_ge(lo_ready.sem, lo_ready.at(i, 1))
                for n in range(4):
                    if n == 1:
                        pe.wait_ge(v_ready.sem, v_ready.at(i, 1))
                    elif n > 1:
                        pe.wait_ge(stack_ready.sem, stack_ready.at(i, n - 1))
                    bank = (1 if causal else 0) + (n % 2) * (-1 if causal else 1)
                    k, m_hi, m_lo = n // 2, (Q_HI, K_HI)[n // 2], (Q_LO, K_LO)[n // 2]
                    for gg in range(2):
                        blk = 2 * (n % 2) + gg
                        o = ps[:, bank, gg * SEQ:(gg + 1) * SEQ]
                        mm(o, spread[:, m_hi + blk, :], hi[:, k * SEQ:(k + 1) * SEQ], start=True, stop=False)
                        last = mm(o, spread[:, m_lo + blk, :], lo[:, k * SEQ:(k + 1) * SEQ], start=False, stop=True)
                    last.then_inc(stack_ps.sem, 1)
                yield
                pe.wait_ge(stack_ready.sem, stack_ready.at(i, 4))
                for j in range(NG + 1):
                    if j < NG:
                        rows = slice(32 * j, 32 * j + ROWS)
                        for n in range(FILLS):
                            c = j * FILLS + n
                            if c < 2:
                                pe.wait_ge(rowmax_ready.sem, rowmax_ready.at(i, NG * FILLS - 1 + c, 1))
                            else:
                                pe.wait_ge(rowmax_ready.sem, rowmax_ready.at(i, c - 1))
                            bank = ps[:, 2 + c % 2, :]
                            if causal:
                                mm(bank, ident16[:, :], masks[:, 0 if n == 0 else 1, :], start=True, stop=False)
                            if causal and n == 0:
                                for h in range(4):
                                    last = mm(bank[:, h * P:(h + 1) * P], QT[p][rows, h, 0:P], KT[p][rows, h, 0:P],
                                              start=False, stop=h == 3)
                            else:
                                t, h0 = (1, 2 * (n - 1)) if causal else (n // 2, 2 * (n % 2))
                                for h in range(2):
                                    last = mm(bank[:, h * SEQ:(h + 1) * SEQ], QT[p][rows, h0 + h, t * P:(t + 1) * P],
                                              KT[p][rows, h0 + h, :], start=not causal, stop=(not causal) or h == 1)
                            last.then_inc(score_ps.sem, 1)
                    if j > 0:
                        m = j - 1
                        pe.wait_ge(rowmax_ready.sem, rowmax_ready.at(i, j * FILLS))
                        if m >= 2:
                            pe.wait_ge(mrow_ready.sem, mrow_ready.at(i, m - 1))
                        bank = (m + 1) % 2 if causal else m % 2
                        for t in range(T):
                            last = nc.tensor.transpose(ps[0:NG, bank, t * P:(t + 1) * P],
                                                       rowmax[:, t, 4 * m:4 * m + 4], g.ident[:, :])
                        last.then_inc(max_ps.sem, 1)
                    yield

            def back(i, p):
                for j in range(NG + 1):
                    if j < NG:
                        rows = slice(32 * j, 32 * j + ROWS + 1)
                        pe.wait_ge(mrow_placed[j], i * 16 + 16)
                        for n in range(FILLS):
                            c = j * FILLS + n
                            if c < 2:
                                pe.wait_ge(exp_done.sem, exp_done.at(i, NG * FILLS - 1 + c, 1))
                            else:
                                pe.wait_ge(exp_done.sem, exp_done.at(i, c - 1))
                            bank = ps[:, 4 + c % 2, :]
                            if causal:
                                mm(bank, ident16[:, :], masks[:, 3 if n == 2 else 2, :], start=True, stop=False)
                            if causal and n == 2:
                                for h in range(4):
                                    last = mm(bank[:, h * P:(h + 1) * P], KT[p][rows, h, P:SEQ], QT[p][rows, h, P:SEQ],
                                              start=False, stop=h == 3)
                            else:
                                t, h0 = n // 2, 2 * (n % 2)
                                for h in range(2):
                                    last = mm(bank[:, h * SEQ:(h + 1) * SEQ], KT[p][rows, h0 + h, t * P:(t + 1) * P],
                                              QT[p][rows, h0 + h, :], start=not causal, stop=(not causal) or h == 1)
                            last.then_inc(sT_ps.sem, 1)
                    if j > 0:
                        m = j - 1
                        pe.wait_ge(exp_done.sem, exp_done.at(i, j * FILLS))
                        if m == 0:
                            pe.wait_ge(cx_ready.sem, cx_ready.at(i, 1, 1))
                        for h in range(4):
                            for t in range(T):
                                o = ps[:, 6, (t * NH + 4 * m + h) * DV:(t * NH + 4 * m + h + 1) * DV]
                                keys = range(t + 1) if causal else range(T)
                                for kt in keys:
                                    if causal and kt == 1:
                                        pt = probs[m % 2][:, 2, h * P:(h + 1) * P]
                                    else:
                                        s0 = (h % 2) * SEQ + t * P
                                        pt = probs[m % 2][:, 2 * kt + h // 2, s0:s0 + P]
                                    last = mm(o, pt, V[p][:, kt, 4 * m + h, :], start=kt == 0, stop=kt == keys[-1])
                        last.then_inc(pv_done.sem, 1)
                    yield
                pe.wait_ge(cx_ready.sem, cx_ready.at(i, 1))
                pe.wait_ge(f_ready.sem, f_ready.at(i, 1, 1))
                for t in range(T):
                    last = nc.tensor.transpose(ps[:, 7, t * P:(t + 1) * P], cx[:, t, :], g.ident[:, :])
                last.then_inc(cxT_ps.sem, 1)
                pe.wait_ge(cxT_ready.sem, cxT_ready.at(i, 1))
                for t in range(T):
                    last = mm(ps[:, 7, t * P:(t + 1) * P], cxT[:, t * P:(t + 1) * P], at["wo"], start=True, stop=True)
                last.then_inc(out_ps.sem, 1)
                yield

            pipeline(pe, front, back)



def load_experts(nc, g, layer, src_gu, src_down, w):
    width = F_EXP[layer]
    last_rows = width - (FC - 1) * P
    with ExitStack() as ctx:
        st = Stage(nc, ctx, f"w{layer}")
        raw_gu = [st.sb(f"raw_gu{k}", [P, 2 * width]) for k in range(2)]
        raw_down = [st.sb(f"raw_down{k}", [P, FC, P]) for k in range(2)]
        loaded = [st.sem(f"loaded{k}") for k in range(2)]
        hi_ready, lo_ready = st.sig("hi_ready", 1), st.sig("lo_ready", 1)
        block = ctx.enter_context(nc.Block())

        def parts(e, k):
            yield raw_gu[k][:, :], w["gu_hi"][:, e, :], w["gu_lo"][:, e, :]
            yield (raw_down[k][:, 0:2, :], w["down_hi"][:, e, 0:2, :], w["down_lo"][:, e, 0:2, :])
            yield (raw_down[k][0:last_rows, 2, :], w["down_hi"][0:last_rows, e, 2, :],
                   w["down_lo"][0:last_rows, e, 2, :])

        def experts(eng, step):
            with eng.Fori(0, NE // 2) as t:
                for k in range(2):
                    step(t * 2 + k, k)

        @block.sync
        def _(sp):
            def step(e, k):
                sp.wait_ge(lo_ready.sem, lo_ready.at(e, 1, 2))
                sp.dma_start(raw_gu[k][:, :], src_gu[e, :, :]).then_inc(loaded[k], 16)
                sp.dma_start(raw_down[k][:, 0:2, :],
                             src_down[e, 0:2 * P, :].rearrange("(c p) d -> p c d", p=P)).then_inc(loaded[k], 16)
                sp.dma_start(raw_down[k][0:last_rows, 2, :], src_down[e, 2 * P:width, :]).then_inc(loaded[k], 16)
            experts(sp, step)

        @block.scalar
        def _(act):
            hi_ready.credit(act)

            def step(e, k):
                act.wait_ge(loaded[k], (e - k) * 24 + 48)
                for raw, hi, lo in parts(e, k):
                    last = nc.scalar.activation(hi, raw, ACT.Copy)
                last.then_inc(hi_ready.sem, 1)
            experts(act, step)

        @block.vector
        def _(dve):
            lo_ready.credit(dve)

            def step(e, k):
                dve.wait_ge(hi_ready.sem, hi_ready.at(e, 1))
                for raw, hi, lo in parts(e, k):
                    last = nc.vector.tensor_tensor(lo, raw, hi.bitcast(F32), ALU.subtract)
                last.then_inc(lo_ready.sem, 1)
            experts(dve, step)


MOE = {
    0: [("router", NE), ("logit_bias", NE), ("iota", NE)],
    3: [("router", NE), ("iota", NE), ("gate_b", NE * FC), ("up_b", NE * FC), ("down_b", P)],
}


def experts(nc, g, layer, blob, w):
    width = F_EXP[layer]
    by_distance = layer == 3
    rows_of = [P, P, width - 2 * P]
    N = NE * FC
    x = g.x
    with ExitStack() as ctx:
        st = Stage(nc, ctx, f"m{layer}")
        ps = st.ps
        wb = st.sb("w", [P, blob.shape[1]])
        at, off = {}, 0
        for name, cols in MOE[layer]:
            at[name] = wb[:, off:off + cols]
            off += cols
        assert off == blob.shape[1]
        router_hi, router_lo = st.sb("router_hi", [P, NE], F32R), st.sb("router_lo", [P, NE], F32R)
        y = st.sb("y", [P, RT, P])
        y_hi, y_lo = st.sb("y_hi", [P, RUN], F32R), st.sb("y_lo", [P, RUN], F32R)
        gate = [st.sb(f"gate{k}", [P, RUN]) for k in range(2)]
        h = [st.sb(f"h{k}", [P, RUN]) for k in range(2)]
        h_hi = [st.sb(f"h_hi{k}", [P, FC, RUN], F32R) for k in range(2)]
        h_lo = [st.sb(f"h_lo{k}", [P, FC, RUN], F32R) for k in range(2)]
        acc = st.sb("acc", [P, RT, P])
        score = st.sb("score", [P, RT, NE])
        top = st.sb("top", [P, RT, 8])
        top_at = st.sb("top_at", [P, RT, 8], U32)
        top_atf = st.sb("top_atf", [P, RT, 2])
        gap, th = st.sb("gap", [P, RT]), st.sb("th", [P, RT])
        share = st.sb("share", [P, RT, 2])
        one_hot = st.sb("one_hot", [P, RT, 2, NE])
        we = st.sb("we", [P, RT, NE])
        norm_in, norm_out = Norm(st, "in", RT), Norm(st, "out", RT)
        if by_distance:
            sq_y = st.sb("sq_y", [P, RT])
            square = st.sb("square", [P, RT, P])
            weT = st.sb("weT", [NE, RUN])
            ones = st.sb("ones", [P, P])
            c2 = st.sb("c2", [P, 3 * NE])
            sq_ready, d2_ready, dist_ready = (st.sig("sq_ready", 1), st.sig("d2_ready", 1), st.sig("dist_ready", 1))
            weT_ps, weT_ready, b2_ps, acc_start = (st.sig("weT_ps", 1), st.sig("weT_ready", 1), st.sig("b2_ps", 1),
                                                   st.sig("acc_start", 1))
            c2_sq, c2_ps, ones_ready = st.sem("c2_sq"), st.sem("c2_ps"), st.sem("ones_ready")
        loaded = st.sem("loaded")
        split_setup = st.sem("router_split")
        y_ready, yT_ps = st.sig("y_ready", 1), st.sig("yT_ps", 1)
        y_hi_ready, y_lo_ready = st.sig("y_hi_ready", 1), st.sig("y_lo_ready", 1)
        router_ps = st.sig("router_ps", 1)
        gap_ready, th_ready = st.sig("gap_ready", 1), st.sig("th_ready", 1)
        we_ready = st.sig("we_ready", 1)
        gate_ps, up_ps = st.sig("gate_ps", N), st.sig("up_ps", N)
        silu_done, h_done = st.sig("silu_done", N), st.sig("h_done", N)
        hi_done, lo_done = st.sig("h_hi_done", N), st.sig("h_lo_done", N)
        down_ps, acc_done = st.sig("down_ps", NE), st.sig("acc_done", NE)
        front_chain = Chain(st.sem("dve_front"), Norm.CHAIN)
        back_chain = Chain(st.sem("dve_back"), 11)
        block = ctx.enter_context(nc.Block())

        def run_pipeline(eng, front, back):
            issue(front(0))
            with eng.Fori(0, RUNS - 1) as t:
                merge(back(t), front(t + 1))
            issue(back(RUNS - 1))

        def nothing(i):
            return iter(())

        def skip(n):
            for _ in range(n):
                yield

        @block.sync
        def _(sp):
            sp.dma_start(wb[:, :], blob).then_inc(loaded, 16)

        @block.gpsimd
        def _(pool):
            norm_in.rstd_ready.credit(pool)
            norm_out.rstd_ready.credit(pool)
            if by_distance:
                dist_ready.credit(pool)

            def front(i):
                yield from skip(20)
                norm_in.power(nc, pool, i, g.minus_half)
                yield

            def back(i):
                if by_distance:
                    yield from skip(1)
                    pool.wait_ge(d2_ready.sem, d2_ready.at(i, 1))
                    nc.gpsimd.tensor_tensor(score[:, :, :], score[:, :, :],
                                            g.plus_half[:, 0:RT * NE].rearrange("p (t e) -> p t e", t=RT),
                                            ALU.pow).then_inc(dist_ready.sem, 1)
                    yield from skip(N + 1)
                else:
                    yield from skip(N + 2)
                norm_out.power(nc, pool, i, g.minus_half)
                yield

            run_pipeline(pool, front, back)

        @block.vector
        def _(dve):
            sigs = [norm_in.var_ready, norm_out.var_ready, y_ready, y_lo_ready, gap_ready, h_done, lo_done,
                    acc_done, front_chain.sig, back_chain.sig, we_ready]
            if by_distance:
                sigs += [d2_ready, acc_start]
            for s in sigs:
                s.credit(dve)
            dve.wait_ge(loaded, 16)
            if by_distance:
                nc.vector.memset(ones[:, :], 1.0).then_inc(ones_ready, 1)
                nc.vector.tensor_tensor(c2[:, 0:NE], at["router"], at["router"], ALU.mult).then_inc(c2_sq, 1)
                dve.wait_ge(c2_sq, 1)
                nc.vector.tensor_scalar(c2[:, 2 * NE:3 * NE], at["router"], -2.0, None, ALU.mult).then_inc(c2_sq, 1)
                dve.wait_ge(c2_ps, 1)
                nc.vector.tensor_copy(c2[:, NE:2 * NE], ps[:, 7, 0:NE])
                source, bias = c2[:, 2 * NE:3 * NE], c2[:, NE:2 * NE]
            else:
                source, bias = at["router"], at["logit_bias"]
            if by_distance:
                dve.wait_ge(c2_sq, 2)
            nc.vector.tensor_copy(router_hi[:, :], source).then_inc(split_setup, 1)
            dve.wait_ge(split_setup, 1)
            nc.vector.tensor_tensor(router_lo[:, :], source, router_hi[:, :].bitcast(F32), ALU.subtract).then_inc(
                split_setup, 1)
            dve.wait_ge(split_setup, 2)

            def front(i):
                front_chain.begin(i)
                yield from skip(20)
                norm_in.moments(nc, dve, front_chain, lambda j: x[:, i * RT + j, :])
                dve.wait_ge(norm_in.rstd_ready.sem, norm_in.rstd_ready.at(i, 1))
                for j in range(RT):
                    last = norm_in.apply(nc, j, y[:, j, :], x[:, i * RT + j, :])
                last.then_inc(y_ready.sem, 1)
                yield from skip(N - 20)
                dve.wait_ge(y_hi_ready.sem, y_hi_ready.at(i, 1))
                nc.vector.tensor_tensor(y_lo[:, :], ps[:, 6, :], y_hi[:, :].bitcast(F32), ALU.subtract).then_inc(
                    y_lo_ready.sem, 1)
                yield
                front_chain.end()

            def route(i, part):
                if part == 0:
                    dve.wait_ge(router_ps.sem, router_ps.at(i, 1))
                    bc = bias.rearrange("p (o e) -> p o e", o=1).to_broadcast([P, RT, NE])
                    nc.vector.tensor_tensor(
                        score[:, :, :], ps[:, 7, 0:RT * NE].rearrange("p (t e) -> p t e", t=RT), bc, ALU.add).then_inc(back_chain.next(), 1)
                    dve.wait_ge(back_chain.sem, back_chain.so_far())
                    if by_distance:
                        dve.wait_ge(sq_ready.sem, sq_ready.at(i, 1))
                        nc.vector.tensor_tensor(
                            score[:, :, :], score[:, :, :],
                            sq_y[:, :].rearrange("p (t o) -> p t o", o=1).to_broadcast([P, RT, NE]), ALU.add).then_inc(back_chain.next(), 1)
                        dve.wait_ge(back_chain.sem, back_chain.so_far())
                        nc.vector.tensor_scalar(score[:, :, :], score[:, :, :], 1e-12, None, ALU.max).then_inc(
                            d2_ready.sem, 1)
                elif part == 1:
                    if by_distance:
                        dve.wait_ge(dist_ready.sem, dist_ready.at(i, 1))
                        own_wait(dve, st.dve_waited)
                    for t in range(RT):
                        last = nc.vector.max(top[:, t, :], score[:, t, :])
                    last.then_inc(back_chain.next(), 1)
                    dve.wait_ge(back_chain.sem, back_chain.so_far())
                    nc.vector.tensor_tensor(gap[:, :], top[:, :, 1], top[:, :, 0], ALU.subtract).then_inc(
                        gap_ready.sem, 1)
                    for t in range(RT):
                        last = nc.vector.max_index(top_at[:, t, :], top[:, t, :], score[:, t, :])
                    last.then_inc(back_chain.next(), 1)
                    dve.wait_ge(back_chain.sem, back_chain.so_far())
                    nc.vector.tensor_copy(top_atf[:, :, :], top_at[:, :, 0:2]).then_inc(back_chain.next(), 1)
                elif part == 2:
                    dve.wait_ge(back_chain.sem, back_chain.so_far())
                    dve.wait_ge(th_ready.sem, th_ready.at(i, 1))
                    nc.vector.tensor_scalar(share[:, :, 0], th[:, :], -0.5, 0.5, ALU.mult, ALU.add)
                    nc.vector.tensor_scalar(share[:, :, 1], th[:, :], 0.5, 0.5, ALU.mult, ALU.add)
                    io = at["iota"].rearrange("p (o e) -> p o e", o=1).to_broadcast([P, RT, NE])
                    for k in range(2):
                        last = nc.vector.tensor_tensor(
                            one_hot[:, :, k, :], io,
                            top_atf[:, :, k:k + 1].to_broadcast([P, RT, NE]), ALU.is_equal)
                    last.then_inc(back_chain.next(), 1)
                    dve.wait_ge(back_chain.sem, back_chain.so_far())
                    for k in range(2):
                        last = nc.vector.tensor_tensor(one_hot[:, :, k, :], one_hot[:, :, k, :],
                                                       share[:, :, k:k + 1].to_broadcast([P, RT, NE]), ALU.mult)
                    last.then_inc(back_chain.next(), 1)
                    dve.wait_ge(back_chain.sem, back_chain.so_far())
                    last = nc.vector.tensor_tensor(we[:, :, :], one_hot[:, :, 0, :], one_hot[:, :, 1, :], ALU.add)
                    if by_distance:
                        last.then_inc(we_ready.sem, 1)
                        dve.wait_ge(we_ready.sem, we_ready.at(i, 1))
                    else:
                        last.then_inc(back_chain.next(), 1)
                        dve.wait_ge(back_chain.sem, back_chain.so_far())
                        nc.vector.memset(we[:, :, NE - 1:NE], 1.0).then_inc(we_ready.sem, 1)
                        dve.wait_ge(we_ready.sem, we_ready.at(i, 1))
                elif part == 3 and by_distance:
                    dve.wait_ge(b2_ps.sem, b2_ps.at(i, 1))
                    nc.vector.tensor_copy(acc[:, :, :], ps[:, 7, :].rearrange("p (t d) -> p t d", t=RT)).then_inc(
                        acc_start.sem, 1)
                    dve.wait_ge(acc_start.sem, acc_start.at(i, 1))

            def back(i):
                back_chain.begin(i)

                def low_part(n):
                    e, c, r = n // FC, n % FC, rows_of[n % FC]
                    dve.wait_ge(hi_done.sem, hi_done.at(i, n + 1))
                    nc.vector.tensor_tensor(h_lo[e % 2][0:r, c, :], h[n % 2][0:r, :],
                                            h_hi[e % 2][0:r, c, :].bitcast(F32), ALU.subtract).then_inc(lo_done.sem, 1)

                def accumulate(e):
                    dve.wait_ge(down_ps.sem, down_ps.at(i, e + 1))
                    if e > 0:
                        dve.wait_ge(acc_done.sem, acc_done.at(i, e))
                    bank = ps[:, 4 + e % 2, :]
                    for t in range(RT):
                        o, d = acc[:, t, :], bank[:, t * P:(t + 1) * P]
                        if e == 0 and not by_distance:
                            last = nc.vector.tensor_scalar(o, d, we[:, t, e:e + 1], None, ALU.mult)
                        else:
                            last = nc.vector.scalar_tensor_tensor(o, d, we[:, t, e:e + 1], o, ALU.mult, ALU.add)
                    last.then_inc(acc_done.sem, 1)

                for n in range(N):
                    e, c, r = n // FC, n % FC, rows_of[n % FC]
                    dve.wait_ge(silu_done.sem, silu_done.at(i, n + 1))
                    dve.wait_ge(up_ps.sem, up_ps.at(i, n + 1))
                    up = ps[0:r, 2 + n % 2, :]
                    if n < 2:
                        dve.wait_ge(lo_done.sem, lo_done.at(i, N - 1 + n, 1))
                    else:
                        dve.wait_ge(lo_done.sem, lo_done.at(i, n - 1))
                    if by_distance:
                        last = nc.vector.scalar_tensor_tensor(h[n % 2][0:r, :], up, at["up_b"][0:r, n:n + 1],
                                                              gate[n % 2][0:r, :], ALU.add, ALU.mult)
                    else:
                        last = nc.vector.tensor_tensor(h[n % 2][0:r, :], up, gate[n % 2][0:r, :], ALU.mult)
                    last.then_inc(h_done.sem, 1)
                    if n > 0:
                        dve.wait_ge(h_done.sem, h_done.at(i, n))
                        low_part(n - 1)
                    if n in (1, 2, 3, 4):
                        route(i, n - 1)
                    if e >= 1 and c == 2:
                        accumulate(e - 1)
                    yield
                dve.wait_ge(h_done.sem, h_done.at(i, N))
                low_part(N - 1)
                yield
                yield
                accumulate(NE - 1)
                dve.wait_ge(acc_done.sem, acc_done.at(i, NE))
                norm_out.moments(nc, dve, back_chain, lambda j: acc[:, j, :])
                yield
                add_normed(nc, dve, back_chain, norm_out, i, x, i * RT, acc)
                dve.wait_ge(back_chain.sem, back_chain.so_far())
                back_chain.end()
                yield

            run_pipeline(dve, front, back)

        @block.scalar
        def _(act):
            nc.scalar.preload_act_table(ACT.Silu)
            sigs = [y_hi_ready, th_ready, silu_done, hi_done]
            if by_distance:
                sigs += [sq_ready, weT_ready]
            for s in sigs:
                s.credit(act)
            act.wait_ge(loaded, 16)

            def front(i):
                yield from skip(N)
                act.wait_ge(yT_ps.sem, yT_ps.at(i, 1))
                act.wait_ge(up_ps.sem, up_ps.at(i, N, 1))
                nc.scalar.activation(y_hi[:, :], ps[:, 6, :], ACT.Copy).then_inc(y_hi_ready.sem, 1)
                if by_distance:
                    act.wait_ge(d2_ready.sem, d2_ready.at(i, 1, 1))
                    for t in range(RT):
                        last = nc.scalar.activation(square[:, t, :], y[:, t, :], ACT.Square, accum_out=sq_y[:, t:t + 1])
                    last.then_inc(sq_ready.sem, 1)
                yield

            def back(i):
                def high_part(n):
                    e, c, r = n // FC, n % FC, rows_of[n % FC]
                    act.wait_ge(h_done.sem, h_done.at(i, n + 1))
                    if e < 2:
                        act.wait_ge(down_ps.sem, down_ps.at(i, e + NE - 1, 1))
                    else:
                        act.wait_ge(down_ps.sem, down_ps.at(i, e - 1))
                    nc.scalar.activation(h_hi[e % 2][0:r, c, :], h[n % 2][0:r, :], ACT.Copy).then_inc(hi_done.sem, 1)

                for n in range(N):
                    e, c, r = n // FC, n % FC, rows_of[n % FC]
                    act.wait_ge(gate_ps.sem, gate_ps.at(i, n + 1))
                    bias = at["gate_b"][0:r, n:n + 1] if by_distance else 0.0
                    nc.scalar.activation(gate[n % 2][0:r, :], ps[0:r, n % 2, :], ACT.Silu, bias=bias).then_inc(
                        silu_done.sem, 1)
                    if n > 0:
                        high_part(n - 1)
                    if n == 2:
                        act.wait_ge(gap_ready.sem, gap_ready.at(i, 1))
                        nc.scalar.activation(th[:, :], gap[:, :], ACT.Tanh, scale=0.5).then_inc(th_ready.sem, 1)
                    if n == 3 and by_distance:
                        act.wait_ge(weT_ps.sem, weT_ps.at(i, 1))
                        nc.scalar.activation(weT[:, :], ps[0:NE, 7, :], ACT.Copy).then_inc(weT_ready.sem, 1)
                    yield
                high_part(N - 1)
                yield

            run_pipeline(act, front, back)

        @block.tensor
        def _(pe):
            mm = nc.tensor.matmul
            sigs = [yT_ps, router_ps, gate_ps, up_ps, down_ps]
            if by_distance:
                sigs += [weT_ps, b2_ps]
            for s in sigs:
                s.credit(pe)
            pe.wait_ge(loaded, 16)
            if by_distance:
                pe.wait_ge(ones_ready, 1)
                pe.wait_ge(c2_sq, 1)
                mm(ps[:, 7, 0:NE], ones[:, :], c2[:, 0:NE], start=True, stop=True).then_inc(c2_ps, 1)
            pe.wait_ge(split_setup, 2)

            def three(o, a_hi, a_lo, b_hi, b_lo, first=True, end=True):
                mm(o, a_hi, b_hi, start=first, stop=False)
                mm(o, a_hi, b_lo, start=False, stop=False)
                return mm(o, a_lo, b_hi, start=False, stop=end)

            def front(i):
                yield from skip(21)
                pe.wait_ge(y_ready.sem, y_ready.at(i, 1))
                pe.wait_ge(y_lo_ready.sem, y_lo_ready.at(i, 1, 1))
                for t in range(RT):
                    last = nc.tensor.transpose(ps[:, 6, t * P:(t + 1) * P], y[:, t, :], g.ident[:, :])
                last.then_inc(yT_ps.sem, 1)
                yield from skip(N + 1 - 21)
                pe.wait_ge(y_lo_ready.sem, y_lo_ready.at(i, 1))
                for t in range(RT):
                    s = slice(t * P, (t + 1) * P)
                    last = three(ps[:, 7, t * NE:(t + 1) * NE], y_hi[:, s], y_lo[:, s], router_hi[:, :], router_lo[:, :])
                last.then_inc(router_ps.sem, 1)
                yield

            def back(i):
                def down(e):
                    pe.wait_ge(lo_done.sem, lo_done.at(i, e * FC + FC))
                    if e < 2:
                        pe.wait_ge(acc_done.sem, acc_done.at(i, e + NE - 1, 1))
                    else:
                        pe.wait_ge(acc_done.sem, acc_done.at(i, e - 1))
                    for t in range(RT):
                        s = slice(t * P, (t + 1) * P)
                        for c in range(FC):
                            r = rows_of[c]
                            last = three(ps[:, 4 + e % 2, s], h_hi[e % 2][0:r, c, s], h_lo[e % 2][0:r, c, s],
                                         w["down_hi"][0:r, e, c, :], w["down_lo"][0:r, e, c, :], c == 0, c == FC - 1)
                    last.then_inc(down_ps.sem, 1)

                for n in range(N):
                    e, c, r = n // FC, n % FC, rows_of[n % FC]
                    for k, (bank, free, done) in enumerate(((n % 2, silu_done, gate_ps), (2 + n % 2, h_done, up_ps))):
                        if n < 2:
                            pe.wait_ge(free.sem, free.at(i, N - 1 + n, 1))
                        else:
                            pe.wait_ge(free.sem, free.at(i, n - 1))
                        s = slice(k * width + c * P, k * width + c * P + r)
                        o = ps[0:r, bank, :]
                        mm(o, w["gu_hi"][:, e, s], y_hi[:, :], start=True, stop=False)
                        mm(o, w["gu_hi"][:, e, s], y_lo[:, :], start=False, stop=False)
                        mm(o, w["gu_lo"][:, e, s], y_hi[:, :], start=False, stop=True).then_inc(done.sem, 1)
                    if e >= 1 and c == 1:
                        down(e - 1)
                    if by_distance and n == 3:
                        pe.wait_ge(we_ready.sem, we_ready.at(i, 1))
                        for t in range(RT):
                            last = nc.tensor.transpose(ps[0:NE, 7, t * P:(t + 1) * P], we[:, t, :], g.ident[:, :])
                        last.then_inc(weT_ps.sem, 1)
                        pe.wait_ge(weT_ready.sem, weT_ready.at(i, 1))
                        for t in range(RT):
                            last = mm(ps[:, 7, t * P:(t + 1) * P], weT[:, t * P:(t + 1) * P], at["down_b"][0:NE, :],
                                      start=True, stop=True)
                        last.then_inc(b2_ps.sem, 1)
                    yield
                yield
                down(NE - 1)
                yield

            run_pipeline(pe, front, back)



F_SEL = 2 * P
SEL = [("nav_w", P), ("nav_b", 1), ("choose_w", NE), ("choose_b", NE), ("wo", P), ("bo", P)]
SEL_EXPERT = [("w1", F_SEL), ("w2", F_SEL), ("b1", F_SEL // P), ("b2", 1)]


def columns(tensor, names):
    at, off = {}, 0
    for name, width in names:
        at[name] = tensor[:, off:off + width]
        off += width
    assert off == tensor.shape[1]
    return at


def selected_ffn(nc, g, layer, blob, experts_dram):
    x = g.x
    with ExitStack() as ctx:
        st = Stage(nc, ctx, f"f{layer}")
        ps = st.ps
        wb = st.sb("w", [P, blob.shape[1]])
        at = columns(wb, SEL)
        expert = [st.sb(f"expert{k}", [P, experts_dram.shape[2]]) for k in range(2)]
        ex = [columns(e, SEL_EXPERT) for e in expert]
        y = [st.sb(f"y{k}", [P, T, P]) for k in range(2)]
        yT = [st.sb(f"yT{k}", [P, SEQ]) for k in range(2)]
        nav = st.sb("nav", [P, 1])
        logits, best = st.sb("logits", [1, NE]), st.sb("best", [1, 8])
        chosen = [st.sb(f"chosen{k}", [1, 8], U32) for k in range(2)]
        hT = st.sb("hT", [P, 2, SEQ])
        rT = st.sb("rT", [P, SEQ])
        f = st.sb("f", [P, T, P])
        bo = st.sb("bo", [P, P])
        norm_in, norm_out = Norm(st, "in", T), Norm(st, "out", T)
        loaded, bo_ready = st.sem("loaded"), st.sem("bo_ready")
        y_ready, yT_ps, yT_ready = st.sig("y_ready", 1), st.sig("yT_ps", 1), st.sig("yT_ready", 1)
        nav_ps, nav_ready = st.sig("nav_ps", 1), st.sig("nav_ready", 1)
        logit_ps, chosen_ready = st.sig("logit_ps", 1), st.sig("chosen_ready", 1)
        expert_loaded = [st.sem(f"expert_loaded{k}") for k in range(2)]
        h_ps, h_ready = st.sig("h_ps", 2), st.sig("h_ready", 2)
        r_ps, r_ready = st.sig("r_ps", 1), st.sig("r_ready", 1)
        out_ps, f_ready = st.sig("out_ps", 1), st.sig("f_ready", 1)
        front_chain = Chain(st.sem("dve_front"), Norm.CHAIN + 2)
        back_chain = Chain(st.sem("dve_back"), Norm.CHAIN + 3)
        block = ctx.enter_context(nc.Block())

        @block.sync
        def _(sp):
            sp.dma_start(wb[:, :], blob).then_inc(loaded, 16)

            def front(i, p):
                yield
                yield
                yield
                sp.wait_ge(chosen_ready.sem, chosen_ready.at(i, 1))
                own_wait(sp, st.sp_waited)
                sp.wait_ge(f_ready.sem, f_ready.at(i, 1, 2))
                own_wait(sp, st.sp_waited)
                e = sp.value_load(chosen[p][0:1, 0:1], min_val=0, max_val=NE - 1)
                sp.dma_start(expert[p][:, :], experts_dram[e, :, :]).then_inc(expert_loaded[p], 16)
                yield

            pipeline(sp, front, lambda i, p: iter(()))

        @block.gpsimd
        def _(pool):
            norm_in.rstd_ready.credit(pool)
            norm_out.rstd_ready.credit(pool)

            def front(i, p):
                norm_in.power(nc, pool, i, g.minus_half)
                yield

            def back(i, p):
                yield
                yield
                norm_out.power(nc, pool, i, g.minus_half)
                yield

            pipeline(pool, front, back)

        @block.vector
        def _(dve):
            for s in (norm_in.var_ready, norm_out.var_ready, y_ready, chosen_ready, f_ready, front_chain.sig,
                      back_chain.sig):
                s.credit(dve)
            dve.wait_ge(loaded, 16)
            nc.vector.tensor_scalar(bo[:, :], at["bo"], 0.3, None, ALU.mult).then_inc(bo_ready, 1)
            dve.wait_ge(bo_ready, 1)

            def front(i, p):
                front_chain.begin(i)
                norm_in.moments(nc, dve, front_chain, lambda j: x[:, i * T + j, :])
                dve.wait_ge(norm_in.rstd_ready.sem, norm_in.rstd_ready.at(i, 1))
                dve.wait_ge(f_ready.sem, f_ready.at(i, 1, 2))
                for j in range(T):
                    last = norm_in.apply(nc, j, y[p][:, j, :], x[:, i * T + j, :])
                last.then_inc(y_ready.sem, 1)
                yield
                yield
                yield
                dve.wait_ge(logit_ps.sem, logit_ps.at(i, 1))
                nc.vector.tensor_tensor(logits[:, :], ps[0:1, 0, 0:NE], at["choose_b"][0:1, :], ALU.add).then_inc(front_chain.next(), 1)
                dve.wait_ge(front_chain.sem, front_chain.so_far())
                own_wait(dve, st.dve_waited)
                nc.vector.max(best[:, :], logits[:, :]).then_inc(front_chain.next(), 1)
                dve.wait_ge(front_chain.sem, front_chain.so_far())
                own_wait(dve, st.dve_waited)
                nc.vector.max_index(chosen[p][:, :], best[:, :], logits[:, :]).then_inc(chosen_ready.sem, 1)
                dve.wait_ge(chosen_ready.sem, chosen_ready.at(i, 1))
                yield
                front_chain.end()

            def back(i, p):
                back_chain.begin(i)
                yield
                yield
                dve.wait_ge(y_ready.sem, y_ready.at(i, 1))
                for t in range(T):
                    last = nc.vector.tensor_tensor(y[p][:, t, :], y[p][:, t, :], bo[:, :], ALU.add)
                last.then_inc(back_chain.next(), 1)
                dve.wait_ge(back_chain.sem, back_chain.so_far())
                dve.wait_ge(out_ps.sem, out_ps.at(i, 1))
                nc.vector.scalar_tensor_tensor(f[:, :, :], ps[:, 5, 0:SEQ].rearrange("p (t d) -> p t d", t=T), 0.3,
                                               y[p][:, :, :], ALU.mult, ALU.add).then_inc(f_ready.sem, 1)
                dve.wait_ge(f_ready.sem, f_ready.at(i, 1))
                norm_out.moments(nc, dve, back_chain, lambda j: f[:, j, :])
                yield
                add_normed(nc, dve, back_chain, norm_out, i, x, i * T, f)
                dve.wait_ge(back_chain.sem, back_chain.so_far())
                back_chain.end()
                yield

            pipeline(dve, front, back)

        @block.scalar
        def _(act):
            nc.scalar.preload_act_table(ACT.Gelu)
            for s in (yT_ready, nav_ready, h_ready, r_ready):
                s.credit(act)
            act.wait_ge(loaded, 16)

            def front(i, p):
                yield
                act.wait_ge(yT_ps.sem, yT_ps.at(i, 1))
                act.wait_ge(h_ps.sem, h_ps.at(i, 2, 2))
                nc.scalar.activation(yT[p][:, :], ps[:, 0, 0:SEQ], ACT.Copy).then_inc(yT_ready.sem, 1)
                yield
                act.wait_ge(nav_ps.sem, nav_ps.at(i, 1))
                nc.scalar.activation(nav[:, :], ps[:, 1, 0:1], ACT.Gelu, bias=at["nav_b"]).then_inc(nav_ready.sem, 1)
                yield

            def back(i, p):
                act.wait_ge(expert_loaded[p], (i - p) * 8 + 16)
                for c in range(2):
                    act.wait_ge(h_ps.sem, h_ps.at(i, c + 1))
                    nc.scalar.activation(hT[:, c, :], ps[:, 2 + c, 0:SEQ], ACT.Gelu, bias=ex[p]["b1"][:, c:c + 1]).then_inc(
                        h_ready.sem, 1)
                yield
                act.wait_ge(r_ps.sem, r_ps.at(i, 1))
                nc.scalar.activation(rT[:, :], ps[:, 4, 0:SEQ], ACT.Identity, bias=ex[p]["b2"]).then_inc(r_ready.sem, 1)
                yield

            pipeline(act, front, back)

        @block.tensor
        def _(pe):
            mm = nc.tensor.matmul
            for s in (yT_ps, nav_ps, logit_ps, h_ps, r_ps, out_ps):
                s.credit(pe)
            pe.wait_ge(loaded, 16)

            def front(i, p):
                yield
                pe.wait_ge(y_ready.sem, y_ready.at(i, 1))
                pe.wait_ge(chosen_ready.sem, chosen_ready.at(i, 1, 1))
                for t in range(T):
                    last = nc.tensor.transpose(ps[:, 0, t * P:(t + 1) * P], y[p][:, t, :], g.ident[:, :])
                last.then_inc(yT_ps.sem, 1)
                yield
                pe.wait_ge(yT_ready.sem, yT_ready.at(i, 1))
                pe.wait_ge(nav_ready.sem, nav_ready.at(i, 1, 1))
                mm(ps[:, 1, 0:1], at["nav_w"], yT[p][:, SEQ - 1:SEQ], start=True, stop=True).then_inc(nav_ps.sem, 1)
                yield
                pe.wait_ge(nav_ready.sem, nav_ready.at(i, 1))
                mm(ps[0:1, 0, 0:NE], nav[:, :], at["choose_w"], start=True, stop=True).then_inc(logit_ps.sem, 1)
                yield

            def back(i, p):
                pe.wait_ge(expert_loaded[p], (i - p) * 8 + 16)
                for c in range(2):
                    pe.wait_ge(h_ready.sem, h_ready.at(i, c + 1, 1))
                    mm(ps[:, 2 + c, 0:SEQ], ex[p]["w1"][:, c * P:(c + 1) * P], yT[p][:, :], start=True,
                       stop=True).then_inc(h_ps.sem, 1)
                yield
                pe.wait_ge(r_ready.sem, r_ready.at(i, 1, 1))
                for c in range(2):
                    pe.wait_ge(h_ready.sem, h_ready.at(i, c + 1))
                    last = mm(ps[:, 4, 0:SEQ], ex[p]["w2"][:, c * P:(c + 1) * P], hT[:, c, :], start=c == 0, stop=c == 1)
                last.then_inc(r_ps.sem, 1)
                yield
                pe.wait_ge(r_ready.sem, r_ready.at(i, 1))
                pe.wait_ge(f_ready.sem, f_ready.at(i, 1, 1))
                for t in range(T):
                    last = mm(ps[:, 5, t * P:(t + 1) * P], rT[:, t * P:(t + 1) * P], at["wo"], start=True, stop=True)
                last.then_inc(out_ps.sem, 1)
                yield

            pipeline(pe, front, back)



MIX = [("wqk", 2 * P), ("wv", P), ("wo", P), ("blocks", P)]


def channel_attention(nc, g, blob):
    SCALE = float(D8) ** -0.5
    x = g.x
    with ExitStack() as ctx:
        st = Stage(nc, ctx, "a3")
        ps = st.ps
        wb = st.sb("w", [P, blob.shape[1]])
        at = columns(wb, MIX)
        y = st.sb("y", [P, T, P])
        yT = st.sb("yT", [P, SEQ])
        qk = [st.sb(f"qk{k}", [P, T, 2 * P]) for k in range(2)]
        vT = [st.sb(f"vT{k}", [P, SEQ]) for k in range(2)]
        z, z_exp, zn = st.sb("z", [P, P]), st.sb("z_exp", [P, P]), st.sb("zn", [P, P])
        top, neg_top, total, recip = (st.sb(n, [P, 1]) for n in ("top", "neg_top", "total", "recip"))
        cxT = st.sb("cxT", [P, SEQ])
        f = st.sb("f", [P, T, P])
        norm_in, norm_out = Norm(st, "in", T), Norm(st, "out", T)
        loaded = st.sem("loaded")
        y_ready, yT_ps, yT_ready = st.sig("y_ready", 1), st.sig("yT_ps", 1), st.sig("yT_ready", 1)
        qk_ps, qk_ready, v_ps, v_ready = (st.sig(n, 1) for n in ("qk_ps", "qk_ready", "v_ps", "v_ready"))
        z_ps, top_ready, exp_ready, zn_ready = (st.sig(n, 1) for n in ("z_ps", "top_ready", "exp_ready", "zn_ready"))
        cxT_ps, cxT_ready, out_ps, f_ready = (st.sig(n, 1) for n in ("cxT_ps", "cxT_ready", "out_ps", "f_ready"))
        front_chain = Chain(st.sem("dve_front"), Norm.CHAIN)
        back_chain = Chain(st.sem("dve_back"), Norm.CHAIN + 5)
        block = ctx.enter_context(nc.Block())

        @block.sync
        def _(sp):
            sp.dma_start(wb[:, :], blob).then_inc(loaded, 16)

        @block.gpsimd
        def _(pool):
            norm_in.rstd_ready.credit(pool)
            norm_out.rstd_ready.credit(pool)

            def front(i, p):
                norm_in.power(nc, pool, i, g.minus_half)
                yield

            def back(i, p):
                yield
                yield
                yield
                norm_out.power(nc, pool, i, g.minus_half)
                yield

            pipeline(pool, front, back)

        @block.vector
        def _(dve):
            for s in (norm_in.var_ready, norm_out.var_ready, y_ready, top_ready, zn_ready, f_ready, front_chain.sig,
                      back_chain.sig):
                s.credit(dve)
            dve.wait_ge(loaded, 16)

            def front(i, p):
                front_chain.begin(i)
                norm_in.moments(nc, dve, front_chain, lambda j: x[:, i * T + j, :])
                dve.wait_ge(norm_in.rstd_ready.sem, norm_in.rstd_ready.at(i, 1))
                for j in range(T):
                    last = norm_in.apply(nc, j, y[:, j, :], x[:, i * T + j, :])
                last.then_inc(y_ready.sem, 1)
                yield
                front_chain.end()

            def back(i, p):
                back_chain.begin(i)
                dve.wait_ge(z_ps.sem, z_ps.at(i, 1))
                nc.vector.tensor_tensor(z[:, :], ps[:, 2, 0:P], at["blocks"], ALU.add).then_inc(back_chain.next(), 1)
                dve.wait_ge(back_chain.sem, back_chain.so_far())
                nc.vector.reduce_max(top[:, :], z[:, :], AX).then_inc(back_chain.next(), 1)
                dve.wait_ge(back_chain.sem, back_chain.so_far())
                nc.vector.tensor_scalar(neg_top[:, :], top[:, :], -SCALE, None, ALU.mult).then_inc(top_ready.sem, 1)
                yield
                dve.wait_ge(exp_ready.sem, exp_ready.at(i, 1))
                nc.vector.reciprocal(recip[:, :], total[:, :]).then_inc(back_chain.next(), 1)
                dve.wait_ge(back_chain.sem, back_chain.so_far())
                nc.vector.tensor_scalar(zn[:, :], z_exp[:, :], recip[:, 0:1], None, ALU.mult).then_inc(zn_ready.sem, 1)
                yield
                yield
                dve.wait_ge(out_ps.sem, out_ps.at(i, 1))
                nc.vector.tensor_copy(f[:, :, :], ps[:, 4, 0:SEQ].rearrange("p (t d) -> p t d", t=T)).then_inc(
                    f_ready.sem, 1)
                dve.wait_ge(f_ready.sem, f_ready.at(i, 1))
                norm_out.moments(nc, dve, back_chain, lambda j: f[:, j, :])
                yield
                add_normed(nc, dve, back_chain, norm_out, i, x, i * T, f)
                dve.wait_ge(back_chain.sem, back_chain.so_far())
                back_chain.end()
                yield

            pipeline(dve, front, back)

        @block.scalar
        def _(act):
            nc.scalar.preload_act_table(ACT.Exp)
            for s in (yT_ready, qk_ready, v_ready, exp_ready, cxT_ready):
                s.credit(act)

            def front(i, p):
                yield
                act.wait_ge(yT_ps.sem, yT_ps.at(i, 1))
                nc.scalar.activation(yT[:, :], ps[:, 0, 0:SEQ], ACT.Copy).then_inc(yT_ready.sem, 1)
                yield
                act.wait_ge(qk_ps.sem, qk_ps.at(i, 1))
                nc.scalar.activation(qk[p][:, :, :], ps[:, 1, :].rearrange("p (t d) -> p t d", t=T), ACT.Copy).then_inc(
                    qk_ready.sem, 1)
                act.wait_ge(v_ps.sem, v_ps.at(i, 1))
                nc.scalar.activation(vT[p][:, :], ps[:, 0, 0:SEQ], ACT.Copy).then_inc(v_ready.sem, 1)
                yield

            def back(i, p):
                act.wait_ge(top_ready.sem, top_ready.at(i, 1))
                act.wait_ge(zn_ready.sem, zn_ready.at(i, 1, 1))
                nc.scalar.activation(z_exp[:, :], z[:, :], ACT.Exp, bias=neg_top[:, :], scale=SCALE,
                                     accum_out=total[:, :]).then_inc(exp_ready.sem, 1)
                yield
                yield
                act.wait_ge(cxT_ps.sem, cxT_ps.at(i, 1))
                nc.scalar.activation(cxT[:, :], ps[:, 3, 0:SEQ], ACT.Copy).then_inc(cxT_ready.sem, 1)
                yield

            pipeline(act, front, back)

        @block.tensor
        def _(pe):
            mm = nc.tensor.matmul
            for s in (yT_ps, qk_ps, v_ps, z_ps, cxT_ps, out_ps):
                s.credit(pe)
            pe.wait_ge(loaded, 16)

            def front(i, p):
                yield
                pe.wait_ge(y_ready.sem, y_ready.at(i, 1))
                pe.wait_ge(v_ready.sem, v_ready.at(i, 1, 1))
                for t in range(T):
                    last = nc.tensor.transpose(ps[:, 0, t * P:(t + 1) * P], y[:, t, :], g.ident[:, :])
                last.then_inc(yT_ps.sem, 1)
                yield
                pe.wait_ge(yT_ready.sem, yT_ready.at(i, 1))
                pe.wait_ge(qk_ready.sem, qk_ready.at(i, 1, 1))
                for t in range(T):
                    last = mm(ps[:, 1, t * 2 * P:(t + 1) * 2 * P], yT[:, t * P:(t + 1) * P], at["wqk"], start=True,
                              stop=True)
                last.then_inc(qk_ps.sem, 1)
                mm(ps[:, 0, 0:SEQ], at["wv"], yT[:, :], start=True, stop=True).then_inc(v_ps.sem, 1)
                yield

            def back(i, p):
                pe.wait_ge(qk_ready.sem, qk_ready.at(i, 1))
                pe.wait_ge(top_ready.sem, top_ready.at(i, 1, 1))
                for t in range(T):
                    last = mm(ps[:, 2, 0:P], qk[p][:, t, P:2 * P], qk[p][:, t, 0:P], start=t == 0, stop=t == T - 1)
                last.then_inc(z_ps.sem, 1)
                yield
                yield
                pe.wait_ge(zn_ready.sem, zn_ready.at(i, 1))
                pe.wait_ge(v_ready.sem, v_ready.at(i, 1))
                pe.wait_ge(cxT_ready.sem, cxT_ready.at(i, 1, 1))
                mm(ps[:, 3, 0:SEQ], zn[:, :], vT[p][:, :], start=True, stop=True).then_inc(cxT_ps.sem, 1)
                yield
                pe.wait_ge(cxT_ready.sem, cxT_ready.at(i, 1))
                pe.wait_ge(f_ready.sem, f_ready.at(i, 1, 1))
                for t in range(T):
                    last = mm(ps[:, 4, t * P:(t + 1) * P], cxT[:, t * P:(t + 1) * P], at["wo"], start=True, stop=True)
                last.then_inc(out_ps.sem, 1)
                yield

            pipeline(pe, front, back)



GQA = [("wq", NH * D64), ("wk", NG * P), ("wv", NG * D64), ("wpost", NH * D64)]


def grouped_attention(nc, g, blob):
    SCALE = float(D64) ** -0.5
    DV = D64 + 1
    PAIRS = NH // 2
    x = g.x
    with ExitStack() as ctx:
        st = Stage(nc, ctx, "a2")
        ps = st.ps
        wb = st.sb("w", [P, blob.shape[1]])
        at = columns(wb, GQA)
        y = [st.sb(f"y{k}", [P, T, P]) for k in range(2)]
        f = st.sb("f", [P, T, P])
        yT = st.sb("yT", [P, SEQ])
        Q = {part: [st.sb(f"q_{part}{k}", [P, PAIRS, SEQ], F32R) for k in range(2)] for part in ("hi", "lo")}
        K = {part: [st.sb(f"k_{part}{k}", [P, 2, NG, SEQ], F32R) for k in range(2)] for part in ("hi", "lo")}
        V = [st.sb(f"V{k}", [P, T, NG, DV]) for k in range(2)]
        rowmax = st.sb("rowmax", [P, T, NH])
        mrow = [st.sb(f"mrow{k}", [NG, SEQ], F32R) for k in range(NG)]
        maxima = st.sb("maxima", [P, NG, HG * SEQ], F32R)
        ones_row = st.sb("ones_row", [P, P], F32R)
        ones_raw = st.sb("ones_raw", [P, P])
        probs = [st.sb(f"probs{k}", [P, 4, BANK]) for k in range(2)]
        recip = st.sb("recip", [P, HG])
        cx = st.sb("cx", [P, T, NH * D64])
        cxT = st.sb("cxT", [P, PAIRS, SEQ])
        norm_in, norm_out = Norm(st, "in", T), Norm(st, "out", T)
        loaded, constants = st.sem("loaded"), st.sem("constants_ready")
        y_ready, yT_ps, yT_ready = st.sig("y_ready", 1), st.sig("yT_ps", 1), st.sig("yT_ready", 1)
        q_ps, q_hi_ready, q_lo_ready = st.sig("q_ps", NG), st.sig("q_hi_ready", NG), st.sig("q_lo_ready", NG)
        k_ps, k_hi_ready, k_lo_ready = st.sig("k_ps", 2), st.sig("k_hi_ready", 2), st.sig("k_lo_ready", 2)
        v_ps, v_ready = st.sig("v_ps", 1), st.sig("v_ready", 1)
        FILLS = 4
        score_ps, rowmax_ready = st.sig("score_ps", NG * FILLS), st.sig("rowmax_ready", NG * FILLS)
        max_ps, mrow_ready = st.sig("max_ps", NG), st.sig("mrow_ready", NG)
        mrow_placed = [st.sem(f"mrow_placed{j}") for j in range(NG)]
        sT_ps, exp_done = st.sig("sT_ps", NG * FILLS), st.sig("exp_done", NG * FILLS)
        pv_done, cx_ready = st.sig("pv_done", NG * T), st.sig("cx_ready", NG * T)
        cxT_ps, cxT_ready = st.sig("cxT_ps", NG), st.sig("cxT_ready", NG)
        out_ps, f_ready = st.sig("out_ps", 1), st.sig("f_ready", 1)
        front_chain = Chain(st.sem("dve_front"), Norm.CHAIN)
        back_chain = Chain(st.sem("dve_back"), Norm.CHAIN + 2 + NG * T)
        block = ctx.enter_context(nc.Block())

        @block.sync
        def _(sp):
            sp.dma_start(wb[:, :], blob).then_inc(loaded, 16)

            def front(i, p):
                for _ in range(5):
                    yield
                for j in range(NG):
                    sp.wait_ge(mrow_ready.sem, mrow_ready.at(i, j + 1))
                    own_wait(sp, st.sp_waited)
                    sp.wait_ge(sT_ps.sem, sT_ps.at(i, (j + 1) * FILLS, 1))
                    sp.dma_start(maxima[0:1, j, :].rearrange("p (h q) -> p h q", h=HG).bitcast(F32),
                                 mrow[j][:, :].bitcast(F32)).then_inc(mrow_placed[j], 16)
                    yield

            pipeline(sp, front, lambda i, p: iter(()))

        @block.gpsimd
        def _(pool):
            norm_in.rstd_ready.credit(pool)
            norm_out.rstd_ready.credit(pool)
            def front(i, p):
                norm_in.power(nc, pool, i, g.minus_half)
                yield

            def back(i, p):
                for _ in range(7):
                    yield
                norm_out.power(nc, pool, i, g.minus_half)
                yield

            pipeline(pool, front, back)

        @block.vector
        def _(dve):
            for s in (norm_in.var_ready, norm_out.var_ready, y_ready, q_lo_ready, k_lo_ready, v_ready,
                      rowmax_ready, cx_ready, f_ready, front_chain.sig, back_chain.sig):
                s.credit(dve)
            for k in range(2):
                for part in ("hi", "lo"):
                    nc.vector.memset(K[part][k][D64:P, 0, :, :].bitcast(F32), 0.0)
                    nc.vector.memset(K[part][k][0:D64, 1, :, :].bitcast(F32), 0.0)
                nc.vector.memset(V[k][:, :, :, D64:DV], 1.0)
            nc.vector.memset(maxima[:, :, :].bitcast(F32), 0.0)
            nc.vector.memset(ones_raw[:, :], 0.0).then_inc(constants, 1)
            dve.wait_ge(constants, 1)
            nc.vector.memset(ones_raw[0:1, :], 1.0).then_inc(constants, 1)
            dve.wait_ge(constants, 2)
            nc.vector.tensor_copy(ones_row[:, :], ones_raw[:, :]).then_inc(constants, 1)
            dve.wait_ge(constants, 3)

            def front(i, p):
                front_chain.begin(i)
                norm_in.moments(nc, dve, front_chain, lambda j: x[:, i * T + j, :])
                dve.wait_ge(norm_in.rstd_ready.sem, norm_in.rstd_ready.at(i, 1))
                dve.wait_ge(f_ready.sem, f_ready.at(i, 1, 2))
                for j in range(T):
                    last = norm_in.apply(nc, j, y[p][:, j, :], x[:, i * T + j, :])
                last.then_inc(y_ready.sem, 1)
                yield
                yield
                for j in range(NG):
                    dve.wait_ge(q_hi_ready.sem, q_hi_ready.at(i, j + 1))
                    nc.vector.tensor_tensor(Q["lo"][p][:, 2 * j:2 * j + 2, :],
                                            ps[:, (j + 1) % 2, :].rearrange("p (h t) -> p h t", h=2),
                                            Q["hi"][p][:, 2 * j:2 * j + 2, :].bitcast(F32), ALU.subtract).then_inc(
                        q_lo_ready.sem, 1)
                    if j == 1:
                        yield
                for n in range(2):
                    dve.wait_ge(k_hi_ready.sem, k_hi_ready.at(i, n + 1))
                    bank = ps[:, (n + 1) % 2, :].rearrange("p (g t) -> p g t", g=2)
                    for half, rows in enumerate((slice(0, D64), slice(D64, P))):
                        last = nc.vector.tensor_tensor(K["lo"][p][rows, half, 2 * n:2 * n + 2, :], bank[rows],
                                                       K["hi"][p][rows, half, 2 * n:2 * n + 2, :].bitcast(F32),
                                                       ALU.subtract)
                    last.then_inc(k_lo_ready.sem, 1)
                dve.wait_ge(v_ps.sem, v_ps.at(i, 1))
                dve.wait_ge(pv_done.sem, pv_done.at(i, NG * T, 2))
                nc.vector.tensor_copy(V[p][:, :, :, 0:D64],
                                      ps[:, 1, :].rearrange("p (t g d) -> p t g d", t=T, g=NG)).then_inc(v_ready.sem, 1)
                yield
                for j in range(NG):
                    if j == 0:
                        dve.wait_ge(max_ps.sem, max_ps.at(i, NG, 1))
                    for n in range(FILLS):
                        c = j * FILLS + n
                        dve.wait_ge(score_ps.sem, score_ps.at(i, c + 1))
                        t, h = n // 2, 4 * j + 2 * (n % 2)
                        nc.vector.reduce_max(rowmax[:, t, h:h + 2], ps[:, 2 + c % 2, :].rearrange("p (h k) -> p h k", h=2),
                                             AX).then_inc(rowmax_ready.sem, 1)
                    yield
                front_chain.end()

            def back(i, p):
                back_chain.begin(i)
                yield
                for j in range(NG):
                    for t in range(T):
                        dve.wait_ge(pv_done.sem, pv_done.at(i, j * T + t + 1))
                        if t == 0 and j == 0:
                            dve.wait_ge(cxT_ps.sem, cxT_ps.at(i, NG, 1))
                        c = ps[:, 6, 0:HG * DV].rearrange("p (h d) -> p h d", h=HG)
                        nc.vector.reciprocal(recip[:, :], c[:, :, D64]).then_inc(back_chain.next(), 1)
                        dve.wait_ge(back_chain.sem, back_chain.so_far())
                        nc.vector.tensor_tensor(
                            cx[:, t, j * HG * D64:(j + 1) * HG * D64].rearrange("p (h d) -> p h d", h=HG), c[:, :, 0:D64],
                            recip[:, :].rearrange("p (h o) -> p h o", o=1).to_broadcast([P, HG, D64]),
                            ALU.mult).then_inc(cx_ready.sem, 1)
                        dve.wait_ge(cx_ready.sem, cx_ready.at(i, j * T + t + 1))
                    yield
                yield
                yield
                dve.wait_ge(out_ps.sem, out_ps.at(i, 1))
                nc.vector.tensor_tensor(f[:, :, :], ps[:, 7, 0:SEQ].rearrange("p (t d) -> p t d", t=T), y[p][:, :, :],
                                        ALU.add).then_inc(f_ready.sem, 1)
                dve.wait_ge(f_ready.sem, f_ready.at(i, 1))
                norm_out.moments(nc, dve, back_chain, lambda j: f[:, j, :])
                yield
                add_normed(nc, dve, back_chain, norm_out, i, x, i * T, f)
                dve.wait_ge(back_chain.sem, back_chain.so_far())
                back_chain.end()
                yield

            pipeline(dve, front, back)

        @block.scalar
        def _(act):
            nc.scalar.preload_act_table(ACT.Exp)
            for s in (yT_ready, q_hi_ready, k_hi_ready, mrow_ready, exp_done, cxT_ready):
                s.credit(act)
            act.wait_ge(constants, 3)

            def front(i, p):
                yield
                act.wait_ge(yT_ps.sem, yT_ps.at(i, 1))
                nc.scalar.activation(yT[:, :], ps[:, 0, 0:SEQ], ACT.Copy).then_inc(yT_ready.sem, 1)
                yield
                act.wait_ge(sT_ps.sem, sT_ps.at(i, NG * FILLS, 2))
                for j in range(NG):
                    act.wait_ge(q_ps.sem, q_ps.at(i, j + 1))
                    nc.scalar.activation(Q["hi"][p][:, 2 * j:2 * j + 2, :],
                                         ps[:, (j + 1) % 2, :].rearrange("p (h t) -> p h t", h=2), ACT.Copy).then_inc(
                        q_hi_ready.sem, 1)
                    if j == 1:
                        yield
                for n in range(2):
                    act.wait_ge(k_ps.sem, k_ps.at(i, n + 1))
                    bank = ps[:, (n + 1) % 2, :].rearrange("p (g t) -> p g t", g=2)
                    for half, rows in enumerate((slice(0, D64), slice(D64, P))):
                        last = nc.scalar.activation(K["hi"][p][rows, half, 2 * n:2 * n + 2, :], bank[rows], ACT.Copy)
                    last.then_inc(k_hi_ready.sem, 1)
                yield
                yield
                for j in range(NG):
                    act.wait_ge(max_ps.sem, max_ps.at(i, j + 1))
                    pe_bank = j % 2
                    if j == 0:
                        act.wait_ge(sT_ps.sem, sT_ps.at(i, NG * FILLS, 1))
                    nc.scalar.activation(mrow[j][:, :], ps[0:NG, pe_bank, 0:SEQ], ACT.Copy, scale=-1.0).then_inc(
                        mrow_ready.sem, 1)
                    yield

            def back(i, p):
                for j in range(NG):
                    if j < 2:
                        act.wait_ge(pv_done.sem, pv_done.at(i, (j + 3) * T, 1))
                    else:
                        act.wait_ge(pv_done.sem, pv_done.at(i, (j - 1) * T))
                    for n in range(FILLS):
                        c = j * FILLS + n
                        act.wait_ge(sT_ps.sem, sT_ps.at(i, c + 1))
                        nc.scalar.activation(probs[j % 2][:, n, :], ps[:, 4 + c % 2, :], ACT.Exp,
                                             scale=SCALE).then_inc(exp_done.sem, 1)
                    if j >= 2:
                        transposed(i, j - 2)
                    yield
                transposed(i, 2)
                yield
                transposed(i, 3)
                yield

            def transposed(i, m):
                act.wait_ge(cxT_ps.sem, cxT_ps.at(i, m + 1))
                if m == 0:
                    act.wait_ge(out_ps.sem, out_ps.at(i, 1, 1))
                nc.scalar.activation(cxT[:, 2 * m:2 * m + 2, :], ps[:, 7, :].rearrange("p (h t) -> p h t", h=2),
                                     ACT.Copy).then_inc(cxT_ready.sem, 1)

            pipeline(act, front, back)

        @block.tensor
        def _(pe):
            mm = nc.tensor.matmul
            for s in (yT_ps, q_ps, k_ps, v_ps, score_ps, max_ps, sT_ps, pv_done, cxT_ps, out_ps):
                s.credit(pe)
            pe.wait_ge(loaded, 16)
            pe.wait_ge(constants, 3)

            def front(i, p):
                yield
                pe.wait_ge(y_ready.sem, y_ready.at(i, 1))
                pe.wait_ge(mrow_ready.sem, mrow_ready.at(i, NG, 1))
                for t in range(T):
                    last = nc.tensor.transpose(ps[:, 0, t * P:(t + 1) * P], y[p][:, t, :], g.ident[:, :])
                last.then_inc(yT_ps.sem, 1)
                yield
                pe.wait_ge(yT_ready.sem, yT_ready.at(i, 1))
                for j in range(NG):
                    if j >= 2:
                        pe.wait_ge(q_lo_ready.sem, q_lo_ready.at(i, j - 1))
                    for h in range(2):
                        o = 2 * j + h
                        last = mm(ps[:, (j + 1) % 2, h * SEQ:(h + 1) * SEQ], at["wq"][:, o * P:(o + 1) * P], yT[:, :],
                                  start=True, stop=True)
                    last.then_inc(q_ps.sem, 1)
                    if j == 1:
                        yield
                for n in range(2):
                    pe.wait_ge(q_lo_ready.sem, q_lo_ready.at(i, n + 3))
                    for h in range(2):
                        o = 2 * n + h
                        last = mm(ps[:, (n + 1) % 2, h * SEQ:(h + 1) * SEQ], at["wk"][:, o * P:(o + 1) * P], yT[:, :],
                                  start=True, stop=True)
                    last.then_inc(k_ps.sem, 1)
                pe.wait_ge(k_lo_ready.sem, k_lo_ready.at(i, 1))
                for t in range(T):
                    last = mm(ps[:, 1, t * SEQ:(t + 1) * SEQ], yT[:, t * P:(t + 1) * P], at["wv"], start=True, stop=True)
                last.then_inc(v_ps.sem, 1)
                yield
                pe.wait_ge(k_lo_ready.sem, k_lo_ready.at(i, 2))
                for j in range(NG + 1):
                    if j < NG:
                        for n in range(FILLS):
                            c = j * FILLS + n
                            if c < 2:
                                pe.wait_ge(rowmax_ready.sem, rowmax_ready.at(i, NG * FILLS - 1 + c, 1))
                            else:
                                pe.wait_ge(rowmax_ready.sem, rowmax_ready.at(i, c - 1))
                            t, pair = n // 2, 2 * j + n % 2
                            for h in range(2):
                                last = mm(ps[:, 2 + c % 2, h * SEQ:(h + 1) * SEQ], Q["hi"][p][:, pair, t * P:(t + 1) * P],
                                          K["hi"][p][:, h, j, :], start=True, stop=True)
                            last.then_inc(score_ps.sem, 1)
                    if j > 0:
                        m = j - 1
                        pe.wait_ge(rowmax_ready.sem, rowmax_ready.at(i, j * FILLS))
                        if m == 0:
                            pe.wait_ge(k_lo_ready.sem, k_lo_ready.at(i, 2))
                        elif m == 1:
                            pe.wait_ge(v_ready.sem, v_ready.at(i, 1))
                        else:
                            pe.wait_ge(mrow_ready.sem, mrow_ready.at(i, m - 1))
                        for t in range(T):
                            last = nc.tensor.transpose(ps[0:NG, m % 2, t * P:(t + 1) * P], rowmax[:, t, 4 * m:4 * m + 4],
                                                       g.ident[:, :])
                        last.then_inc(max_ps.sem, 1)
                    yield

            def scores(i, p, j, n):
                c = j * FILLS + n
                if c < 2:
                    pe.wait_ge(exp_done.sem, exp_done.at(i, NG * FILLS - 1 + c, 1))
                else:
                    pe.wait_ge(exp_done.sem, exp_done.at(i, c - 1))
                t, pair = n // 2, 2 * j + n % 2
                keys = slice(t * P, (t + 1) * P)
                bank = ps[:, 4 + c % 2, :]
                mm(bank, ones_row[:, :], maxima[:, j, (n % 2) * BANK:(n % 2 + 1) * BANK], start=True, stop=False)
                for h in range(2):
                    o = bank[:, h * SEQ:(h + 1) * SEQ]
                    mm(o, K["hi"][p][:, h, j, keys], Q["hi"][p][:, pair, :], start=False, stop=False)
                    mm(o, K["hi"][p][:, h, j, keys], Q["lo"][p][:, pair, :], start=False, stop=False)
                    last = mm(o, K["lo"][p][:, h, j, keys], Q["hi"][p][:, pair, :], start=False, stop=h == 1)
                last.then_inc(sT_ps.sem, 1)

            def values(i, p, j, t):
                c = j * T + t
                pe.wait_ge(exp_done.sem, exp_done.at(i, (j + 1) * FILLS))
                if c == 0:
                    pe.wait_ge(cx_ready.sem, cx_ready.at(i, NG * T, 1))
                else:
                    pe.wait_ge(cx_ready.sem, cx_ready.at(i, c))
                for h in range(HG):
                    for kt in range(T):
                        s0 = (h % 2) * SEQ + t * P
                        last = mm(ps[:, 6, h * DV:(h + 1) * DV], probs[j % 2][:, 2 * kt + h // 2, s0:s0 + P],
                                  V[p][:, kt, j, :], start=kt == 0, stop=kt == T - 1)
                last.then_inc(pv_done.sem, 1)

            def transposed(i, m):
                pe.wait_ge(cx_ready.sem, cx_ready.at(i, (m + 1) * T))
                if m == 0:
                    pe.wait_ge(f_ready.sem, f_ready.at(i, 1, 1))
                else:
                    pe.wait_ge(cxT_ready.sem, cxT_ready.at(i, m))
                for h in range(2):
                    for t in range(T):
                        o = (2 * m + h) * P
                        last = nc.tensor.transpose(ps[:, 7, h * SEQ + t * P:h * SEQ + (t + 1) * P], cx[:, t, o:o + P],
                                                   g.ident[:, :])
                last.then_inc(cxT_ps.sem, 1)

            def back(i, p):
                for j in range(NG + 2):
                    if j < NG:
                        pe.wait_ge(mrow_placed[j], i * 16 + 16)
                        scores(i, p, j, 0)
                        scores(i, p, j, 1)
                    if 0 < j <= NG:
                        values(i, p, j - 1, 0)
                    if j < NG:
                        scores(i, p, j, 2)
                        scores(i, p, j, 3)
                    if 0 < j <= NG:
                        values(i, p, j - 1, 1)
                    if j >= 2:
                        transposed(i, j - 2)
                    yield
                pe.wait_ge(cxT_ready.sem, cxT_ready.at(i, NG))
                for t in range(T):
                    for pair in range(PAIRS):
                        last = mm(ps[:, 7, t * P:(t + 1) * P], cxT[:, pair, t * P:(t + 1) * P],
                                  at["wpost"][:, pair * P:(pair + 1) * P], start=pair == 0, stop=pair == PAIRS - 1)
                last.then_inc(out_ps.sem, 1)
                yield

            pipeline(pe, front, back)


ATT8 = {
    0: [("wqk", 2 * P), ("wv", P), ("wo", P), ("vb", P), ("ob", P), ("qkb", 2)],
    1: [("wqk", 2 * P), ("wrot", 2 * P), ("wv", P), ("wo", P), ("ob", P), ("cos", 2 * SEQ), ("sin", 2 * SEQ)],
}


class Globals:
    pass


def expert_weights(nc, ctx, layer):
    sb = lambda name, shape: ctx.enter_context(nc.sbuf_tensor(f"e{layer}_{name}", shape, F32R))
    return {f"{k}_{part}": sb(f"{k}_{part}", shape) for part in ("hi", "lo")
            for k, shape in (("gu", [P, NE, 2 * F_EXP[layer]]), ("down", [P, NE, FC, P]))}


def program(nc, a, out_dram, only=None):
    g = Globals()
    with ExitStack() as ctx:
        def sb(name, shape, dt=F32):
            return ctx.enter_context(nc.sbuf_tensor(name, shape, dt))

        g.x = sb("x", [P, TILES, P])
        g.ident = sb("ident", [P, P])
        g.minus_half = sb("minus_half", [P, 8])
        g.plus_half = sb("plus_half", [P, 32])
        g.ones_rows = sb("ones_rows", [P, 1])
        g.spread, g.masks = a["spread"], a["masks"]

        with nc.semaphore("x_loaded") as x_loaded, nc.Block() as block:
            @block.sync
            def _(sp):
                sp.dma_start(g.x[:, :, :], a["x"].rearrange("b (t p) d -> p (b t) d", p=P)).then_inc(x_loaded, 16)
                sp.dma_start(g.ident[:, :], a["ident"]).then_inc(x_loaded, 16)
                sp.dma_start(g.ones_rows[:, :], a["ones_rows"]).then_inc(x_loaded, 16)
                sp.wait_ge(x_loaded, 48)

            @block.vector
            def _(dve):
                nc.vector.memset(g.minus_half[:, :], -0.5)
                nc.vector.memset(g.plus_half[:, :], 0.5)

        n = 99 if only is None else only
        if n > 0:
            attention8(nc, g, 0, a["att0"])
        if n > 1:
            with ExitStack() as part:
                w = expert_weights(nc, part, 0)
                load_experts(nc, g, 0, a["gu0"], a["down0"], w)
                experts(nc, g, 0, a["moe0"], w)
        if n > 2:
            attention8(nc, g, 1, a["att1"])
        if n > 3:
            selected_ffn(nc, g, 1, a["ffn1"], a["experts1"])
        if n > 4:
            grouped_attention(nc, g, a["att2"])
        if n > 5:
            selected_ffn(nc, g, 2, a["ffn2"], a["experts2"])
        if n > 6:
            channel_attention(nc, g, a["att3"])
        if n > 7:
            with ExitStack() as part:
                w = expert_weights(nc, part, 3)
                load_experts(nc, g, 3, a["gu3"], a["down3"], w)
                experts(nc, g, 3, a["moe3"], w)

        with nc.semaphore("x_stored") as x_stored, nc.Block() as block:
            @block.sync
            def _(sp):
                sp.dma_start(out_dram.rearrange("b (t p) d -> p (b t) d", p=P), g.x[:, :, :]).then_inc(x_stored, 16)
                sp.wait_ge(x_stored, 16)


def packed(inputs):
    f32 = lambda k: np.asarray(inputs[k], np.float32)
    rows = lambda v: np.broadcast_to(v, (P, v.shape[-1]))
    cols = lambda v: v.reshape(-1, P).T
    a = {"x": f32("L0_attn_x"), "ident": np.eye(P, dtype=np.float32)}
    spread = np.zeros((P, 16, P), np.float32)
    ones = np.zeros((P, 1), np.float32)
    parts = [(0, (0, 16)), (4, (8,)), (8, (0, 8)), (12, (16,))]
    for first, places in parts:
        for blk in range(NG):
            for j in range(NG):
                for d in range(D8):
                    for at in places:
                        spread[(4 * j + blk) * D8 + d, first + blk, 32 * j + at + d] = 1.0
    for j in range(NG):
        ones[32 * j + ROWS, 0] = 1.0
    a["spread"], a["ones_rows"] = spread, ones
    r = np.arange(P)
    m = np.where(r[None, :] > r[:, None], MASKED, 0.0)
    z = np.zeros((P, P))
    a["masks"] = np.stack([np.hstack(v) for v in ([m] * 4, [z, m, z, m], [m.T, z, m.T, z], [m.T] * 4)],
                          axis=1).astype(np.float32)
    a["att0"] = np.hstack([f32("L0_attn_qkv_w"), f32("L0_attn_out_w"), rows(f32("L0_attn_qkv_b")[2 * P:]),
                           rows(f32("L0_attn_out_b")), cols(f32("L0_attn_qkv_b")[:2 * P])])
    qkv1 = f32("L1_attn_w_qkv")
    theta = (1.0 / 10000.0 ** (np.arange(0, D8, 2, dtype=np.float32) / D8)).astype(np.float32)
    angles = np.outer(np.arange(SEQ, dtype=np.float32), theta).astype(np.float32).T
    sign = np.repeat(np.array([-1.0, 1.0], np.float32), D8 // 2)[:, None]
    cos = np.tile(np.cos(np.vstack([angles, angles])), (NH, 2)).astype(np.float32)
    sin = np.tile(sign * np.sin(np.vstack([angles, angles])), (NH, 2)).astype(np.float32)
    turned = qkv1[:, :2 * P].reshape(P, 2 * NH, 2, D8 // 2)[:, :, ::-1].reshape(P, 2 * P)
    a["att1"] = np.hstack([qkv1[:, :2 * P], turned, qkv1[:, 2 * P:], f32("L1_attn_w_out"), rows(f32("L1_attn_b_out")),
                           cos, sin])
    for k in (1, 2):
        c = lambda n: f32(f"L{k}_ffn_{n}")
        a[f"ffn{k}"] = np.hstack([c("Wp1"), cols(c("bp1")), c("Wp2"), rows(c("bp2")), c("Wo"), rows(c("bo"))])
        w2 = c("W2").reshape(NE, 2, P, P).transpose(0, 2, 1, 3).reshape(NE, P, 2 * P)
        a[f"experts{k}"] = np.concatenate([c("W1"), w2, c("b1").reshape(NE, 2, P).transpose(0, 2, 1),
                                           c("b2")[:, :, None]], axis=2)
    wk = f32("L2_attn_Wk").reshape(P, NG, 1, D64)
    post = f32("L2_attn_Wpost").reshape(NH // 2, P, P).transpose(1, 0, 2).reshape(P, NH * D64)
    a["att2"] = np.hstack([f32("L2_attn_Wq"), np.broadcast_to(wk, (P, NG, 2, D64)).reshape(P, NG * P),
                           f32("L2_attn_Wv"), post])
    head = np.arange(P) // D8
    blocks = np.where(head[:, None] == head[None, :], 0.0, MASKED).astype(np.float32)
    a["att3"] = np.hstack([f32("L3_attn_Wq").T, f32("L3_attn_Wk").T, f32("L3_attn_Wv").T, f32("L3_attn_Wo").T, blocks])
    iota = rows(np.arange(NE, dtype=np.float32))
    t = lambda k: f32(k).T
    pad = lambda v, n: np.pad(v, [(0, n - v.shape[0])] + [(0, 0)] * (v.ndim - 1))
    gate0, up0, down0 = (np.concatenate([f32(f"L0_ffn_r{c}"), f32(f"L0_ffn_s{c}")[None]]) for c in "gud")
    a["gu0"] = np.concatenate([gate0.transpose(0, 2, 1), up0.transpose(0, 2, 1)], axis=2)
    a["down0"] = down0.transpose(0, 2, 1)
    logit_bias = np.full((NE,), MASKED, np.float32)
    logit_bias[:NE - 1] = f32("L0_ffn_rb")
    a["moe0"] = np.hstack([pad(f32("L0_ffn_wr"), NE).T, rows(logit_bias), iota])
    a["gu3"] = np.concatenate([f32("L3_ffn_Wg"), f32("L3_ffn_W1")], axis=2)
    a["down3"] = f32("L3_ffn_W2")

    def chunks(b):
        b = np.pad(b, ((0, 0), (0, FC * P - b.shape[1])))
        return b.reshape(NE * FC, P).T

    a["moe3"] = np.hstack([t("L3_ffn_centroid"), iota, chunks(f32("L3_ffn_bg")), chunks(f32("L3_ffn_b1")),
                           pad(f32("L3_ffn_b2"), P)])
    return a


def kernel(**inputs):
    import concourse.bacc as bacc
    from concourse.bass_utils import run_bass_kernel_spmd

    nc = bacc.Bacc("TRN2", target_bir_lowering=False, num_devices=1)
    a = {k: np.ascontiguousarray(v) for k, v in packed(inputs).items()}
    shape = (SEQS, SEQ, P)
    aps = {k: nc.dram_tensor(f"in_{k}", v.shape, mybir.dt.from_np(v.dtype), kind="ExternalInput").ap() for k, v in a.items()}
    out = nc.dram_tensor("out", shape, F32, kind="ExternalOutput").ap()
    program(nc, aps, out)
    r = run_bass_kernel_spmd(nc, [{f"in_{k}": v for k, v in a.items()}], core_ids=[0])
    return r.results[0]["out"]
```

```python
from contextlib import ExitStack

import numpy as np
import concourse.bass as bass
from concourse import mybir

F32 = mybir.dt.float32
F32R = mybir.dt.float32r
U32 = mybir.dt.uint32
BF16 = mybir.dt.bfloat16
ALU = mybir.AluOpType
ACT = mybir.ActivationFunctionType
AX = mybir.AxisListType.X

P = 128
SEQS = 8
SEQ = 256
T = SEQ // P
TILES = SEQS * T
NH = 16
NG = 4
HG = NH // NG
EPS = 1e-5
MASKED = -1e30
BANK = 512
D8 = 8
D64 = 64
ROWS = 24
NE = 8
F_EXP = {0: 352, 3: 342}
FC = 3
RT = 4
RUN = RT * P
RUNS = TILES // RT
DEPTH = 2


class Signal:

    def __init__(self, sem, per):
        self.sem, self.per = sem, per

    def credit(self, eng):
        eng.sem_inc(self.sem, DEPTH * self.per)

    def at(self, i, c, back=0):
        assert 1 <= c <= self.per and 0 <= back <= DEPTH
        return i * self.per + ((DEPTH - back) * self.per + c)


def own_wait(eng, sem):
    eng.sem_inc(sem, 1)


class Chain:

    def __init__(self, sem, per):
        self.sem, self.sig, self.per, self.n = sem, Signal(sem, per), per, 0

    def begin(self, i):
        self.i, self.n = i, 0

    def next(self):
        self.n += 1
        return self.sem

    def so_far(self):
        return self.sig.at(self.i, self.n)

    def end(self):
        assert self.n == self.per, f"{self.n} signals, not {self.per}"


def merge(*parts):
    parts = list(parts)
    while parts:
        for part in list(parts):
            if next(part, "end") == "end":
                parts.remove(part)


def skip(n):
    for _ in range(n):
        yield


def issue(part):
    for _ in part:
        pass


def pipeline(eng, front, back):
    issue(front(0, 0))
    with eng.Fori(0, (SEQS - 2) // 2) as t:
        merge(back(t * 2, 0), front(t * 2 + 1, 1))
        merge(back(t * 2 + 1, 1), front(t * 2 + 2, 0))
    merge(back(SEQS - 2, 0), front(SEQS - 1, 1))
    issue(back(SEQS - 1, 1))


def pipeline3(eng, front, back, finish):
    issue(front(0, 0))
    merge(back(0, 0), front(1, 1))
    with eng.Fori(0, (SEQS - 2) // 2) as t:
        merge(finish(t * 2), back(t * 2 + 1, 1), front(t * 2 + 2, 0))
        merge(finish(t * 2 + 1), back(t * 2 + 2, 0), front(t * 2 + 3, 1))
    merge(finish(SEQS - 2), back(SEQS - 1, 1))
    issue(finish(SEQS - 1))


def nothing(*_):
    return iter(())


class Stage:

    def __init__(self, nc, ctx, name):
        self.nc, self.ctx, self.name = nc, ctx, name
        self.sems = []
        ctx.callback(self.release)
        self.dve_waited, self.sp_waited = self.sem("dve_waited"), self.sem("sp_waited")
        self.ps = ctx.enter_context(nc.psum_tensor(f"{name}_banks", [P, 8, BANK], F32))

    def sb(self, name, shape, dt=F32):
        return self.ctx.enter_context(self.nc.sbuf_tensor(f"{self.name}_{name}", shape, dt))

    def sem(self, name):
        self.sems.append(self.nc.alloc_semaphore(name=f"{self.name}_{name}"))
        return self.sems[-1]

    def release(self):
        self.nc.clear_and_free_semaphores(self.sems)
        self.nc.all_engine_barrier()

    def sig(self, name, per):
        return Signal(self.sem(name), per)



class Norm:

    def __init__(self, st, name, n):
        self.n = n
        self.waited = st.dve_waited
        self.stats = st.sb(f"{name}_stats", [P, n, 6])
        self.mean_var = st.sb(f"{name}_mean_var", [P, n, 2])
        self.var = st.sb(f"{name}_var", [P, n])
        self.rstd = st.sb(f"{name}_rstd", [P, n])
        self.var_ready = st.sig(f"{name}_var_ready", 1)
        self.rstd_ready = st.sig(f"{name}_rstd_ready", 1)

    CHAIN = 2

    def moments(self, nc, dve, chain, src):
        for j in range(self.n):
            last = nc.vector.bn_stats(self.stats[:, j, :], src(j))
        last.then_inc(chain.next(), 1)
        dve.wait_ge(chain.sem, chain.so_far())
        own_wait(dve, self.waited)
        for j in range(self.n):
            last = nc.vector.bn_aggr(self.mean_var[:, j, :], self.stats[:, j, :])
        last.then_inc(chain.next(), 1)
        dve.wait_ge(chain.sem, chain.so_far())
        nc.vector.tensor_scalar(self.var[:, :], self.mean_var[:, :, 1], EPS, None, ALU.add).then_inc(
            self.var_ready.sem, 1)

    def power(self, nc, pool, i, minus_half):
        pool.wait_ge(self.var_ready.sem, self.var_ready.at(i, 1))
        nc.gpsimd.tensor_tensor(self.rstd[:, :], self.var[:, :], minus_half[:, 0:self.n], ALU.pow).then_inc(
            self.rstd_ready.sem, 1)

    def apply(self, nc, j, out, src):
        return nc.vector.tensor_scalar(out, src, self.mean_var[:, j, 0:1], self.rstd[:, j:j + 1],
                                       ALU.subtract, ALU.mult)


def add_normed(nc, dve, chain, norm, i, x, tile0, f):
    dve.wait_ge(norm.rstd_ready.sem, norm.rstd_ready.at(i, 1))
    for j in range(norm.n):
        last = norm.apply(nc, j, f[:, j, :], f[:, j, :])
    last.then_inc(chain.next(), 1)
    dve.wait_ge(chain.sem, chain.so_far())
    for j in range(norm.n):
        last = nc.vector.tensor_tensor(x[:, tile0 + j, :], x[:, tile0 + j, :], f[:, j, :], ALU.add)
    last.then_inc(chain.next(), 1)



def attention8(nc, g, layer, blob):
    causal, rope = layer == 0, layer == 1
    FILLS = 3 if causal else 4
    SCALE = float(D8) ** -0.5
    DV = D8 + 1
    COLS = 32
    x = g.x
    with ExitStack() as ctx:
        st = Stage(nc, ctx, f"a{layer}")
        ps = st.ps
        n_w = blob.shape[1]
        w = st.sb("w", [P, n_w])
        at, off = {}, 0
        for name, width in ATT8[layer]:
            at[name] = w[:, off:off + width]
            off += width
        assert off == n_w
        spread_raw = st.sb("spread_raw", [P, 16, P])
        spread = st.sb("spread", [P, 16, P], F32R)
        if causal:
            masks = st.sb("masks", [P, 4, BANK], BF16)
            masks_raw = st.sb("masks_raw", [P, 4, BANK])
            ident16 = st.sb("ident16", [P, P], BF16)
        y = st.sb("y", [P, T, P])
        f = st.sb("f", [P, T, P])
        yT = st.sb("yT", [P, SEQ])
        qk = st.sb("qk", [P, 2 * SEQ])
        rot = st.sb("rot", [P, 2 * SEQ])
        hi = st.sb("hi", [P, 2 * SEQ], F32R)
        lo = st.sb("lo", [P, 2 * SEQ], F32R)
        QT = [st.sb(f"QT{k}", [P, NG, SEQ], F32R) for k in range(2)]
        KT = [st.sb(f"KT{k}", [P, NG, SEQ], F32R) for k in range(2)]
        V = [st.sb(f"V{k}", [P, T, NH, COLS]) for k in range(2)]
        raw = [st.sb(f"raw{k}", [P, SEQ]) for k in range(2)]
        pick = st.sb("pick", [P, HG * DV])
        rowmax = st.sb("rowmax", [P, T, NH])
        mrow = [[st.sb(f"mrow{k}{j}", [NG, SEQ], F32R) for j in range(NG)] for k in range(2)]
        probs = [st.sb(f"probs{k}", [P, FILLS, BANK]) for k in range(2)]
        recip = st.sb("recip", [P, T, NH])
        cx = st.sb("cx", [P, T, P])
        cxT = st.sb("cxT", [P, SEQ])
        norm_in, norm_out = Norm(st, "in", T), Norm(st, "out", T)

        loaded = st.sem("weights_loaded")
        constants = st.sem("constants_ready")
        spread_ready = st.sem("spread_ready")
        y_ready, yT_ps, yT_ready = st.sig("y_ready", 1), st.sig("yT_ps", 1), st.sig("yT_ready", 1)
        qk_ps, qk_ready = st.sig("qk_ps", 1), st.sig("qk_ready", 1)
        hi_ready, lo_ready = st.sig("hi_ready", 1), st.sig("lo_ready", 1)
        v_ps, v_ready = st.sig("v_ps", 1), st.sig("v_ready", 1)
        stack_ps, stack_ready = st.sig("stack_ps", 4), st.sig("stack_ready", 4)
        score_ps, rowmax_ready = st.sig("score_ps", NG * FILLS), st.sig("rowmax_ready", NG * FILLS)
        max_ps, mrow_ready = st.sig("max_ps", NG), st.sig("mrow_ready", NG)
        mrow_placed = [st.sem(f"mrow_placed{j}") for j in range(NG)]
        sT_ps, exp_done = st.sig("sT_ps", NG * FILLS), st.sig("exp_done", NG * FILLS)
        pv_done, raw_ready, picked = st.sig("pv_done", NG), st.sig("raw_ready", NG), st.sig("picked", NG)
        cx_ready = st.sig("cx_ready", 1)
        cxT_ps, cxT_ready = st.sig("cxT_ps", 1), st.sig("cxT_ready", 1)
        out_ps, f_ready = st.sig("out_ps", 1), st.sig("f_ready", 1)
        front_chain = Chain(st.sem("dve_front"), Norm.CHAIN + (2 if rope else 0))
        back_chain = Chain(st.sem("dve_back"), Norm.CHAIN + 3)

        Q_HI, Q_LO, K_HI, K_LO = (4 * k for k in range(4))
        HEAD = 6
        GROUPS = (NG + 1) * FILLS
        block = ctx.enter_context(nc.Block())

        @block.sync
        def _(sp):
            sp.dma_start(w[:, :], blob).then_inc(loaded, 16)
            sp.dma_start(spread_raw[:, :, :], g.spread).then_inc(loaded, 16)
            sp.dma_start(pick[:, :], g.pick).then_inc(loaded, 16)
            if causal:
                sp.dma_start(masks_raw[:, :, :], g.masks).then_inc(loaded, 16)

            def front(i, p):
                yield from skip(HEAD + FILLS + 2)
                for j in range(NG):
                    sp.wait_ge(mrow_ready.sem, mrow_ready.at(i, j + 1))
                    sp.dma_start(QT[p][32 * j + ROWS:32 * j + ROWS + 1, :, :].bitcast(F32),
                                 mrow[p][j][:, :].bitcast(F32)).then_inc(
                        mrow_placed[j], 16)
                    yield from skip(FILLS)

            pipeline(sp, front, lambda i, p: iter(()))

        @block.gpsimd
        def _(pool):
            norm_in.rstd_ready.credit(pool)
            norm_out.rstd_ready.credit(pool)

            def front(i, p):
                norm_in.power(nc, pool, i, g.minus_half)
                yield

            def back(i, p):
                yield from skip(GROUPS + 2)
                norm_out.power(nc, pool, i, g.minus_half)
                yield

            pipeline(pool, front, back)

        @block.vector
        def _(dve):
            for s in (norm_in.var_ready, norm_out.var_ready, y_ready, qk_ready, lo_ready, v_ready,
                      rowmax_ready, cx_ready, f_ready, front_chain.sig, back_chain.sig):
                s.credit(dve)
            dve.wait_ge(loaded, 64 if causal else 48)
            if causal:
                nc.vector.tensor_copy(masks[:, :, :], masks_raw[:, :, :])
                nc.vector.tensor_copy(ident16[:, :], g.ident[:, :])
            nc.vector.tensor_copy(spread[:, :, :], spread_raw[:, :, :]).then_inc(spread_ready, 1)
            for k in range(2):
                nc.vector.memset(V[k][:, :, :, DV:COLS], 0.0)
                nc.vector.memset(V[k][:, :, :, D8:DV], 1.0).then_inc(constants, 1)
            dve.wait_ge(constants, 2)

            def front(i, p):
                front_chain.begin(i)
                norm_in.moments(nc, dve, front_chain, lambda j: x[:, i * T + j, :])
                dve.wait_ge(norm_in.rstd_ready.sem, norm_in.rstd_ready.at(i, 1))
                for j in range(T):
                    last = norm_in.apply(nc, j, y[:, j, :], x[:, i * T + j, :])
                last.then_inc(y_ready.sem, 1)
                yield from skip(2)
                dve.wait_ge(qk_ps.sem, qk_ps.at(i, 1))
                if rope:
                    nc.vector.tensor_tensor(qk[:, :], ps[:, 1, :], at["cos"], ALU.mult).then_inc(front_chain.next(), 1)
                    nc.vector.tensor_tensor(rot[:, :], ps[:, 0, :], at["sin"], ALU.mult).then_inc(front_chain.next(), 1)
                    dve.wait_ge(front_chain.sem, front_chain.so_far())
                    nc.vector.tensor_tensor(qk[:, :], qk[:, :], rot[:, :], ALU.add).then_inc(qk_ready.sem, 1)
                else:
                    for k in range(2):
                        last = nc.vector.tensor_scalar(qk[:, k * SEQ:(k + 1) * SEQ], ps[:, 1, k * SEQ:(k + 1) * SEQ],
                                                       at["qkb"][:, k:k + 1], None, ALU.add)
                    last.then_inc(qk_ready.sem, 1)
                yield
                dve.wait_ge(hi_ready.sem, hi_ready.at(i, 1))
                dve.wait_ge(qk_ready.sem, qk_ready.at(i, 1))
                nc.vector.tensor_tensor(lo[:, :], qk[:, :], hi[:, :].bitcast(F32), ALU.subtract).then_inc(
                    lo_ready.sem, 1)
                dve.wait_ge(v_ps.sem, v_ps.at(i, 1))
                v_bank = ps[:, 0 if causal else 1, 0:SEQ].rearrange("p (t h d) -> p t h d", t=T, h=NH)
                dve.wait_ge(pv_done.sem, pv_done.at(i, NG, 2))
                for t in range(T):
                    if causal:
                        last = nc.vector.tensor_tensor(V[p][:, t, :, 0:D8], v_bank[:, t],
                                                       at["vb"].rearrange("p (h d) -> p h d", h=NH), ALU.add)
                    else:
                        last = nc.vector.tensor_copy(V[p][:, t, :, 0:D8], v_bank[:, t])
                last.then_inc(v_ready.sem, 1)
                yield from skip(HEAD - 3)
                for j in range(NG):
                    if j == 0:
                        dve.wait_ge(max_ps.sem, max_ps.at(i, NG, 1))
                    for n in range(FILLS):
                        c = j * FILLS + n
                        dve.wait_ge(score_ps.sem, score_ps.at(i, c + 1))
                        bank = ps[:, 2 + c % 2, :]
                        if causal and n == 0:
                            o, src = rowmax[:, 0, 4 * j:4 * j + 4], bank.rearrange("p (h k) -> p h k", h=4)
                        else:
                            t, h = (1, 4 * j + 2 * (n - 1)) if causal else (n // 2, 4 * j + 2 * (n % 2))
                            o, src = rowmax[:, t, h:h + 2], bank.rearrange("p (h k) -> p h k", h=2)
                        nc.vector.reduce_max(o, src, AX).then_inc(rowmax_ready.sem, 1)
                        yield
                front_chain.end()

            def back(i, p):
                back_chain.begin(i)
                yield from skip(GROUPS)
                dve.wait_ge(picked.sem, picked.at(i, NG))
                c = ps[:, 7, 0:T * NH * DV].rearrange("p (t h d) -> p t h d", t=T, h=NH)
                nc.vector.reciprocal(recip[:, :, :], c[:, :, :, D8]).then_inc(back_chain.next(), 1)
                dve.wait_ge(back_chain.sem, back_chain.so_far())
                for t in range(T):
                    last = nc.vector.tensor_tensor(cx[:, t, :].rearrange("p (h d) -> p h d", h=NH), c[:, t, :, 0:D8],
                                                   recip[:, t, :].rearrange("p (h o) -> p h o", o=1).to_broadcast([P, NH, D8]), ALU.mult)
                last.then_inc(cx_ready.sem, 1)
                yield from skip(2)
                dve.wait_ge(out_ps.sem, out_ps.at(i, 1))
                for t in range(T):
                    last = nc.vector.tensor_tensor(f[:, t, :], ps[:, 6, SEQ + t * P:SEQ + (t + 1) * P], at["ob"], ALU.add)
                last.then_inc(f_ready.sem, 1)
                dve.wait_ge(f_ready.sem, f_ready.at(i, 1))
                norm_out.moments(nc, dve, back_chain, lambda j: f[:, j, :])
                yield
                add_normed(nc, dve, back_chain, norm_out, i, x, i * T, f)
                dve.wait_ge(back_chain.sem, back_chain.so_far())
                back_chain.end()

            pipeline(dve, front, back)

        @block.scalar
        def _(act):
            nc.scalar.preload_act_table(ACT.Exp)
            for s in (yT_ready, hi_ready, stack_ready, mrow_ready, exp_done, raw_ready, cxT_ready):
                s.credit(act)

            def front(i, p):
                yield
                act.wait_ge(yT_ps.sem, yT_ps.at(i, 1))
                nc.scalar.activation(yT[:, :], ps[:, 0, 0:SEQ], ACT.Copy).then_inc(yT_ready.sem, 1)
                yield from skip(2)
                act.wait_ge(qk_ready.sem, qk_ready.at(i, 1))
                act.wait_ge(stack_ps.sem, stack_ps.at(i, 4, 1))
                nc.scalar.activation(hi[:, :], qk[:, :], ACT.Copy).then_inc(hi_ready.sem, 1)
                yield
                act.wait_ge(sT_ps.sem, sT_ps.at(i, NG * FILLS, 2))
                for n in range(4):
                    act.wait_ge(stack_ps.sem, stack_ps.at(i, n + 1))
                    bank = ps[:, (1 if causal else 0) + (n % 2) * (-1 if causal else 1), :].rearrange(
                        "p (g t) -> p g t", g=2)
                    g2 = 2 * (n % 2)
                    if n < 2:
                        nc.scalar.activation(QT[p][:, g2:g2 + 2, :], bank, ACT.Copy).then_inc(stack_ready.sem, 1)
                    else:
                        nc.scalar.activation(KT[p][:, g2:g2 + 2, :], bank, ACT.Identity,
                                             bias=g.ones_rows[:, :]).then_inc(stack_ready.sem, 1)
                    if n % 2 == 1:
                        yield
                yield from skip(2)
                for j in range(NG):
                    yield from skip(FILLS)
                    act.wait_ge(max_ps.sem, max_ps.at(i, j + 1))
                    bank = (j + 1) % 2 if causal else j % 2
                    nc.scalar.activation(mrow[p][j][:, :], ps[0:NG, bank, 0:SEQ], ACT.Copy, scale=-1.0).then_inc(
                        mrow_ready.sem, 1)

            def to_sbuf(i, m):
                act.wait_ge(pv_done.sem, pv_done.at(i, m + 1))
                if m < 2:
                    act.wait_ge(picked.sem, picked.at(i, m + 3, 1))
                else:
                    act.wait_ge(picked.sem, picked.at(i, m - 1))
                nc.scalar.activation(raw[m % 2][:, :], ps[:, 6, 0:SEQ], ACT.Copy).then_inc(raw_ready.sem, 1)

            def back(i, p):
                for j in range(NG):
                    if j < 2:
                        act.wait_ge(pv_done.sem, pv_done.at(i, j + 3, 1))
                    else:
                        act.wait_ge(pv_done.sem, pv_done.at(i, j - 1))
                    for n in range(FILLS):
                        c = j * FILLS + n
                        act.wait_ge(sT_ps.sem, sT_ps.at(i, c + 1))
                        nc.scalar.activation(probs[j % 2][:, n, :], ps[:, 4 + c % 2, :], ACT.Exp,
                                             scale=SCALE).then_inc(exp_done.sem, 1)
                        if j > 0 and n == FILLS - 1:
                            to_sbuf(i, j - 1)
                        yield
                yield from skip(FILLS - 1)
                to_sbuf(i, NG - 1)
                yield from skip(2)
                act.wait_ge(cxT_ps.sem, cxT_ps.at(i, 1))
                nc.scalar.activation(cxT[:, :], ps[:, 6, 0:SEQ], ACT.Copy).then_inc(cxT_ready.sem, 1)
                yield

            pipeline(act, front, back)

        @block.tensor
        def _(pe):
            mm = nc.tensor.matmul
            for s in (yT_ps, qk_ps, v_ps, stack_ps, score_ps, max_ps, sT_ps, pv_done, picked, cxT_ps, out_ps):
                s.credit(pe)
            pe.wait_ge(loaded, 64 if causal else 48)
            pe.wait_ge(spread_ready, 1)
            pe.wait_ge(constants, 2)

            def front(i, p):
                yield
                pe.wait_ge(y_ready.sem, y_ready.at(i, 1))
                pe.wait_ge(mrow_ready.sem, mrow_ready.at(i, NG, 1))
                for t in range(T):
                    last = nc.tensor.transpose(ps[:, 0, t * P:(t + 1) * P], y[:, t, :], g.ident[:, :])
                last.then_inc(yT_ps.sem, 1)
                yield
                pe.wait_ge(yT_ready.sem, yT_ready.at(i, 1))
                for k in range(2):
                    last = mm(ps[:, 1, k * SEQ:(k + 1) * SEQ], at["wqk"][:, k * P:(k + 1) * P], yT[:, :],
                              start=True, stop=True)
                if rope:
                    for k in range(2):
                        last = mm(ps[:, 0, k * SEQ:(k + 1) * SEQ], at["wrot"][:, k * P:(k + 1) * P], yT[:, :],
                                  start=True, stop=True)
                last.then_inc(qk_ps.sem, 1)
                yield
                if rope:
                    pe.wait_ge(qk_ready.sem, qk_ready.at(i, 1))
                vb = 0 if causal else 1
                for t in range(T):
                    last = mm(ps[:, vb, t * P:(t + 1) * P], yT[:, t * P:(t + 1) * P], at["wv"], start=True, stop=True)
                last.then_inc(v_ps.sem, 1)
                yield
                pe.wait_ge(hi_ready.sem, hi_ready.at(i, 1))
                pe.wait_ge(lo_ready.sem, lo_ready.at(i, 1))
                for n in range(4):
                    if n == 1:
                        pe.wait_ge(v_ready.sem, v_ready.at(i, 1))
                    elif n > 1:
                        pe.wait_ge(stack_ready.sem, stack_ready.at(i, n - 1))
                    bank = (1 if causal else 0) + (n % 2) * (-1 if causal else 1)
                    k, m_hi, m_lo = n // 2, (Q_HI, K_HI)[n // 2], (Q_LO, K_LO)[n // 2]
                    for gg in range(2):
                        blk = 2 * (n % 2) + gg
                        o = ps[:, bank, gg * SEQ:(gg + 1) * SEQ]
                        mm(o, spread[:, m_hi + blk, :], hi[:, k * SEQ:(k + 1) * SEQ], start=True, stop=False)
                        last = mm(o, spread[:, m_lo + blk, :], lo[:, k * SEQ:(k + 1) * SEQ], start=False, stop=True)
                    last.then_inc(stack_ps.sem, 1)
                    if n % 2 == 1:
                        yield
                pe.wait_ge(stack_ready.sem, stack_ready.at(i, 4))
                for j in range(NG + 1):
                    rows = slice(32 * j, 32 * j + ROWS)
                    for n in range(FILLS):
                        if j < NG:
                            c = j * FILLS + n
                            if c < 2:
                                pe.wait_ge(rowmax_ready.sem, rowmax_ready.at(i, NG * FILLS - 1 + c, 1))
                            else:
                                pe.wait_ge(rowmax_ready.sem, rowmax_ready.at(i, c - 1))
                            bank = ps[:, 2 + c % 2, :]
                            if causal:
                                mm(bank, ident16[:, :], masks[:, 0 if n == 0 else 1, :], start=True, stop=False)
                            if causal and n == 0:
                                for h in range(4):
                                    last = mm(bank[:, h * P:(h + 1) * P], QT[p][rows, h, 0:P], KT[p][rows, h, 0:P],
                                              start=False, stop=h == 3)
                            else:
                                t, h0 = (1, 2 * (n - 1)) if causal else (n // 2, 2 * (n % 2))
                                for h in range(2):
                                    last = mm(bank[:, h * SEQ:(h + 1) * SEQ], QT[p][rows, h0 + h, t * P:(t + 1) * P],
                                              KT[p][rows, h0 + h, :], start=not causal, stop=(not causal) or h == 1)
                            last.then_inc(score_ps.sem, 1)
                        if j > 0 and n == 1:
                            m = j - 1
                            pe.wait_ge(rowmax_ready.sem, rowmax_ready.at(i, j * FILLS))
                            if m >= 2:
                                pe.wait_ge(mrow_ready.sem, mrow_ready.at(i, m - 1))
                            bank = (m + 1) % 2 if causal else m % 2
                            for t in range(T):
                                last = nc.tensor.transpose(ps[0:NG, bank, t * P:(t + 1) * P],
                                                           rowmax[:, t, 4 * m:4 * m + 4], g.ident[:, :])
                            last.then_inc(max_ps.sem, 1)
                        yield

            def transpose_group(i, m):
                pe.wait_ge(raw_ready.sem, raw_ready.at(i, m + 1))
                if m == 0:
                    pe.wait_ge(cx_ready.sem, cx_ready.at(i, 1, 1))
                for t in range(T):
                    o = (t * NH + HG * m) * DV
                    last = mm(ps[:, 7, o:o + HG * DV], raw[m % 2][:, t * P:(t + 1) * P], pick[:, :], start=True, stop=True)
                last.then_inc(picked.sem, 1)

            def values(i, p, m, kt):
                if kt == 0:
                    pe.wait_ge(exp_done.sem, exp_done.at(i, (m + 1) * FILLS))
                    if m == 0:
                        pe.wait_ge(f_ready.sem, f_ready.at(i, 1, 1))
                    else:
                        pe.wait_ge(raw_ready.sem, raw_ready.at(i, m))
                for h in range(HG):
                    o = ps[h * COLS:(h + 1) * COLS, 6, :]
                    v = V[p][:, kt, HG * m + h, :]
                    if causal and kt == 1:
                        last = mm(o[:, P:SEQ], v, probs[m % 2][:, 2, h * P:(h + 1) * P], start=False, stop=True)
                    else:
                        last = mm(o[:, 0:SEQ], v, probs[m % 2][:, 2 * kt + h // 2, (h % 2) * SEQ:(h % 2 + 1) * SEQ],
                                  start=kt == 0, stop=kt == T - 1)
                if kt == T - 1:
                    last.then_inc(pv_done.sem, 1)

            def back(i, p):
                for j in range(NG + 1):
                    rows = slice(32 * j, 32 * j + ROWS + 1)
                    for n in range(FILLS):
                        if j < NG:
                            if n == 0:
                                pe.wait_ge(mrow_placed[j], i * 16 + 16)
                            c = j * FILLS + n
                            if c < 2:
                                pe.wait_ge(exp_done.sem, exp_done.at(i, NG * FILLS - 1 + c, 1))
                            else:
                                pe.wait_ge(exp_done.sem, exp_done.at(i, c - 1))
                            bank = ps[:, 4 + c % 2, :]
                            if causal:
                                mm(bank, ident16[:, :], masks[:, 3 if n == 2 else 2, :], start=True, stop=False)
                            if causal and n == 2:
                                for h in range(4):
                                    last = mm(bank[:, h * P:(h + 1) * P], KT[p][rows, h, P:SEQ], QT[p][rows, h, P:SEQ],
                                              start=False, stop=h == 3)
                            else:
                                t, h0 = n // 2, 2 * (n % 2)
                                for h in range(2):
                                    last = mm(bank[:, h * SEQ:(h + 1) * SEQ], KT[p][rows, h0 + h, t * P:(t + 1) * P],
                                              QT[p][rows, h0 + h, :], start=not causal, stop=(not causal) or h == 1)
                            last.then_inc(sT_ps.sem, 1)
                        if n == 0 and j > 1:
                            transpose_group(i, j - 2)
                        if j > 0 and 1 <= n <= T:
                            values(i, p, j - 1, n - 1)
                        yield
                transpose_group(i, NG - 1)
                yield
                pe.wait_ge(cx_ready.sem, cx_ready.at(i, 1))
                for t in range(T):
                    last = nc.tensor.transpose(ps[:, 6, t * P:(t + 1) * P], cx[:, t, :], g.ident[:, :])
                last.then_inc(cxT_ps.sem, 1)
                yield
                pe.wait_ge(cxT_ready.sem, cxT_ready.at(i, 1))
                for t in range(T):
                    last = mm(ps[:, 6, SEQ + t * P:SEQ + (t + 1) * P], cxT[:, t * P:(t + 1) * P], at["wo"],
                              start=True, stop=True)
                last.then_inc(out_ps.sem, 1)
                yield

            pipeline(pe, front, back)



def load_experts(nc, g, layer, src_gu, src_down, w):
    width = F_EXP[layer]
    last_rows = width - (FC - 1) * P
    with ExitStack() as ctx:
        st = Stage(nc, ctx, f"w{layer}")
        raw_gu = [st.sb(f"raw_gu{k}", [P, 2 * width]) for k in range(2)]
        raw_down = [st.sb(f"raw_down{k}", [P, FC, P]) for k in range(2)]
        loaded = [st.sem(f"loaded{k}") for k in range(2)]
        hi_ready, lo_ready = st.sig("hi_ready", 1), st.sig("lo_ready", 1)
        block = ctx.enter_context(nc.Block())

        def parts(e, k):
            yield raw_gu[k][:, :], w["gu_hi"][:, e, :], w["gu_lo"][:, e, :]
            yield (raw_down[k][:, 0:2, :], w["down_hi"][:, e, 0:2, :], w["down_lo"][:, e, 0:2, :])
            yield (raw_down[k][0:last_rows, 2, :], w["down_hi"][0:last_rows, e, 2, :],
                   w["down_lo"][0:last_rows, e, 2, :])

        def experts(eng, step):
            with eng.Fori(0, NE // 2) as t:
                for k in range(2):
                    step(t * 2 + k, k)

        @block.sync
        def _(sp):
            def step(e, k):
                sp.wait_ge(lo_ready.sem, lo_ready.at(e, 1, 2))
                sp.dma_start(raw_gu[k][:, :], src_gu[e, :, :]).then_inc(loaded[k], 16)
                sp.dma_start(raw_down[k][:, 0:2, :],
                             src_down[e, 0:2 * P, :].rearrange("(c p) d -> p c d", p=P)).then_inc(loaded[k], 16)
                sp.dma_start(raw_down[k][0:last_rows, 2, :], src_down[e, 2 * P:width, :]).then_inc(loaded[k], 16)
            experts(sp, step)

        @block.scalar
        def _(act):
            hi_ready.credit(act)

            def step(e, k):
                act.wait_ge(loaded[k], (e - k) * 24 + 48)
                for raw, hi, lo in parts(e, k):
                    last = nc.scalar.activation(hi, raw, ACT.Copy)
                last.then_inc(hi_ready.sem, 1)
            experts(act, step)

        @block.vector
        def _(dve):
            lo_ready.credit(dve)

            def step(e, k):
                dve.wait_ge(hi_ready.sem, hi_ready.at(e, 1))
                for raw, hi, lo in parts(e, k):
                    last = nc.vector.tensor_tensor(lo, raw, hi.bitcast(F32), ALU.subtract)
                last.then_inc(lo_ready.sem, 1)
            experts(dve, step)


MOE = {
    0: [("router", NE), ("logit_bias", NE), ("iota", NE), ("pick_expert", NE * P)],
    3: [("router", NE), ("iota", NE), ("pick_expert", NE * P), ("gate_b", NE * FC), ("up_b", NE * FC), ("down_b", P)],
}


def experts(nc, g, layer, blob, w):
    width = F_EXP[layer]
    by_distance = layer == 3
    rows_of = [P, P, width - 2 * P]
    N = NE * FC
    RING = 4
    LOW = 32
    WROWS = LOW + NE
    x = g.x
    with ExitStack() as ctx:
        st = Stage(nc, ctx, f"m{layer}")
        ps = st.ps
        wb = st.sb("w", [P, blob.shape[1]])
        at = columns(wb, MOE[layer])
        y = st.sb("y", [P, RT, P])
        yT = st.sb("yT", [P, RUN])
        y_hi, y_lo = st.sb("y_hi", [P, RUN], F32R), st.sb("y_lo", [P, RUN], F32R)
        gate = [st.sb(f"gate{k}", [P, RUN]) for k in range(2)]
        gated = [st.sb(f"gated{k}", [P, RUN]) for k in range(2)]
        weights = [st.sb(f"weights{k}", [P, RUN]) for k in range(2)]
        h = [st.sb(f"h{k}", [P, RUN]) for k in range(2)]
        h_hi = st.sb("h_hi", [P, RING, RUN], F32R)
        h_lo = st.sb("h_lo", [P, RING, RUN], F32R)
        accT = st.sb("accT", [P, RUN])
        f = st.sb("f", [P, RT, P])
        score = st.sb("score", [P, RT, NE])
        top = st.sb("top", [P, RT, 8])
        top_at = st.sb("top_at", [P, RT, 8], U32)
        top_atf = st.sb("top_atf", [P, RT, 2])
        gap, th = st.sb("gap", [P, RT]), st.sb("th", [P, RT])
        share = st.sb("share", [P, RT, 2])
        one_hot = st.sb("one_hot", [P, RT, 2, NE])
        we = st.sb("we", [P, RT, NE])
        we_parts = st.sb("we_parts", [P, RT, WROWS])
        we_hi = st.sb("we_hi", [P, RT, NE], F32R)
        weT = st.sb("weT", [WROWS, RUN], F32R)
        pick_expert = st.sb("pick_expert", [WROWS, NE * P], F32R)
        norm_in, norm_out = Norm(st, "in", RT), Norm(st, "out", RT)
        if by_distance:
            down_b_hi, down_b_lo = st.sb("down_b_hi", [WROWS, P], F32R), st.sb("down_b_lo", [WROWS, P], F32R)
            sq_y = st.sb("sq_y", [P, RT])
            square = st.sb("square", [P, RT, P])
            ones = st.sb("ones", [P, P])
            c2 = st.sb("c2", [P, 3 * NE])
            sq_ready, d2_ready, dist_ready = (st.sig("sq_ready", 1), st.sig("d2_ready", 1), st.sig("dist_ready", 1))
            c2_sq, c2_ps, ones_ready = st.sem("c2_sq"), st.sem("c2_ps"), st.sem("ones_ready")
        loaded, constants = st.sem("loaded"), st.sem("constants_ready")
        y_ready, yT_ps, yT_ready = st.sig("y_ready", 1), st.sig("yT_ps", 1), st.sig("yT_ready", 1)
        y_hi_ready, y_lo_ready = st.sig("y_hi_ready", 1), st.sig("y_lo_ready", 1)
        router_ps, gap_ready, th_ready = st.sig("router_ps", 1), st.sig("gap_ready", 1), st.sig("th_ready", 1)
        we_ready, weT_ps, weT_ready = st.sig("we_ready", 1), st.sig("weT_ps", 1), st.sig("weT_ready", 1)
        weights_ps, weights_ready = st.sig("weights_ps", NE), st.sig("weights_ready", NE)
        gate_ps, up_ps = st.sig("gate_ps", N), st.sig("up_ps", N)
        silu_done, gated_done, h_done = st.sig("silu_done", N), st.sig("gated_done", N), st.sig("h_done", N)
        hi_done, lo_done, down_done = st.sig("h_hi_done", N), st.sig("h_lo_done", N), st.sig("down_done", N)
        accT_ready, f_ps, f_ready = st.sig("accT_ready", 1), st.sig("f_ps", 1), st.sig("f_ready", 1)
        front_chain = Chain(st.sem("dve_front"), Norm.CHAIN + (9 if by_distance else 9))
        back_chain = Chain(st.sem("dve_back"), Norm.CHAIN + 2)
        block = ctx.enter_context(nc.Block())

        def run_pipeline(eng, front, back, finish):
            issue(front(0))
            merge(back(0), front(1))
            with eng.Fori(1, RUNS - 1) as t:
                merge(finish(t - 1), back(t), front(t + 1))
            merge(finish(RUNS - 2), back(RUNS - 1))
            issue(finish(RUNS - 1))

        @block.sync
        def _(sp):
            sp.dma_start(wb[:, :], blob).then_inc(loaded, 16)

        @block.gpsimd
        def _(pool):
            for s in [norm_in.rstd_ready, norm_out.rstd_ready, gated_done] + ([dist_ready] if by_distance else []):
                s.credit(pool)

            def front(k):
                yield from skip(6)
                norm_in.power(nc, pool, k, g.minus_half)
                yield from skip(8)
                if by_distance:
                    pool.wait_ge(d2_ready.sem, d2_ready.at(k, 1))
                    nc.gpsimd.tensor_tensor(score[:, :, :], score[:, :, :],
                                            g.plus_half[:, 0:RT * NE].rearrange("p (t e) -> p t e", t=RT),
                                            ALU.pow).then_inc(dist_ready.sem, 1)

            def back(i):
                for n in range(N):
                    e, r = n // FC, rows_of[n % FC]
                    if n % FC == 0:
                        pool.wait_ge(weights_ready.sem, weights_ready.at(i, e + 1))
                    pool.wait_ge(silu_done.sem, silu_done.at(i, n + 1))
                    if n < 2:
                        pool.wait_ge(h_done.sem, h_done.at(i, N - 1 + n, 1))
                    else:
                        pool.wait_ge(h_done.sem, h_done.at(i, n - 1))
                    nc.gpsimd.tensor_tensor(gated[n % 2][0:r, :], gate[n % 2][0:r, :], weights[e % 2][0:r, :],
                                            ALU.mult).then_inc(gated_done.sem, 1)
                    yield

            def finish(i):
                yield from skip(7)
                norm_out.power(nc, pool, i, g.minus_half)
                yield

            run_pipeline(pool, front, back, finish)

        @block.vector
        def _(dve):
            sigs = [norm_in.var_ready, norm_out.var_ready, y_ready, y_lo_ready, gap_ready, h_done, lo_done,
                    front_chain.sig, back_chain.sig, we_ready]
            if by_distance:
                sigs += [d2_ready]
            for s in sigs:
                s.credit(dve)
            dve.wait_ge(loaded, 16)
            nc.vector.memset(we_parts[:, :, :], 0.0)
            nc.vector.tensor_copy(pick_expert[:, :], at["pick_expert"][0:WROWS, :]).then_inc(constants, 1)
            if by_distance:
                nc.vector.tensor_copy(down_b_hi[:, :], at["down_b"][0:WROWS, :]).then_inc(constants, 1)
                dve.wait_ge(constants, 2)
                nc.vector.tensor_tensor(down_b_lo[:, :], at["down_b"][0:WROWS, :], down_b_hi[:, :].bitcast(F32),
                                        ALU.subtract).then_inc(constants, 1)
                nc.vector.memset(ones[:, :], 1.0).then_inc(ones_ready, 1)
                nc.vector.tensor_tensor(c2[:, 0:NE], at["router"], at["router"], ALU.mult).then_inc(c2_sq, 1)
                dve.wait_ge(c2_sq, 1)
                nc.vector.tensor_scalar(c2[:, 2 * NE:3 * NE], at["router"], -2.0, None, ALU.mult).then_inc(c2_sq, 1)
                dve.wait_ge(c2_ps, 1)
                nc.vector.tensor_copy(c2[:, NE:2 * NE], ps[:, 7, 0:NE]).then_inc(constants, 1)
                dve.wait_ge(constants, 4)
                bias = c2[:, NE:2 * NE]
            else:
                bias = at["logit_bias"]
                dve.wait_ge(constants, 1)

            def hidden(i, n):
                r = rows_of[n % FC]
                dve.wait_ge(up_ps.sem, up_ps.at(i, n + 1))
                dve.wait_ge(gated_done.sem, gated_done.at(i, n + 1))
                if n < 2:
                    dve.wait_ge(lo_done.sem, lo_done.at(i, N - 1 + n, 1))
                else:
                    dve.wait_ge(lo_done.sem, lo_done.at(i, n - 1))
                up = ps[0:r, 2 + n % 3, :]
                if by_distance:
                    last = nc.vector.scalar_tensor_tensor(h[n % 2][0:r, :], up, at["up_b"][0:r, n:n + 1],
                                                          gated[n % 2][0:r, :], ALU.add, ALU.mult)
                else:
                    last = nc.vector.tensor_tensor(h[n % 2][0:r, :], up, gated[n % 2][0:r, :], ALU.mult)
                last.then_inc(h_done.sem, 1)

            def low_part(i, n):
                r = rows_of[n % FC]
                dve.wait_ge(h_done.sem, h_done.at(i, n + 1))
                dve.wait_ge(hi_done.sem, hi_done.at(i, n + 1))
                nc.vector.tensor_tensor(h_lo[0:r, n % RING, :], h[n % 2][0:r, :],
                                        h_hi[0:r, n % RING, :].bitcast(F32), ALU.subtract).then_inc(lo_done.sem, 1)

            def front(k):
                front_chain.begin(k)
                yield from skip(5)
                norm_in.moments(nc, dve, front_chain, lambda j: x[:, k * RT + j, :])
                yield from skip(2)
                dve.wait_ge(norm_in.rstd_ready.sem, norm_in.rstd_ready.at(k, 1))
                dve.wait_ge(yT_ps.sem, yT_ps.at(k, 1, 1))
                if by_distance:
                    dve.wait_ge(sq_ready.sem, sq_ready.at(k, 1, 1))
                for j in range(RT):
                    last = norm_in.apply(nc, j, y[:, j, :], x[:, k * RT + j, :])
                last.then_inc(y_ready.sem, 1)
                yield from skip(6)
                dve.wait_ge(router_ps.sem, router_ps.at(k, 1))
                bc = bias.rearrange("p (o e) -> p o e", o=1).to_broadcast([P, RT, NE])
                nc.vector.tensor_tensor(score[:, :, :], ps[:, 6, 0:RT * NE].rearrange("p (t e) -> p t e", t=RT), bc,
                                        ALU.add).then_inc(front_chain.next(), 1)
                dve.wait_ge(front_chain.sem, front_chain.so_far())
                if by_distance:
                    dve.wait_ge(sq_ready.sem, sq_ready.at(k, 1))
                    nc.vector.tensor_tensor(
                        score[:, :, :], score[:, :, :],
                        sq_y[:, :].rearrange("p (t o) -> p t o", o=1).to_broadcast([P, RT, NE]),
                        ALU.add).then_inc(front_chain.next(), 1)
                    dve.wait_ge(front_chain.sem, front_chain.so_far())
                    nc.vector.tensor_scalar(score[:, :, :], score[:, :, :], 1e-12, None, ALU.max).then_inc(
                        d2_ready.sem, 1)
                yield from skip(2)
                if by_distance:
                    dve.wait_ge(dist_ready.sem, dist_ready.at(k, 1))
                    own_wait(dve, st.dve_waited)
                for t in range(RT):
                    last = nc.vector.max(top[:, t, :], score[:, t, :])
                last.then_inc(front_chain.next(), 1)
                dve.wait_ge(front_chain.sem, front_chain.so_far())
                nc.vector.tensor_tensor(gap[:, :], top[:, :, 1], top[:, :, 0], ALU.subtract).then_inc(
                    gap_ready.sem, 1)
                for t in range(RT):
                    last = nc.vector.max_index(top_at[:, t, :], top[:, t, :], score[:, t, :])
                last.then_inc(front_chain.next(), 1)
                dve.wait_ge(front_chain.sem, front_chain.so_far())
                nc.vector.tensor_copy(top_atf[:, :, :], top_at[:, :, 0:2]).then_inc(front_chain.next(), 1)
                yield from skip(2)
                dve.wait_ge(front_chain.sem, front_chain.so_far())
                dve.wait_ge(th_ready.sem, th_ready.at(k, 1))
                nc.vector.tensor_scalar(share[:, :, 0], th[:, :], -0.5, 0.5, ALU.mult, ALU.add)
                nc.vector.tensor_scalar(share[:, :, 1], th[:, :], 0.5, 0.5, ALU.mult, ALU.add)
                io = at["iota"].rearrange("p (o e) -> p o e", o=1).to_broadcast([P, RT, NE])
                for c in range(2):
                    last = nc.vector.tensor_tensor(one_hot[:, :, c, :], io,
                                                   top_atf[:, :, c:c + 1].to_broadcast([P, RT, NE]), ALU.is_equal)
                last.then_inc(front_chain.next(), 1)
                dve.wait_ge(front_chain.sem, front_chain.so_far())
                for c in range(2):
                    last = nc.vector.tensor_tensor(one_hot[:, :, c, :], one_hot[:, :, c, :],
                                                   share[:, :, c:c + 1].to_broadcast([P, RT, NE]), ALU.mult)
                last.then_inc(front_chain.next(), 1)
                dve.wait_ge(front_chain.sem, front_chain.so_far())
                yield
                nc.vector.tensor_tensor(we[:, :, :], one_hot[:, :, 0, :], one_hot[:, :, 1, :], ALU.add).then_inc(
                    front_chain.next(), 1)
                dve.wait_ge(front_chain.sem, front_chain.so_far())
                if not by_distance:
                    nc.vector.memset(we[:, :, NE - 1:NE], 1.0).then_inc(front_chain.next(), 1)
                    dve.wait_ge(front_chain.sem, front_chain.so_far())
                nc.vector.tensor_copy(we_hi[:, :, :], we[:, :, :]).then_inc(front_chain.next(), 1)
                dve.wait_ge(front_chain.sem, front_chain.so_far())
                dve.wait_ge(weT_ps.sem, weT_ps.at(k, 1, 1))
                nc.vector.tensor_copy(we_parts[:, :, 0:NE], we_hi[:, :, :].bitcast(F32))
                nc.vector.tensor_tensor(we_parts[:, :, LOW:WROWS], we[:, :, :], we_hi[:, :, :].bitcast(F32),
                                        ALU.subtract).then_inc(we_ready.sem, 1)
                dve.wait_ge(we_ready.sem, we_ready.at(k, 1))
                yield from skip(N - 18)
                dve.wait_ge(y_hi_ready.sem, y_hi_ready.at(k, 1))
                nc.vector.tensor_tensor(y_lo[:, :], yT[:, :], y_hi[:, :].bitcast(F32), ALU.subtract).then_inc(
                    y_lo_ready.sem, 1)
                front_chain.end()

            def back(i):
                for n in range(N):
                    if n >= 1:
                        hidden(i, n - 1)
                    if n >= 2:
                        low_part(i, n - 2)
                    yield

            def finish(i):
                back_chain.begin(i)
                hidden(i, N - 1)
                low_part(i, N - 2)
                yield
                low_part(i, N - 1)
                yield from skip(5)
                dve.wait_ge(f_ready.sem, f_ready.at(i, 1))
                norm_out.moments(nc, dve, back_chain, lambda j: f[:, j, :])
                yield from skip(2)
                add_normed(nc, dve, back_chain, norm_out, i, x, i * RT, f)
                dve.wait_ge(back_chain.sem, back_chain.so_far())
                back_chain.end()

            run_pipeline(dve, front, back, finish)

        @block.scalar
        def _(act):
            nc.scalar.preload_act_table(ACT.Silu)
            sigs = [yT_ready, y_hi_ready, th_ready, weT_ready, weights_ready, silu_done, hi_done, accT_ready, f_ready]
            if by_distance:
                sigs += [sq_ready]
            for s in sigs:
                s.credit(act)
            act.wait_ge(loaded, 16)

            def expert_weights_row(i, e):
                act.wait_ge(weights_ps.sem, weights_ps.at(i, e + 1))
                if e < 2:
                    act.wait_ge(gated_done.sem, gated_done.at(i, N + FC * (e - 1), 1))
                else:
                    act.wait_ge(gated_done.sem, gated_done.at(i, FC * (e - 1)))
                nc.scalar.activation(weights[e % 2][:, :], ps[:, 7, :], ACT.Copy).then_inc(weights_ready.sem, 1)

            def high_part(i, n):
                r = rows_of[n % FC]
                act.wait_ge(h_done.sem, h_done.at(i, n + 1))
                if n < RING:
                    act.wait_ge(down_done.sem, down_done.at(i, N - RING + 1 + n, 1))
                else:
                    act.wait_ge(down_done.sem, down_done.at(i, n - RING + 1))
                nc.scalar.activation(h_hi[0:r, n % RING, :], h[n % 2][0:r, :], ACT.Copy).then_inc(hi_done.sem, 1)

            def front(k):
                yield from skip(10)
                act.wait_ge(yT_ps.sem, yT_ps.at(k, 1))
                act.wait_ge(y_lo_ready.sem, y_lo_ready.at(k, 1, 1))
                nc.scalar.activation(yT[:, :], ps[:, 6, :], ACT.Copy).then_inc(yT_ready.sem, 1)
                if by_distance:
                    act.wait_ge(y_ready.sem, y_ready.at(k, 1))
                    act.wait_ge(d2_ready.sem, d2_ready.at(k, 1, 1))
                    for t in range(RT):
                        last = nc.scalar.activation(square[:, t, :], y[:, t, :], ACT.Square, accum_out=sq_y[:, t:t + 1])
                    last.then_inc(sq_ready.sem, 1)
                yield from skip(6)
                act.wait_ge(gap_ready.sem, gap_ready.at(k, 1))
                nc.scalar.activation(th[:, :], gap[:, :], ACT.Tanh, scale=0.5).then_inc(th_ready.sem, 1)
                yield from skip(6)
                act.wait_ge(weT_ps.sem, weT_ps.at(k, 1))
                nc.scalar.activation(weT[:, :], ps[0:WROWS, 6, :], ACT.Copy).then_inc(weT_ready.sem, 1)
                yield from skip(N - 22)
                act.wait_ge(yT_ready.sem, yT_ready.at(k, 1))
                act.wait_ge(up_ps.sem, up_ps.at(k, N, 1))
                nc.scalar.activation(y_hi[:, :], yT[:, :], ACT.Copy).then_inc(y_hi_ready.sem, 1)

            def back(i):
                for n in range(N):
                    r = rows_of[n % FC]
                    if n == 0:
                        expert_weights_row(i, 0)
                    act.wait_ge(gate_ps.sem, gate_ps.at(i, n + 1))
                    if n < 2:
                        act.wait_ge(gated_done.sem, gated_done.at(i, N - 1 + n, 1))
                    else:
                        act.wait_ge(gated_done.sem, gated_done.at(i, n - 1))
                    bias = at["gate_b"][0:r, n:n + 1] if by_distance else 0.0
                    nc.scalar.activation(gate[n % 2][0:r, :], ps[0:r, n % 2, :], ACT.Silu, bias=bias).then_inc(
                        silu_done.sem, 1)
                    if n >= 2:
                        high_part(i, n - 2)
                    if n % FC == FC - 1 and n < N - 1:
                        expert_weights_row(i, n // FC + 1)
                    yield

            def finish(i):
                high_part(i, N - 2)
                yield
                high_part(i, N - 1)
                yield from skip(2)
                act.wait_ge(down_done.sem, down_done.at(i, N))
                act.wait_ge(f_ps.sem, f_ps.at(i, 1, 1))
                nc.scalar.activation(accT[:, :], ps[:, 5, :], ACT.Copy).then_inc(accT_ready.sem, 1)
                yield from skip(2)
                act.wait_ge(f_ps.sem, f_ps.at(i, 1))
                act.wait_ge(back_chain.sem, back_chain.sig.at(i, back_chain.per, 1))
                nc.scalar.activation(f[:, :, :], ps[:, 6, :].rearrange("p (t d) -> p t d", t=RT), ACT.Copy).then_inc(
                    f_ready.sem, 1)
                yield

            run_pipeline(act, front, back, finish)

        @block.tensor
        def _(pe):
            mm = nc.tensor.matmul
            for s in (yT_ps, router_ps, weT_ps, weights_ps, gate_ps, up_ps, down_done, f_ps):
                s.credit(pe)
            pe.wait_ge(loaded, 16)
            if by_distance:
                pe.wait_ge(ones_ready, 1)
                pe.wait_ge(c2_sq, 1)
                mm(ps[:, 7, 0:NE], ones[:, :], c2[:, 0:NE], start=True, stop=True).then_inc(c2_ps, 1)
            pe.wait_ge(constants, 4 if by_distance else 1)
            router = c2[:, 2 * NE:3 * NE] if by_distance else at["router"]

            def front(k):
                yield from skip(9)
                pe.wait_ge(y_ready.sem, y_ready.at(k, 1))
                pe.wait_ge(f_ready.sem, f_ready.at(k, 1, 2))
                for t in range(RT):
                    last = nc.tensor.transpose(ps[:, 6, t * P:(t + 1) * P], y[:, t, :], g.ident[:, :])
                last.then_inc(yT_ps.sem, 1)
                yield from skip(3)
                pe.wait_ge(yT_ready.sem, yT_ready.at(k, 1))
                for t in range(RT):
                    last = mm(ps[:, 6, t * NE:(t + 1) * NE], yT[:, t * P:(t + 1) * P], router, start=True, stop=True)
                last.then_inc(router_ps.sem, 1)
                yield from skip(9)
                pe.wait_ge(we_ready.sem, we_ready.at(k, 1))
                for t in range(RT):
                    last = mm(ps[0:WROWS, 6, t * P:(t + 1) * P], we_parts[:, t, :], g.ident[:, :], start=True, stop=True)
                last.then_inc(weT_ps.sem, 1)
                yield

            def down(i, n):
                e, c, r = n // FC, n % FC, rows_of[n % FC]
                if n == 0:
                    pe.wait_ge(accT_ready.sem, accT_ready.at(i, 1, 1))
                    if by_distance:
                        mm(ps[:, 5, :], down_b_hi[:, :], weT[:, :], start=True, stop=False)
                        mm(ps[:, 5, :], down_b_lo[:, :], weT[:, :], start=False, stop=False)
                pe.wait_ge(lo_done.sem, lo_done.at(i, n + 1))
                hi, lo = w["down_hi"][0:r, e, c, :], w["down_lo"][0:r, e, c, :]
                mm(ps[:, 5, :], hi, h_hi[0:r, n % RING, :], start=n == 0 and not by_distance, stop=False)
                mm(ps[:, 5, :], lo, h_hi[0:r, n % RING, :], start=False, stop=False)
                mm(ps[:, 5, :], hi, h_lo[0:r, n % RING, :], start=False, stop=n == N - 1).then_inc(down_done.sem, 1)

            def weights_of(i, e):
                if e == 0:
                    pe.wait_ge(weT_ready.sem, weT_ready.at(i, 1))
                    pe.wait_ge(weights_ready.sem, weights_ready.at(i, NE, 1))
                else:
                    pe.wait_ge(weights_ready.sem, weights_ready.at(i, e))
                mm(ps[:, 7, :], pick_expert[:, e * P:(e + 1) * P], weT[:, :], start=True, stop=True).then_inc(
                    weights_ps.sem, 1)

            def back(i):
                for n in range(N):
                    e, c, r = n // FC, n % FC, rows_of[n % FC]
                    if n == 0:
                        weights_of(i, 0)
                        pe.wait_ge(y_hi_ready.sem, y_hi_ready.at(i, 1))
                        pe.wait_ge(y_lo_ready.sem, y_lo_ready.at(i, 1))
                    for k, (bank, done) in enumerate(((n % 2, gate_ps), (2 + n % 3, up_ps))):
                        if k == 0 and n < 2:
                            pe.wait_ge(silu_done.sem, silu_done.at(i, N - 1 + n, 1))
                        elif k == 0:
                            pe.wait_ge(silu_done.sem, silu_done.at(i, n - 1))
                        elif n < 3:
                            pe.wait_ge(h_done.sem, h_done.at(i, N - 2 + n, 1))
                        else:
                            pe.wait_ge(h_done.sem, h_done.at(i, n - 2))
                        s = slice(k * width + c * P, k * width + c * P + r)
                        o = ps[0:r, bank, :]
                        mm(o, w["gu_hi"][:, e, s], y_hi[:, :], start=True, stop=False)
                        mm(o, w["gu_hi"][:, e, s], y_lo[:, :], start=False, stop=False)
                        mm(o, w["gu_lo"][:, e, s], y_hi[:, :], start=False, stop=True).then_inc(done.sem, 1)
                    if c == 1 and e + 1 < NE:
                        weights_of(i, e + 1)
                    if n == 4:
                        down(i, 0)
                    if n >= 4:
                        down(i, n - 3)
                    yield

            def finish(i):
                for n in range(N - 3, N):
                    down(i, n)
                    yield
                yield
                pe.wait_ge(accT_ready.sem, accT_ready.at(i, 1))
                for t in range(RT):
                    last = nc.tensor.transpose(ps[:, 6, t * P:(t + 1) * P], accT[:, t * P:(t + 1) * P], g.ident[:, :])
                last.then_inc(f_ps.sem, 1)
                yield

            run_pipeline(pe, front, back, finish)



F_SEL = 2 * P
SEL = [("nav_w", P), ("nav_b", 1), ("choose_w", NE), ("choose_b", NE), ("wo", P), ("bo", P)]
SEL_EXPERT = [("w1", F_SEL), ("w2", F_SEL), ("b1", F_SEL // P), ("b2", 1)]


def columns(tensor, names):
    at, off = {}, 0
    for name, width in names:
        at[name] = tensor[:, off:off + width]
        off += width
    assert off == tensor.shape[1]
    return at


def selected_ffn(nc, g, layer, blob, experts_dram):
    x = g.x
    with ExitStack() as ctx:
        st = Stage(nc, ctx, f"f{layer}")
        ps = st.ps
        wb = st.sb("w", [P, blob.shape[1]])
        at = columns(wb, SEL)
        expert = [st.sb(f"expert{k}", [P, experts_dram.shape[2]]) for k in range(2)]
        ex = [columns(e, SEL_EXPERT) for e in expert]
        y = [st.sb(f"y{k}", [P, T, P]) for k in range(2)]
        yT = [st.sb(f"yT{k}", [P, SEQ]) for k in range(2)]
        nav = st.sb("nav", [P, 1])
        logits, best = st.sb("logits", [1, NE]), st.sb("best", [1, 8])
        chosen = [st.sb(f"chosen{k}", [1, 8], U32) for k in range(2)]
        hT = st.sb("hT", [P, 2, SEQ])
        rT = st.sb("rT", [P, SEQ])
        f = st.sb("f", [P, T, P])
        bo = st.sb("bo", [P, P])
        norm_in, norm_out = Norm(st, "in", T), Norm(st, "out", T)
        loaded, bo_ready = st.sem("loaded"), st.sem("bo_ready")
        y_ready, yT_ps, yT_ready = st.sig("y_ready", 1), st.sig("yT_ps", 1), st.sig("yT_ready", 1)
        nav_ps, nav_ready = st.sig("nav_ps", 1), st.sig("nav_ready", 1)
        logit_ps, chosen_ready = st.sig("logit_ps", 1), st.sig("chosen_ready", 1)
        expert_loaded = [st.sem(f"expert_loaded{k}") for k in range(2)]
        h_ps, h_ready = st.sig("h_ps", 2), st.sig("h_ready", 2)
        r_ps, r_ready = st.sig("r_ps", 1), st.sig("r_ready", 1)
        out_ps, f_ready = st.sig("out_ps", 1), st.sig("f_ready", 1)
        front_chain = Chain(st.sem("dve_front"), Norm.CHAIN + 2)
        back_chain = Chain(st.sem("dve_back"), Norm.CHAIN + 3)
        block = ctx.enter_context(nc.Block())

        @block.sync
        def _(sp):
            sp.dma_start(wb[:, :], blob).then_inc(loaded, 16)

            def front(i, p):
                yield
                yield
                yield
                sp.wait_ge(chosen_ready.sem, chosen_ready.at(i, 1))
                own_wait(sp, st.sp_waited)
                sp.wait_ge(f_ready.sem, f_ready.at(i, 1, 2))
                own_wait(sp, st.sp_waited)
                e = sp.value_load(chosen[p][0:1, 0:1], min_val=0, max_val=NE - 1)
                sp.dma_start(expert[p][:, :], experts_dram[e, :, :]).then_inc(expert_loaded[p], 16)
                yield

            pipeline(sp, front, lambda i, p: iter(()))

        @block.gpsimd
        def _(pool):
            norm_in.rstd_ready.credit(pool)
            norm_out.rstd_ready.credit(pool)

            def front(i, p):
                norm_in.power(nc, pool, i, g.minus_half)
                yield

            def back(i, p):
                yield
                yield
                norm_out.power(nc, pool, i, g.minus_half)
                yield

            pipeline(pool, front, back)

        @block.vector
        def _(dve):
            for s in (norm_in.var_ready, norm_out.var_ready, y_ready, chosen_ready, f_ready, front_chain.sig,
                      back_chain.sig):
                s.credit(dve)
            dve.wait_ge(loaded, 16)
            nc.vector.tensor_scalar(bo[:, :], at["bo"], 0.3, None, ALU.mult).then_inc(bo_ready, 1)
            dve.wait_ge(bo_ready, 1)

            def front(i, p):
                front_chain.begin(i)
                norm_in.moments(nc, dve, front_chain, lambda j: x[:, i * T + j, :])
                dve.wait_ge(norm_in.rstd_ready.sem, norm_in.rstd_ready.at(i, 1))
                dve.wait_ge(f_ready.sem, f_ready.at(i, 1, 2))
                for j in range(T):
                    last = norm_in.apply(nc, j, y[p][:, j, :], x[:, i * T + j, :])
                last.then_inc(y_ready.sem, 1)
                yield
                yield
                yield
                dve.wait_ge(logit_ps.sem, logit_ps.at(i, 1))
                nc.vector.tensor_tensor(logits[:, :], ps[0:1, 0, 0:NE], at["choose_b"][0:1, :], ALU.add).then_inc(front_chain.next(), 1)
                dve.wait_ge(front_chain.sem, front_chain.so_far())
                own_wait(dve, st.dve_waited)
                nc.vector.max(best[:, :], logits[:, :]).then_inc(front_chain.next(), 1)
                dve.wait_ge(front_chain.sem, front_chain.so_far())
                own_wait(dve, st.dve_waited)
                nc.vector.max_index(chosen[p][:, :], best[:, :], logits[:, :]).then_inc(chosen_ready.sem, 1)
                dve.wait_ge(chosen_ready.sem, chosen_ready.at(i, 1))
                yield
                front_chain.end()

            def back(i, p):
                back_chain.begin(i)
                yield
                yield
                dve.wait_ge(y_ready.sem, y_ready.at(i, 1))
                for t in range(T):
                    last = nc.vector.tensor_tensor(y[p][:, t, :], y[p][:, t, :], bo[:, :], ALU.add)
                last.then_inc(back_chain.next(), 1)
                dve.wait_ge(back_chain.sem, back_chain.so_far())
                dve.wait_ge(out_ps.sem, out_ps.at(i, 1))
                nc.vector.scalar_tensor_tensor(f[:, :, :], ps[:, 5, 0:SEQ].rearrange("p (t d) -> p t d", t=T), 0.3,
                                               y[p][:, :, :], ALU.mult, ALU.add).then_inc(f_ready.sem, 1)
                dve.wait_ge(f_ready.sem, f_ready.at(i, 1))
                norm_out.moments(nc, dve, back_chain, lambda j: f[:, j, :])
                yield
                add_normed(nc, dve, back_chain, norm_out, i, x, i * T, f)
                dve.wait_ge(back_chain.sem, back_chain.so_far())
                back_chain.end()
                yield

            pipeline(dve, front, back)

        @block.scalar
        def _(act):
            nc.scalar.preload_act_table(ACT.Gelu)
            for s in (yT_ready, nav_ready, h_ready, r_ready):
                s.credit(act)
            act.wait_ge(loaded, 16)

            def front(i, p):
                yield
                act.wait_ge(yT_ps.sem, yT_ps.at(i, 1))
                act.wait_ge(h_ps.sem, h_ps.at(i, 2, 2))
                nc.scalar.activation(yT[p][:, :], ps[:, 0, 0:SEQ], ACT.Copy).then_inc(yT_ready.sem, 1)
                yield
                act.wait_ge(nav_ps.sem, nav_ps.at(i, 1))
                nc.scalar.activation(nav[:, :], ps[:, 1, 0:1], ACT.Gelu, bias=at["nav_b"]).then_inc(nav_ready.sem, 1)
                yield

            def back(i, p):
                act.wait_ge(expert_loaded[p], (i - p) * 8 + 16)
                for c in range(2):
                    act.wait_ge(h_ps.sem, h_ps.at(i, c + 1))
                    nc.scalar.activation(hT[:, c, :], ps[:, 2 + c, 0:SEQ], ACT.Gelu, bias=ex[p]["b1"][:, c:c + 1]).then_inc(
                        h_ready.sem, 1)
                yield
                act.wait_ge(r_ps.sem, r_ps.at(i, 1))
                nc.scalar.activation(rT[:, :], ps[:, 4, 0:SEQ], ACT.Identity, bias=ex[p]["b2"]).then_inc(r_ready.sem, 1)
                yield

            pipeline(act, front, back)

        @block.tensor
        def _(pe):
            mm = nc.tensor.matmul
            for s in (yT_ps, nav_ps, logit_ps, h_ps, r_ps, out_ps):
                s.credit(pe)
            pe.wait_ge(loaded, 16)

            def front(i, p):
                yield
                pe.wait_ge(y_ready.sem, y_ready.at(i, 1))
                pe.wait_ge(chosen_ready.sem, chosen_ready.at(i, 1, 1))
                for t in range(T):
                    last = nc.tensor.transpose(ps[:, 0, t * P:(t + 1) * P], y[p][:, t, :], g.ident[:, :])
                last.then_inc(yT_ps.sem, 1)
                yield
                pe.wait_ge(yT_ready.sem, yT_ready.at(i, 1))
                pe.wait_ge(nav_ready.sem, nav_ready.at(i, 1, 1))
                mm(ps[:, 1, 0:1], at["nav_w"], yT[p][:, SEQ - 1:SEQ], start=True, stop=True).then_inc(nav_ps.sem, 1)
                yield
                pe.wait_ge(nav_ready.sem, nav_ready.at(i, 1))
                mm(ps[0:1, 0, 0:NE], nav[:, :], at["choose_w"], start=True, stop=True).then_inc(logit_ps.sem, 1)
                yield

            def back(i, p):
                pe.wait_ge(expert_loaded[p], (i - p) * 8 + 16)
                for c in range(2):
                    pe.wait_ge(h_ready.sem, h_ready.at(i, c + 1, 1))
                    mm(ps[:, 2 + c, 0:SEQ], ex[p]["w1"][:, c * P:(c + 1) * P], yT[p][:, :], start=True,
                       stop=True).then_inc(h_ps.sem, 1)
                yield
                pe.wait_ge(r_ready.sem, r_ready.at(i, 1, 1))
                for c in range(2):
                    pe.wait_ge(h_ready.sem, h_ready.at(i, c + 1))
                    last = mm(ps[:, 4, 0:SEQ], ex[p]["w2"][:, c * P:(c + 1) * P], hT[:, c, :], start=c == 0, stop=c == 1)
                last.then_inc(r_ps.sem, 1)
                yield
                pe.wait_ge(r_ready.sem, r_ready.at(i, 1))
                pe.wait_ge(f_ready.sem, f_ready.at(i, 1, 1))
                for t in range(T):
                    last = mm(ps[:, 5, t * P:(t + 1) * P], rT[:, t * P:(t + 1) * P], at["wo"], start=True, stop=True)
                last.then_inc(out_ps.sem, 1)
                yield

            pipeline(pe, front, back)



MIX = [("wqk", 2 * P), ("wv", P), ("wo", P), ("blocks", P)]


def channel_attention(nc, g, blob):
    SCALE = float(D8) ** -0.5
    x = g.x
    with ExitStack() as ctx:
        st = Stage(nc, ctx, "a3")
        ps = st.ps
        wb = st.sb("w", [P, blob.shape[1]])
        at = columns(wb, MIX)
        y = st.sb("y", [P, T, P])
        yT = st.sb("yT", [P, SEQ])
        qk = [st.sb(f"qk{k}", [P, T, 2 * P]) for k in range(2)]
        vT = [st.sb(f"vT{k}", [P, SEQ]) for k in range(2)]
        z, z_exp, zn = st.sb("z", [P, P]), st.sb("z_exp", [P, P]), st.sb("zn", [P, P])
        top, neg_top, total, recip = (st.sb(n, [P, 1]) for n in ("top", "neg_top", "total", "recip"))
        cxT = st.sb("cxT", [P, SEQ])
        f = st.sb("f", [P, T, P])
        norm_in, norm_out = Norm(st, "in", T), Norm(st, "out", T)
        loaded = st.sem("loaded")
        y_ready, yT_ps, yT_ready = st.sig("y_ready", 1), st.sig("yT_ps", 1), st.sig("yT_ready", 1)
        qk_ps, qk_ready, v_ps, v_ready = (st.sig(n, 1) for n in ("qk_ps", "qk_ready", "v_ps", "v_ready"))
        z_ps, top_ready, exp_ready, zn_ready = (st.sig(n, 1) for n in ("z_ps", "top_ready", "exp_ready", "zn_ready"))
        cxT_ps, cxT_ready, out_ps, f_ready = (st.sig(n, 1) for n in ("cxT_ps", "cxT_ready", "out_ps", "f_ready"))
        front_chain = Chain(st.sem("dve_front"), Norm.CHAIN)
        back_chain = Chain(st.sem("dve_back"), Norm.CHAIN + 5)
        block = ctx.enter_context(nc.Block())

        @block.sync
        def _(sp):
            sp.dma_start(wb[:, :], blob).then_inc(loaded, 16)

        @block.gpsimd
        def _(pool):
            norm_in.rstd_ready.credit(pool)
            norm_out.rstd_ready.credit(pool)

            def front(i, p):
                norm_in.power(nc, pool, i, g.minus_half)
                yield

            def back(i, p):
                yield
                yield
                yield
                norm_out.power(nc, pool, i, g.minus_half)
                yield

            pipeline(pool, front, back)

        @block.vector
        def _(dve):
            for s in (norm_in.var_ready, norm_out.var_ready, y_ready, top_ready, zn_ready, f_ready, front_chain.sig,
                      back_chain.sig):
                s.credit(dve)
            dve.wait_ge(loaded, 16)

            def front(i, p):
                front_chain.begin(i)
                norm_in.moments(nc, dve, front_chain, lambda j: x[:, i * T + j, :])
                dve.wait_ge(norm_in.rstd_ready.sem, norm_in.rstd_ready.at(i, 1))
                for j in range(T):
                    last = norm_in.apply(nc, j, y[:, j, :], x[:, i * T + j, :])
                last.then_inc(y_ready.sem, 1)
                yield
                front_chain.end()

            def back(i, p):
                back_chain.begin(i)
                dve.wait_ge(z_ps.sem, z_ps.at(i, 1))
                nc.vector.tensor_tensor(z[:, :], ps[:, 2, 0:P], at["blocks"], ALU.add).then_inc(back_chain.next(), 1)
                dve.wait_ge(back_chain.sem, back_chain.so_far())
                nc.vector.reduce_max(top[:, :], z[:, :], AX).then_inc(back_chain.next(), 1)
                dve.wait_ge(back_chain.sem, back_chain.so_far())
                nc.vector.tensor_scalar(neg_top[:, :], top[:, :], -SCALE, None, ALU.mult).then_inc(top_ready.sem, 1)
                yield
                dve.wait_ge(exp_ready.sem, exp_ready.at(i, 1))
                nc.vector.reciprocal(recip[:, :], total[:, :]).then_inc(back_chain.next(), 1)
                dve.wait_ge(back_chain.sem, back_chain.so_far())
                nc.vector.tensor_scalar(zn[:, :], z_exp[:, :], recip[:, 0:1], None, ALU.mult).then_inc(zn_ready.sem, 1)
                yield
                yield
                dve.wait_ge(out_ps.sem, out_ps.at(i, 1))
                nc.vector.tensor_copy(f[:, :, :], ps[:, 4, 0:SEQ].rearrange("p (t d) -> p t d", t=T)).then_inc(
                    f_ready.sem, 1)
                dve.wait_ge(f_ready.sem, f_ready.at(i, 1))
                norm_out.moments(nc, dve, back_chain, lambda j: f[:, j, :])
                yield
                add_normed(nc, dve, back_chain, norm_out, i, x, i * T, f)
                dve.wait_ge(back_chain.sem, back_chain.so_far())
                back_chain.end()
                yield

            pipeline(dve, front, back)

        @block.scalar
        def _(act):
            nc.scalar.preload_act_table(ACT.Exp)
            for s in (yT_ready, qk_ready, v_ready, exp_ready, cxT_ready):
                s.credit(act)

            def front(i, p):
                yield
                act.wait_ge(yT_ps.sem, yT_ps.at(i, 1))
                nc.scalar.activation(yT[:, :], ps[:, 0, 0:SEQ], ACT.Copy).then_inc(yT_ready.sem, 1)
                yield
                act.wait_ge(qk_ps.sem, qk_ps.at(i, 1))
                nc.scalar.activation(qk[p][:, :, :], ps[:, 1, :].rearrange("p (t d) -> p t d", t=T), ACT.Copy).then_inc(
                    qk_ready.sem, 1)
                act.wait_ge(v_ps.sem, v_ps.at(i, 1))
                nc.scalar.activation(vT[p][:, :], ps[:, 0, 0:SEQ], ACT.Copy).then_inc(v_ready.sem, 1)
                yield

            def back(i, p):
                act.wait_ge(top_ready.sem, top_ready.at(i, 1))
                act.wait_ge(zn_ready.sem, zn_ready.at(i, 1, 1))
                nc.scalar.activation(z_exp[:, :], z[:, :], ACT.Exp, bias=neg_top[:, :], scale=SCALE,
                                     accum_out=total[:, :]).then_inc(exp_ready.sem, 1)
                yield
                yield
                act.wait_ge(cxT_ps.sem, cxT_ps.at(i, 1))
                nc.scalar.activation(cxT[:, :], ps[:, 3, 0:SEQ], ACT.Copy).then_inc(cxT_ready.sem, 1)
                yield

            pipeline(act, front, back)

        @block.tensor
        def _(pe):
            mm = nc.tensor.matmul
            for s in (yT_ps, qk_ps, v_ps, z_ps, cxT_ps, out_ps):
                s.credit(pe)
            pe.wait_ge(loaded, 16)

            def front(i, p):
                yield
                pe.wait_ge(y_ready.sem, y_ready.at(i, 1))
                pe.wait_ge(v_ready.sem, v_ready.at(i, 1, 1))
                for t in range(T):
                    last = nc.tensor.transpose(ps[:, 0, t * P:(t + 1) * P], y[:, t, :], g.ident[:, :])
                last.then_inc(yT_ps.sem, 1)
                yield
                pe.wait_ge(yT_ready.sem, yT_ready.at(i, 1))
                pe.wait_ge(qk_ready.sem, qk_ready.at(i, 1, 1))
                for t in range(T):
                    last = mm(ps[:, 1, t * 2 * P:(t + 1) * 2 * P], yT[:, t * P:(t + 1) * P], at["wqk"], start=True,
                              stop=True)
                last.then_inc(qk_ps.sem, 1)
                mm(ps[:, 0, 0:SEQ], at["wv"], yT[:, :], start=True, stop=True).then_inc(v_ps.sem, 1)
                yield

            def back(i, p):
                pe.wait_ge(qk_ready.sem, qk_ready.at(i, 1))
                pe.wait_ge(top_ready.sem, top_ready.at(i, 1, 1))
                for t in range(T):
                    last = mm(ps[:, 2, 0:P], qk[p][:, t, P:2 * P], qk[p][:, t, 0:P], start=t == 0, stop=t == T - 1)
                last.then_inc(z_ps.sem, 1)
                yield
                yield
                pe.wait_ge(zn_ready.sem, zn_ready.at(i, 1))
                pe.wait_ge(v_ready.sem, v_ready.at(i, 1))
                pe.wait_ge(cxT_ready.sem, cxT_ready.at(i, 1, 1))
                mm(ps[:, 3, 0:SEQ], zn[:, :], vT[p][:, :], start=True, stop=True).then_inc(cxT_ps.sem, 1)
                yield
                pe.wait_ge(cxT_ready.sem, cxT_ready.at(i, 1))
                pe.wait_ge(f_ready.sem, f_ready.at(i, 1, 1))
                for t in range(T):
                    last = mm(ps[:, 4, t * P:(t + 1) * P], cxT[:, t * P:(t + 1) * P], at["wo"], start=True, stop=True)
                last.then_inc(out_ps.sem, 1)
                yield

            pipeline(pe, front, back)



GQA = [("wq", NH * D64), ("wk", NG * P), ("wv", NG * D64), ("wpost", NH * D64),
       ("spread_sums", NH // 2 * P)]


def grouped_attention(nc, g, blob):
    SCALE = float(D64) ** -0.5
    COLS = 32
    PAIRS = NH // 2
    x = g.x
    with ExitStack() as ctx:
        st = Stage(nc, ctx, "a2")
        ps = st.ps
        wb = st.sb("w", [P, blob.shape[1]])
        at = columns(wb, GQA)
        y = [st.sb(f"y{k}", [P, T, P]) for k in range(2)]
        f = st.sb("f", [P, T, P])
        yT = st.sb("yT", [P, SEQ])
        Q = {part: [st.sb(f"q_{part}{k}", [P, PAIRS, SEQ], F32R) for k in range(2)] for part in ("hi", "lo")}
        K = {part: [st.sb(f"k_{part}{k}", [P, 2, NG, SEQ], F32R) for k in range(2)] for part in ("hi", "lo")}
        V = [st.sb(f"V{k}", [P, T, NG, D64]) for k in range(2)]
        sum_cols = st.sb("sum_cols", [P, NG, COLS])
        rowmax = st.sb("rowmax", [P, T, NH])
        mrow = [st.sb(f"mrow{k}", [NG, SEQ], F32R) for k in range(NG)]
        maxima = st.sb("maxima", [P, NG, HG * SEQ], F32R)
        ones_row = st.sb("ones_row", [P, P], F32R)
        ones_raw = st.sb("ones_raw", [P, P])
        probs = [st.sb(f"probs{k}", [P, 4, BANK]) for k in range(2)]
        recip = st.sb("recip", [P, SEQ])
        skip_y = st.sb("skip_y", [P, T, P])
        craw = st.sb("craw", [P, PAIRS, SEQ])
        cxT = st.sb("cxT", [P, PAIRS, SEQ])
        norm_in, norm_out = Norm(st, "in", T), Norm(st, "out", T)
        loaded, constants = st.sem("loaded"), st.sem("constants_ready")
        y_ready, yT_ps, yT_ready = st.sig("y_ready", 1), st.sig("yT_ps", 1), st.sig("yT_ready", 1)
        q_ps, q_hi_ready, q_lo_ready = st.sig("q_ps", NG), st.sig("q_hi_ready", NG), st.sig("q_lo_ready", NG)
        k_ps, k_hi_ready, k_lo_ready = st.sig("k_ps", 2), st.sig("k_hi_ready", 2), st.sig("k_lo_ready", 2)
        v_ps, v_ready = st.sig("v_ps", 1), st.sig("v_ready", 1)
        FILLS = 4
        score_ps, rowmax_ready = st.sig("score_ps", NG * FILLS), st.sig("rowmax_ready", NG * FILLS)
        max_ps, mrow_ready = st.sig("max_ps", NG), st.sig("mrow_ready", NG)
        mrow_placed = [st.sem(f"mrow_placed{j}") for j in range(NG)]
        sT_ps, exp_done = st.sig("sT_ps", NG * FILLS), st.sig("exp_done", NG * FILLS)
        pv_done, craw_ready = st.sig("pv_done", NG), st.sig("craw_ready", NG)
        recip_ready, recip_ps, cxT_ready = st.sig("recip_ready", 1), st.sig("recip_ps", NG), st.sig("cxT_ready", NG)
        skip_ready = st.sig("skip_ready", 1)
        out_ps, f_ready = st.sig("out_ps", 1), st.sig("f_ready", 1)
        front_chain = Chain(st.sem("dve_front"), Norm.CHAIN)
        back_chain = Chain(st.sem("dve_back"), Norm.CHAIN + 2)
        HEAD = 5
        FINISH = 8
        block = ctx.enter_context(nc.Block())

        @block.sync
        def _(sp):
            sp.dma_start(wb[:, :], blob).then_inc(loaded, 16)

            def front(i, p):
                yield from skip(HEAD + FILLS + 2)
                for j in range(NG):
                    sp.wait_ge(mrow_ready.sem, mrow_ready.at(i, j + 1))
                    own_wait(sp, st.sp_waited)
                    sp.wait_ge(sT_ps.sem, sT_ps.at(i, (j + 1) * FILLS, 1))
                    sp.dma_start(maxima[0:1, j, :].rearrange("p (h q) -> p h q", h=HG).bitcast(F32),
                                 mrow[j][:, :].bitcast(F32)).then_inc(mrow_placed[j], 16)
                    yield from skip(FILLS)

            pipeline3(sp, front, nothing, nothing)

        @block.gpsimd
        def _(pool):
            norm_in.rstd_ready.credit(pool)
            norm_out.rstd_ready.credit(pool)
            def front(i, p):
                norm_in.power(nc, pool, i, g.minus_half)
                yield

            def finish(i):
                yield from skip(7)
                norm_out.power(nc, pool, i, g.minus_half)
                yield

            pipeline3(pool, front, nothing, finish)

        @block.vector
        def _(dve):
            for s in (norm_in.var_ready, norm_out.var_ready, y_ready, q_lo_ready, k_lo_ready, v_ready,
                      rowmax_ready, recip_ready, cxT_ready, skip_ready, f_ready, front_chain.sig, back_chain.sig):
                s.credit(dve)
            for k in range(2):
                for part in ("hi", "lo"):
                    nc.vector.memset(K[part][k][D64:P, 0, :, :].bitcast(F32), 0.0)
                    nc.vector.memset(K[part][k][0:D64, 1, :, :].bitcast(F32), 0.0)
            nc.vector.memset(maxima[:, :, :].bitcast(F32), 0.0)
            nc.vector.memset(sum_cols[:, :, :], 0.0)
            nc.vector.memset(ones_raw[:, :], 0.0).then_inc(constants, 1)
            dve.wait_ge(constants, 1)
            for j in range(NG):
                nc.vector.memset(sum_cols[:, j, :].rearrange("p (c r) -> p c r", r=NG)[:, :, j:j + 1], 1.0)
            nc.vector.memset(ones_raw[0:1, :], 1.0).then_inc(constants, 1)
            dve.wait_ge(constants, 2)
            nc.vector.tensor_copy(ones_row[:, :], ones_raw[:, :]).then_inc(constants, 1)
            dve.wait_ge(constants, 3)

            def front(i, p):
                front_chain.begin(i)
                norm_in.moments(nc, dve, front_chain, lambda j: x[:, i * T + j, :])
                dve.wait_ge(norm_in.rstd_ready.sem, norm_in.rstd_ready.at(i, 1))
                dve.wait_ge(skip_ready.sem, skip_ready.at(i, 1, 2))
                for j in range(T):
                    last = norm_in.apply(nc, j, y[p][:, j, :], x[:, i * T + j, :])
                last.then_inc(y_ready.sem, 1)
                yield
                yield
                for j in range(NG):
                    dve.wait_ge(q_hi_ready.sem, q_hi_ready.at(i, j + 1))
                    nc.vector.tensor_tensor(Q["lo"][p][:, 2 * j:2 * j + 2, :],
                                            ps[:, (j + 1) % 2, :].rearrange("p (h t) -> p h t", h=2),
                                            Q["hi"][p][:, 2 * j:2 * j + 2, :].bitcast(F32), ALU.subtract).then_inc(
                        q_lo_ready.sem, 1)
                    if j == 1:
                        yield
                for n in range(2):
                    dve.wait_ge(k_hi_ready.sem, k_hi_ready.at(i, n + 1))
                    bank = ps[:, (n + 1) % 2, :].rearrange("p (g t) -> p g t", g=2)
                    for half, rows in enumerate((slice(0, D64), slice(D64, P))):
                        last = nc.vector.tensor_tensor(K["lo"][p][rows, half, 2 * n:2 * n + 2, :], bank[rows],
                                                       K["hi"][p][rows, half, 2 * n:2 * n + 2, :].bitcast(F32),
                                                       ALU.subtract)
                    last.then_inc(k_lo_ready.sem, 1)
                dve.wait_ge(v_ps.sem, v_ps.at(i, 1))
                dve.wait_ge(pv_done.sem, pv_done.at(i, NG, 2))
                nc.vector.tensor_copy(V[p][:, :, :, :],
                                      ps[:, 1, :].rearrange("p (t g d) -> p t g d", t=T, g=NG)).then_inc(v_ready.sem, 1)
                yield from skip(HEAD - 3)
                for j in range(NG):
                    if j == 0:
                        dve.wait_ge(max_ps.sem, max_ps.at(i, NG, 1))
                    for n in range(FILLS):
                        c = j * FILLS + n
                        dve.wait_ge(score_ps.sem, score_ps.at(i, c + 1))
                        t, h = n // 2, 4 * j + 2 * (n % 2)
                        nc.vector.reduce_max(rowmax[:, t, h:h + 2], ps[:, 2 + c % 2, :].rearrange("p (h k) -> p h k", h=2),
                                             AX).then_inc(rowmax_ready.sem, 1)
                        yield
                front_chain.end()

            def back(i, p):
                yield from skip(FINISH)
                dve.wait_ge(y_ready.sem, y_ready.at(i, 1))
                nc.vector.tensor_copy(skip_y[:, :, :], y[p][:, :, :]).then_inc(skip_ready.sem, 1)
                yield

            def finish(i):
                back_chain.begin(i)
                dve.wait_ge(pv_done.sem, pv_done.at(i, NG))
                nc.vector.reciprocal(recip[:, :], ps[:, 7, 0:SEQ]).then_inc(recip_ready.sem, 1)
                yield
                for j in range(NG):
                    dve.wait_ge(recip_ps.sem, recip_ps.at(i, j + 1))
                    dve.wait_ge(craw_ready.sem, craw_ready.at(i, j + 1))
                    nc.vector.tensor_tensor(cxT[:, 2 * j:2 * j + 2, :], ps[:, 6, :].rearrange("p (h t) -> p h t", h=2),
                                            craw[:, 2 * j:2 * j + 2, :], ALU.mult).then_inc(cxT_ready.sem, 1)
                    yield
                dve.wait_ge(out_ps.sem, out_ps.at(i, 1))
                nc.vector.tensor_copy(f[:, :, :], ps[:, 7, SEQ:2 * SEQ].rearrange("p (t d) -> p t d", t=T)).then_inc(
                    f_ready.sem, 1)
                yield
                dve.wait_ge(f_ready.sem, f_ready.at(i, 1))
                norm_out.moments(nc, dve, back_chain, lambda j: f[:, j, :])
                yield from skip(2)
                add_normed(nc, dve, back_chain, norm_out, i, x, i * T, f)
                dve.wait_ge(back_chain.sem, back_chain.so_far())
                back_chain.end()

            pipeline3(dve, front, back, finish)

        @block.scalar
        def _(act):
            nc.scalar.preload_act_table(ACT.Exp)
            for s in (yT_ready, q_hi_ready, k_hi_ready, mrow_ready, exp_done, craw_ready):
                s.credit(act)
            act.wait_ge(constants, 3)

            def front(i, p):
                yield
                act.wait_ge(yT_ps.sem, yT_ps.at(i, 1))
                nc.scalar.activation(yT[:, :], ps[:, 0, 0:SEQ], ACT.Copy).then_inc(yT_ready.sem, 1)
                yield
                act.wait_ge(sT_ps.sem, sT_ps.at(i, NG * FILLS, 2))
                for j in range(NG):
                    act.wait_ge(q_ps.sem, q_ps.at(i, j + 1))
                    nc.scalar.activation(Q["hi"][p][:, 2 * j:2 * j + 2, :],
                                         ps[:, (j + 1) % 2, :].rearrange("p (h t) -> p h t", h=2), ACT.Copy).then_inc(
                        q_hi_ready.sem, 1)
                    if j == 1:
                        yield
                for n in range(2):
                    act.wait_ge(k_ps.sem, k_ps.at(i, n + 1))
                    bank = ps[:, (n + 1) % 2, :].rearrange("p (g t) -> p g t", g=2)
                    for half, rows in enumerate((slice(0, D64), slice(D64, P))):
                        last = nc.scalar.activation(K["hi"][p][rows, half, 2 * n:2 * n + 2, :], bank[rows], ACT.Copy)
                    last.then_inc(k_hi_ready.sem, 1)
                yield from skip(HEAD - 1)
                for j in range(NG):
                    yield from skip(FILLS)
                    act.wait_ge(max_ps.sem, max_ps.at(i, j + 1))
                    pe_bank = j % 2
                    act.wait_ge(sT_ps.sem, sT_ps.at(i, (j + 1) * FILLS, 1))
                    nc.scalar.activation(mrow[j][:, :], ps[0:NG, pe_bank, 0:SEQ], ACT.Copy, scale=-1.0).then_inc(
                        mrow_ready.sem, 1)

            def back(i, p):
                for j in range(NG + 1):
                    for n in range(FILLS):
                        if n == 0 and j > 1:
                            to_sbuf(i, j - 2)
                        if j < NG:
                            if n == 0 and j < 2:
                                act.wait_ge(pv_done.sem, pv_done.at(i, j + 3, 1))
                            elif n == 0:
                                act.wait_ge(pv_done.sem, pv_done.at(i, j - 1))
                            c = j * FILLS + n
                            act.wait_ge(sT_ps.sem, sT_ps.at(i, c + 1))
                            nc.scalar.activation(probs[j % 2][:, n, :], ps[:, 4 + c % 2, :], ACT.Exp,
                                                 scale=SCALE).then_inc(exp_done.sem, 1)
                        yield
                to_sbuf(i, NG - 1)
                yield

            def to_sbuf(i, m):
                act.wait_ge(pv_done.sem, pv_done.at(i, m + 1))
                act.wait_ge(cxT_ready.sem, cxT_ready.at(i, m + 1, 1))
                nc.scalar.activation(craw[:, 2 * m:2 * m + 2, :], ps[:, 6, :].rearrange("p (h t) -> p h t", h=2),
                                     ACT.Copy).then_inc(craw_ready.sem, 1)

            pipeline3(act, front, back, nothing)

        @block.tensor
        def _(pe):
            mm = nc.tensor.matmul
            for s in (yT_ps, q_ps, k_ps, v_ps, score_ps, max_ps, sT_ps, pv_done, recip_ps, out_ps):
                s.credit(pe)
            pe.wait_ge(loaded, 16)
            pe.wait_ge(constants, 3)

            def front(i, p):
                yield
                pe.wait_ge(y_ready.sem, y_ready.at(i, 1))
                pe.wait_ge(mrow_ready.sem, mrow_ready.at(i, NG, 1))
                for t in range(T):
                    last = nc.tensor.transpose(ps[:, 0, t * P:(t + 1) * P], y[p][:, t, :], g.ident[:, :])
                last.then_inc(yT_ps.sem, 1)
                yield
                pe.wait_ge(yT_ready.sem, yT_ready.at(i, 1))
                for j in range(NG):
                    if j >= 2:
                        pe.wait_ge(q_lo_ready.sem, q_lo_ready.at(i, j - 1))
                    for h in range(2):
                        o = 2 * j + h
                        last = mm(ps[:, (j + 1) % 2, h * SEQ:(h + 1) * SEQ], at["wq"][:, o * P:(o + 1) * P], yT[:, :],
                                  start=True, stop=True)
                    last.then_inc(q_ps.sem, 1)
                    if j == 1:
                        yield
                for n in range(2):
                    pe.wait_ge(q_lo_ready.sem, q_lo_ready.at(i, n + 3))
                    for h in range(2):
                        o = 2 * n + h
                        last = mm(ps[:, (n + 1) % 2, h * SEQ:(h + 1) * SEQ], at["wk"][:, o * P:(o + 1) * P], yT[:, :],
                                  start=True, stop=True)
                    last.then_inc(k_ps.sem, 1)
                pe.wait_ge(k_lo_ready.sem, k_lo_ready.at(i, 1))
                for t in range(T):
                    last = mm(ps[:, 1, t * SEQ:(t + 1) * SEQ], yT[:, t * P:(t + 1) * P], at["wv"], start=True, stop=True)
                last.then_inc(v_ps.sem, 1)
                yield from skip(HEAD - 3)
                pe.wait_ge(k_lo_ready.sem, k_lo_ready.at(i, 2))
                for j in range(NG + 1):
                    for n in range(FILLS):
                        if j < NG:
                            c = j * FILLS + n
                            if c < 2:
                                pe.wait_ge(rowmax_ready.sem, rowmax_ready.at(i, NG * FILLS - 1 + c, 1))
                            else:
                                pe.wait_ge(rowmax_ready.sem, rowmax_ready.at(i, c - 1))
                            t, pair = n // 2, 2 * j + n % 2
                            for h in range(2):
                                last = mm(ps[:, 2 + c % 2, h * SEQ:(h + 1) * SEQ], Q["hi"][p][:, pair, t * P:(t + 1) * P],
                                          K["hi"][p][:, h, j, :], start=True, stop=True)
                            last.then_inc(score_ps.sem, 1)
                        if j > 0 and n == 1:
                            m = j - 1
                            pe.wait_ge(rowmax_ready.sem, rowmax_ready.at(i, j * FILLS))
                            if m == 0:
                                pe.wait_ge(k_lo_ready.sem, k_lo_ready.at(i, 2))
                            elif m == 1:
                                pe.wait_ge(v_ready.sem, v_ready.at(i, 1))
                            else:
                                pe.wait_ge(mrow_ready.sem, mrow_ready.at(i, m - 1))
                            for t in range(T):
                                last = nc.tensor.transpose(ps[0:NG, m % 2, t * P:(t + 1) * P], rowmax[:, t, 4 * m:4 * m + 4],
                                                           g.ident[:, :])
                            last.then_inc(max_ps.sem, 1)
                        yield

            def scores(i, p, j, n):
                c = j * FILLS + n
                if c < 2:
                    pe.wait_ge(exp_done.sem, exp_done.at(i, NG * FILLS - 1 + c, 1))
                else:
                    pe.wait_ge(exp_done.sem, exp_done.at(i, c - 1))
                t, pair = n // 2, 2 * j + n % 2
                keys = slice(t * P, (t + 1) * P)
                bank = ps[:, 4 + c % 2, :]
                mm(bank, ones_row[:, :], maxima[:, j, (n % 2) * BANK:(n % 2 + 1) * BANK], start=True, stop=False)
                for h in range(2):
                    o = bank[:, h * SEQ:(h + 1) * SEQ]
                    mm(o, K["hi"][p][:, h, j, keys], Q["hi"][p][:, pair, :], start=False, stop=False)
                    mm(o, K["hi"][p][:, h, j, keys], Q["lo"][p][:, pair, :], start=False, stop=False)
                    last = mm(o, K["lo"][p][:, h, j, keys], Q["hi"][p][:, pair, :], start=False, stop=h == 1)
                last.then_inc(sT_ps.sem, 1)

            def values(i, p, m, u):
                if u == 0:
                    pe.wait_ge(exp_done.sem, exp_done.at(i, (m + 1) * FILLS))
                    if m == 0:
                        pe.wait_ge(cxT_ready.sem, cxT_ready.at(i, NG, 1))
                    else:
                        pe.wait_ge(craw_ready.sem, craw_ready.at(i, m))
                for kt in range(T):
                    for h in range(2):
                        mm(ps[h * D64:(h + 1) * D64, 6, u * SEQ:(u + 1) * SEQ], V[p][:, kt, m, :],
                           probs[m % 2][:, 2 * kt + u, h * SEQ:(h + 1) * SEQ], start=kt == 0, stop=kt == T - 1)
                if u == 1:
                    if m == 0:
                        pe.wait_ge(f_ready.sem, f_ready.at(i, 1, 1))
                    for kt in range(T):
                        for h in range(HG):
                            last = mm(ps[h * COLS:(h + 1) * COLS, 7, 0:SEQ], sum_cols[:, m, :],
                                      probs[m % 2][:, 2 * kt + h // 2, (h % 2) * SEQ:(h % 2 + 1) * SEQ],
                                      start=m == 0 and kt == 0, stop=m == NG - 1 and kt == T - 1)
                    last.then_inc(pv_done.sem, 1)

            def back(i, p):
                for j in range(NG + 1):
                    for n in range(FILLS):
                        if j < NG:
                            if n == 0:
                                pe.wait_ge(mrow_placed[j], i * 16 + 16)
                            scores(i, p, j, n)
                        if j > 0 and n >= 2:
                            values(i, p, j - 1, n - 2)
                        yield

            def finish(i):
                yield
                for j in range(NG + 1):
                    if j < NG:
                        pe.wait_ge(recip_ready.sem, recip_ready.at(i, 1))
                        if j == 0:
                            pe.wait_ge(craw_ready.sem, craw_ready.at(i, NG))
                        else:
                            pe.wait_ge(cxT_ready.sem, cxT_ready.at(i, j))
                        for u in range(2):
                            last = mm(ps[:, 6, u * SEQ:(u + 1) * SEQ], at["spread_sums"][:, (2 * j + u) * P:(2 * j + u + 1) * P],
                                      recip[:, :], start=True, stop=True)
                        last.then_inc(recip_ps.sem, 1)
                    if j > 0:
                        if j == 1:
                            pe.wait_ge(skip_ready.sem, skip_ready.at(i, 1))
                            mm(ps[:, 7, SEQ:2 * SEQ], g.ident[:, :], skip_y[:, :, :].rearrange("p t d -> p (t d)"),
                               start=True, stop=False)
                        pe.wait_ge(cxT_ready.sem, cxT_ready.at(i, j))
                        for pair in (2 * j - 2, 2 * j - 1):
                            for t in range(T):
                                last = mm(ps[:, 7, SEQ + t * P:SEQ + (t + 1) * P], cxT[:, pair, t * P:(t + 1) * P],
                                          at["wpost"][:, pair * P:(pair + 1) * P], start=False,
                                          stop=pair == PAIRS - 1 and t == T - 1)
                        if j == NG:
                            last.then_inc(out_ps.sem, 1)
                    yield

            pipeline3(pe, front, back, finish)


ATT8 = {
    0: [("wqk", 2 * P), ("wv", P), ("wo", P), ("vb", P), ("ob", P), ("qkb", 2)],
    1: [("wqk", 2 * P), ("wrot", 2 * P), ("wv", P), ("wo", P), ("ob", P), ("cos", 2 * SEQ), ("sin", 2 * SEQ)],
}


class Globals:
    pass


def expert_weights(nc, ctx, layer):
    sb = lambda name, shape: ctx.enter_context(nc.sbuf_tensor(f"e{layer}_{name}", shape, F32R))
    return {f"{k}_{part}": sb(f"{k}_{part}", shape) for part in ("hi", "lo")
            for k, shape in (("gu", [P, NE, 2 * F_EXP[layer]]), ("down", [P, NE, FC, P]))}


def program(nc, a, out_dram, only=None):
    g = Globals()
    with ExitStack() as ctx:
        def sb(name, shape, dt=F32):
            return ctx.enter_context(nc.sbuf_tensor(name, shape, dt))

        g.x = sb("x", [P, TILES, P])
        g.ident = sb("ident", [P, P])
        g.minus_half = sb("minus_half", [P, 8])
        g.plus_half = sb("plus_half", [P, 32])
        g.ones_rows = sb("ones_rows", [P, 1])
        g.spread, g.masks, g.pick = a["spread"], a["masks"], a["pick"]

        with nc.semaphore("x_loaded") as x_loaded, nc.Block() as block:
            @block.sync
            def _(sp):
                sp.dma_start(g.x[:, :, :], a["x"].rearrange("b (t p) d -> p (b t) d", p=P)).then_inc(x_loaded, 16)
                sp.dma_start(g.ident[:, :], a["ident"]).then_inc(x_loaded, 16)
                sp.dma_start(g.ones_rows[:, :], a["ones_rows"]).then_inc(x_loaded, 16)
                sp.wait_ge(x_loaded, 48)

            @block.vector
            def _(dve):
                nc.vector.memset(g.minus_half[:, :], -0.5)
                nc.vector.memset(g.plus_half[:, :], 0.5)

        n = 99 if only is None else only
        if n > 0:
            attention8(nc, g, 0, a["att0"])
        if n > 1:
            with ExitStack() as part:
                w = expert_weights(nc, part, 0)
                load_experts(nc, g, 0, a["gu0"], a["down0"], w)
                experts(nc, g, 0, a["moe0"], w)
        if n > 2:
            attention8(nc, g, 1, a["att1"])
        if n > 3:
            selected_ffn(nc, g, 1, a["ffn1"], a["experts1"])
        if n > 4:
            grouped_attention(nc, g, a["att2"])
        if n > 5:
            selected_ffn(nc, g, 2, a["ffn2"], a["experts2"])
        if n > 6:
            channel_attention(nc, g, a["att3"])
        if n > 7:
            with ExitStack() as part:
                w = expert_weights(nc, part, 3)
                load_experts(nc, g, 3, a["gu3"], a["down3"], w)
                experts(nc, g, 3, a["moe3"], w)

        with nc.semaphore("x_stored") as x_stored, nc.Block() as block:
            @block.sync
            def _(sp):
                sp.dma_start(out_dram.rearrange("b (t p) d -> p (b t) d", p=P), g.x[:, :, :]).then_inc(x_stored, 16)
                sp.wait_ge(x_stored, 16)


def packed(inputs):
    f32 = lambda k: np.asarray(inputs[k], np.float32)
    rows = lambda v: np.broadcast_to(v, (P, v.shape[-1]))
    cols = lambda v: v.reshape(-1, P).T
    a = {"x": f32("L0_attn_x"), "ident": np.eye(P, dtype=np.float32)}
    spread = np.zeros((P, 16, P), np.float32)
    ones = np.zeros((P, 1), np.float32)
    parts = [(0, (0, 16)), (4, (8,)), (8, (0, 8)), (12, (16,))]
    for first, places in parts:
        for blk in range(NG):
            for j in range(NG):
                for d in range(D8):
                    for at in places:
                        spread[(4 * j + blk) * D8 + d, first + blk, 32 * j + at + d] = 1.0
    for j in range(NG):
        ones[32 * j + ROWS, 0] = 1.0
    a["spread"], a["ones_rows"] = spread, ones
    pick = np.zeros((HG, 32, HG, D8 + 1), np.float32)
    for h in range(HG):
        pick[h, 0:D8 + 1, h] = np.eye(D8 + 1)
    a["pick"] = pick.reshape(P, HG * (D8 + 1))
    r = np.arange(P)
    m = np.where(r[None, :] > r[:, None], MASKED, 0.0)
    z = np.zeros((P, P))
    a["masks"] = np.stack([np.hstack(v) for v in ([m] * 4, [z, m, z, m], [m.T, z, m.T, z], [m.T] * 4)],
                          axis=1).astype(np.float32)
    a["att0"] = np.hstack([f32("L0_attn_qkv_w"), f32("L0_attn_out_w"), rows(f32("L0_attn_qkv_b")[2 * P:]),
                           rows(f32("L0_attn_out_b")), cols(f32("L0_attn_qkv_b")[:2 * P])])
    qkv1 = f32("L1_attn_w_qkv")
    theta = (1.0 / 10000.0 ** (np.arange(0, D8, 2, dtype=np.float32) / D8)).astype(np.float32)
    angles = np.outer(np.arange(SEQ, dtype=np.float32), theta).astype(np.float32).T
    sign = np.repeat(np.array([-1.0, 1.0], np.float32), D8 // 2)[:, None]
    cos = np.tile(np.cos(np.vstack([angles, angles])), (NH, 2)).astype(np.float32)
    sin = np.tile(sign * np.sin(np.vstack([angles, angles])), (NH, 2)).astype(np.float32)
    turned = qkv1[:, :2 * P].reshape(P, 2 * NH, 2, D8 // 2)[:, :, ::-1].reshape(P, 2 * P)
    a["att1"] = np.hstack([qkv1[:, :2 * P], turned, qkv1[:, 2 * P:], f32("L1_attn_w_out"), rows(f32("L1_attn_b_out")),
                           cos, sin])
    for k in (1, 2):
        c = lambda n: f32(f"L{k}_ffn_{n}")
        a[f"ffn{k}"] = np.hstack([c("Wp1"), cols(c("bp1")), c("Wp2"), rows(c("bp2")), c("Wo"), rows(c("bo"))])
        w2 = c("W2").reshape(NE, 2, P, P).transpose(0, 2, 1, 3).reshape(NE, P, 2 * P)
        a[f"experts{k}"] = np.concatenate([c("W1"), w2, c("b1").reshape(NE, 2, P).transpose(0, 2, 1),
                                           c("b2")[:, :, None]], axis=2)
    wk = f32("L2_attn_Wk").reshape(P, NG, 1, D64)
    post = f32("L2_attn_Wpost").reshape(NH // 2, P, P).transpose(1, 0, 2).reshape(P, NH * D64)
    spread_sums = np.zeros((P, NG, 2, 2, D64), np.float32)
    for j in range(NG):
        for h in range(HG):
            spread_sums[32 * h + j, j, h // 2, h % 2] = 1.0
    a["att2"] = np.hstack([f32("L2_attn_Wq"), np.broadcast_to(wk, (P, NG, 2, D64)).reshape(P, NG * P),
                           f32("L2_attn_Wv"), post, spread_sums.reshape(P, -1)])
    head = np.arange(P) // D8
    blocks = np.where(head[:, None] == head[None, :], 0.0, MASKED).astype(np.float32)
    a["att3"] = np.hstack([f32("L3_attn_Wq").T, f32("L3_attn_Wk").T, f32("L3_attn_Wv").T, f32("L3_attn_Wo").T, blocks])
    iota = rows(np.arange(NE, dtype=np.float32))
    t = lambda k: f32(k).T
    pad = lambda v, n: np.pad(v, [(0, n - v.shape[0])] + [(0, 0)] * (v.ndim - 1))
    gate0, up0, down0 = (np.concatenate([f32(f"L0_ffn_r{c}"), f32(f"L0_ffn_s{c}")[None]]) for c in "gud")
    a["gu0"] = np.concatenate([gate0.transpose(0, 2, 1), up0.transpose(0, 2, 1)], axis=2)
    a["down0"] = down0.transpose(0, 2, 1)
    logit_bias = np.full((NE,), MASKED, np.float32)
    logit_bias[:NE - 1] = f32("L0_ffn_rb")
    twice = lambda v: pad(np.concatenate([pad(v, 32), v]), P)
    pick_expert = twice(np.repeat(np.eye(NE, dtype=np.float32), P, axis=1))
    a["moe0"] = np.hstack([pad(f32("L0_ffn_wr"), NE).T, rows(logit_bias), iota, pick_expert])
    a["gu3"] = np.concatenate([f32("L3_ffn_Wg"), f32("L3_ffn_W1")], axis=2)
    a["down3"] = f32("L3_ffn_W2")

    def chunks(b):
        b = np.pad(b, ((0, 0), (0, FC * P - b.shape[1])))
        return b.reshape(NE * FC, P).T

    a["moe3"] = np.hstack([t("L3_ffn_centroid"), iota, pick_expert, chunks(f32("L3_ffn_bg")), chunks(f32("L3_ffn_b1")),
                           twice(f32("L3_ffn_b2"))])
    return a


def kernel(**inputs):
    import concourse.bacc as bacc
    from concourse.bass_utils import run_bass_kernel_spmd

    nc = bacc.Bacc("TRN2", target_bir_lowering=False, num_devices=1)
    a = {k: np.ascontiguousarray(v) for k, v in packed(inputs).items()}
    shape = (SEQS, SEQ, P)
    aps = {k: nc.dram_tensor(f"in_{k}", v.shape, mybir.dt.from_np(v.dtype), kind="ExternalInput").ap() for k, v in a.items()}
    out = nc.dram_tensor("out", shape, F32, kind="ExternalOutput").ap()
    program(nc, aps, out)
    r = run_bass_kernel_spmd(nc, [{f"in_{k}": v for k, v in a.items()}], core_ids=[0])
    return r.results[0]["out"]
```

```python
from contextlib import ExitStack

import numpy as np
import concourse.bass as bass
from concourse import mybir

F32 = mybir.dt.float32
F32R = mybir.dt.float32r
U32 = mybir.dt.uint32
BF16 = mybir.dt.bfloat16
ALU = mybir.AluOpType
ACT = mybir.ActivationFunctionType
AX = mybir.AxisListType.X

P = 128
SEQS = 8
SEQ = 256
T = SEQ // P
TILES = SEQS * T
NH = 16
NG = 4
HG = NH // NG
EPS = 1e-5
MASKED = -1e30
BANK = 512
D8 = 8
D64 = 64
ROWS = 24
NE = 8
F_EXP = {0: 352, 3: 342}
FC = 3
RT = 4
RUN = RT * P
RUNS = TILES // RT
DEPTH = 2


class Signal:

    def __init__(self, sem, per):
        self.sem, self.per = sem, per

    def credit(self, eng):
        eng.sem_inc(self.sem, DEPTH * self.per)

    def at(self, i, c, back=0):
        assert 1 <= c <= self.per and 0 <= back <= DEPTH
        return i * self.per + ((DEPTH - back) * self.per + c)


def own_wait(eng, sem):
    eng.sem_inc(sem, 1)


class Chain:

    def __init__(self, sem, per):
        self.sem, self.sig, self.per, self.n = sem, Signal(sem, per), per, 0

    def begin(self, i):
        self.i, self.n = i, 0

    def next(self):
        self.n += 1
        return self.sem

    def so_far(self):
        return self.sig.at(self.i, self.n)

    def end(self):
        assert self.n == self.per, f"{self.n} signals, not {self.per}"


def merge(*parts):
    parts = list(parts)
    while parts:
        for part in list(parts):
            if next(part, "end") == "end":
                parts.remove(part)


def skip(n):
    for _ in range(n):
        yield


def issue(part):
    for _ in part:
        pass


def pipeline(eng, front, back):
    issue(front(0, 0))
    with eng.Fori(0, (SEQS - 2) // 2) as t:
        merge(back(t * 2, 0), front(t * 2 + 1, 1))
        merge(back(t * 2 + 1, 1), front(t * 2 + 2, 0))
    merge(back(SEQS - 2, 0), front(SEQS - 1, 1))
    issue(back(SEQS - 1, 1))


def pipeline3(eng, front, back, finish):
    issue(front(0, 0))
    merge(back(0, 0), front(1, 1))
    with eng.Fori(0, (SEQS - 2) // 2) as t:
        merge(finish(t * 2), back(t * 2 + 1, 1), front(t * 2 + 2, 0))
        merge(finish(t * 2 + 1), back(t * 2 + 2, 0), front(t * 2 + 3, 1))
    merge(finish(SEQS - 2), back(SEQS - 1, 1))
    issue(finish(SEQS - 1))


def pipeline_early(eng, early, front, back, finish):
    issue(early(0, 0))
    merge(front(0, 0), early(1, 1))
    merge(back(0, 0), front(1, 1), early(2, 0))
    with eng.Fori(0, (SEQS - 4) // 2) as t:
        merge(finish(t * 2), back(t * 2 + 1, 1), front(t * 2 + 2, 0), early(t * 2 + 3, 1))
        merge(finish(t * 2 + 1), back(t * 2 + 2, 0), front(t * 2 + 3, 1), early(t * 2 + 4, 0))
    merge(finish(SEQS - 4), back(SEQS - 3, 1), front(SEQS - 2, 0), early(SEQS - 1, 1))
    merge(finish(SEQS - 3), back(SEQS - 2, 0), front(SEQS - 1, 1))
    merge(finish(SEQS - 2), back(SEQS - 1, 1))
    issue(finish(SEQS - 1))


def nothing(*_):
    return iter(())


class Stage:

    def __init__(self, nc, ctx, name):
        self.nc, self.ctx, self.name = nc, ctx, name
        self.sems = []
        ctx.callback(self.release)
        self.dve_waited, self.sp_waited = self.sem("dve_waited"), self.sem("sp_waited")
        self.ps = ctx.enter_context(nc.psum_tensor(f"{name}_banks", [P, 8, BANK], F32))

    def sb(self, name, shape, dt=F32):
        return self.ctx.enter_context(self.nc.sbuf_tensor(f"{self.name}_{name}", shape, dt))

    def sem(self, name):
        self.sems.append(self.nc.alloc_semaphore(name=f"{self.name}_{name}"))
        return self.sems[-1]

    def release(self):
        self.nc.clear_and_free_semaphores(self.sems)
        self.nc.all_engine_barrier()

    def sig(self, name, per):
        return Signal(self.sem(name), per)



class Norm:

    def __init__(self, st, name, n):
        self.n = n
        self.waited = st.dve_waited
        self.stats = st.sb(f"{name}_stats", [P, n, 6])
        self.mean_var = st.sb(f"{name}_mean_var", [P, n, 2])
        self.var = st.sb(f"{name}_var", [P, n])
        self.rstd = st.sb(f"{name}_rstd", [P, n])
        self.var_ready = st.sig(f"{name}_var_ready", 1)
        self.rstd_ready = st.sig(f"{name}_rstd_ready", 1)

    CHAIN = 2

    def moments(self, nc, dve, chain, src):
        for j in range(self.n):
            last = nc.vector.bn_stats(self.stats[:, j, :], src(j))
        last.then_inc(chain.next(), 1)
        dve.wait_ge(chain.sem, chain.so_far())
        own_wait(dve, self.waited)
        for j in range(self.n):
            last = nc.vector.bn_aggr(self.mean_var[:, j, :], self.stats[:, j, :])
        last.then_inc(chain.next(), 1)
        dve.wait_ge(chain.sem, chain.so_far())
        nc.vector.tensor_scalar(self.var[:, :], self.mean_var[:, :, 1], EPS, None, ALU.add).then_inc(
            self.var_ready.sem, 1)

    def power(self, nc, pool, i, minus_half):
        pool.wait_ge(self.var_ready.sem, self.var_ready.at(i, 1))
        nc.gpsimd.tensor_tensor(self.rstd[:, :], self.var[:, :], minus_half[:, 0:self.n], ALU.pow).then_inc(
            self.rstd_ready.sem, 1)

    def apply(self, nc, j, out, src):
        return nc.vector.tensor_scalar(out, src, self.mean_var[:, j, 0:1], self.rstd[:, j:j + 1],
                                       ALU.subtract, ALU.mult)


def add_normed(nc, dve, chain, norm, i, x, tile0, f):
    dve.wait_ge(norm.rstd_ready.sem, norm.rstd_ready.at(i, 1))
    for j in range(norm.n):
        last = norm.apply(nc, j, f[:, j, :], f[:, j, :])
    last.then_inc(chain.next(), 1)
    dve.wait_ge(chain.sem, chain.so_far())
    for j in range(norm.n):
        last = nc.vector.tensor_tensor(x[:, tile0 + j, :], x[:, tile0 + j, :], f[:, j, :], ALU.add)
    last.then_inc(chain.next(), 1)



def attention8(nc, g, layer, key, prefetch=None):
    causal, rope = layer == 0, layer == 1
    FILLS = 3 if causal else 4
    SCALE = float(D8) ** -0.5
    DV = D8 + 1
    COLS = 32
    x = g.x
    with ExitStack() as ctx:
        st = Stage(nc, ctx, f"a{layer}")
        ps = st.ps
        at = columns(g.w[key], ATT8[layer])
        spread = st.sb("spread", [P, 16, P], F32R)
        if causal:
            masks = st.sb("masks", [P, 4, BANK], BF16)
            ident16 = st.sb("ident16", [P, P], BF16)
        y = st.sb("y", [P, T, P])
        f = st.sb("f", [P, T, P])
        yT = st.sb("yT", [P, SEQ])
        qk = st.sb("qk", [P, 2 * SEQ])
        rot = st.sb("rot", [P, 2 * SEQ])
        hi = st.sb("hi", [P, 2 * SEQ], F32R)
        lo = st.sb("lo", [P, 2 * SEQ], F32R)
        QT = [st.sb(f"QT{k}", [P, NG, SEQ], F32R) for k in range(2)]
        KT = [st.sb(f"KT{k}", [P, NG, SEQ], F32R) for k in range(2)]
        V = [st.sb(f"V{k}", [P, T, NH, COLS]) for k in range(2)]
        raw = [st.sb(f"raw{k}", [P, SEQ]) for k in range(2)]
        pick = g.pick
        rowmax = st.sb("rowmax", [P, T, NH])
        mrow = [[st.sb(f"mrow{k}{j}", [NG, SEQ], F32R) for j in range(NG)] for k in range(2)]
        probs = [st.sb(f"probs{k}", [P, FILLS, BANK]) for k in range(2)]
        recip = st.sb("recip", [P, T, NH])
        cx = st.sb("cx", [P, T, P])
        cxT = st.sb("cxT", [P, SEQ])
        norm_in, norm_out = Norm(st, "in", T), Norm(st, "out", T)

        loaded = g.loaded[key]
        constants = st.sem("constants_ready")
        spread_ready = st.sem("spread_ready")
        y_ready, yT_ps, yT_ready = st.sig("y_ready", 1), st.sig("yT_ps", 1), st.sig("yT_ready", 1)
        qk_ps, rot_ps, qk_ready = st.sig("qk_ps", 1), st.sig("rot_ps", 1), st.sig("qk_ready", 1)
        hi_ready, lo_ready = st.sig("hi_ready", 1), st.sig("lo_ready", 1)
        v_ps, v_ready = st.sig("v_ps", 1), st.sig("v_ready", 1)
        stack_ps, stack_ready = st.sig("stack_ps", 4), st.sig("stack_ready", 4)
        score_ps, rowmax_ready = st.sig("score_ps", NG * FILLS), st.sig("rowmax_ready", NG * FILLS)
        max_ps, mrow_ready = st.sig("max_ps", NG), st.sig("mrow_ready", NG)
        mrow_placed = [st.sem(f"mrow_placed{j}") for j in range(NG)]
        sT_ps, exp_done = st.sig("sT_ps", NG * FILLS), st.sig("exp_done", NG * FILLS)
        pv_done, raw_ready, picked = st.sig("pv_done", NG), st.sig("raw_ready", NG), st.sig("picked", NG)
        cx_ready = st.sig("cx_ready", 1)
        cxT_ps, cxT_ready = st.sig("cxT_ps", 1), st.sig("cxT_ready", 1)
        out_ps, f_ready = st.sig("out_ps", 1), st.sig("f_ready", 1)
        cos_ready = st.sig("cos_ready", 1)
        early_chain = Chain(st.sem("dve_early"), Norm.CHAIN + (1 if rope else 0))
        back_chain = Chain(st.sem("dve_back"), Norm.CHAIN + 3)

        Q_HI, Q_LO, K_HI, K_LO = (4 * k for k in range(4))
        MOMENTS, POWER, APPLY, TRANSPOSE, TO_SBUF, QK, QK_READ, ROT, ROT_READ, HI, LO = (
            (7, 8, 9, 10, 10, 11, 12, 13, 13, 14, 15) if causal else tuple(range(7, 18)))
        HEAD = 3
        GROUPS = (NG + 1) * FILLS
        block = ctx.enter_context(nc.Block())

        @block.sync
        def _(sp):
            if prefetch:
                prefetch(sp)

            def front(i, p):
                yield from skip(HEAD + FILLS + 2)
                for j in range(NG):
                    sp.wait_ge(mrow_ready.sem, mrow_ready.at(i, j + 1))
                    sp.dma_start(QT[p][32 * j + ROWS:32 * j + ROWS + 1, :, :].bitcast(F32),
                                 mrow[p][j][:, :].bitcast(F32)).then_inc(
                        mrow_placed[j], 16)
                    yield from skip(FILLS)

            pipeline_early(sp, nothing, front, nothing, nothing)

        @block.gpsimd
        def _(pool):
            norm_in.rstd_ready.credit(pool)
            norm_out.rstd_ready.credit(pool)

            def early(i, p):
                yield from skip(POWER)
                norm_in.power(nc, pool, i, g.minus_half)
                yield

            def finish(i):
                yield from skip(5)
                norm_out.power(nc, pool, i, g.minus_half)
                yield

            pipeline_early(pool, early, nothing, nothing, finish)

        @block.vector
        def _(dve):
            for s in (norm_in.var_ready, norm_out.var_ready, y_ready, qk_ready, lo_ready, v_ready,
                      rowmax_ready, cx_ready, f_ready, cos_ready, early_chain.sig, back_chain.sig):
                s.credit(dve)
            dve.wait_ge(g.loaded["shared"], 48)
            if causal:
                nc.vector.tensor_copy(masks[:, :, :], g.masks[:, :, :])
                nc.vector.tensor_copy(ident16[:, :], g.ident[:, :])
            nc.vector.tensor_copy(spread[:, :, :], g.spread[:, :, :]).then_inc(spread_ready, 1)
            for k in range(2):
                nc.vector.memset(V[k][:, :, :, DV:COLS], 0.0)
                nc.vector.memset(V[k][:, :, :, D8:DV], 1.0).then_inc(constants, 1)
            dve.wait_ge(constants, 2)
            dve.wait_ge(loaded, 16)

            def early(i, p):
                early_chain.begin(i)
                yield from skip(MOMENTS)
                norm_in.moments(nc, dve, early_chain, lambda j: x[:, i * T + j, :])
                yield from skip(APPLY - MOMENTS)
                dve.wait_ge(norm_in.rstd_ready.sem, norm_in.rstd_ready.at(i, 1))
                dve.wait_ge(yT_ps.sem, yT_ps.at(i, 1, 1))
                for j in range(T):
                    last = norm_in.apply(nc, j, y[:, j, :], x[:, i * T + j, :])
                last.then_inc(y_ready.sem, 1)
                yield from skip(QK_READ - APPLY)
                dve.wait_ge(qk_ps.sem, qk_ps.at(i, 1))
                dve.wait_ge(hi_ready.sem, hi_ready.at(i, 1, 1))
                if rope:
                    nc.vector.tensor_tensor(qk[:, :], ps[:, 1, :], at["cos"], ALU.mult).then_inc(cos_ready.sem, 1)
                else:
                    for k in range(2):
                        last = nc.vector.tensor_scalar(qk[:, k * SEQ:(k + 1) * SEQ], ps[:, 1, k * SEQ:(k + 1) * SEQ],
                                                       at["qkb"][:, k:k + 1], None, ALU.add)
                    last.then_inc(qk_ready.sem, 1)
                yield from skip(ROT_READ - QK_READ)
                if rope:
                    dve.wait_ge(rot_ps.sem, rot_ps.at(i, 1))
                    nc.vector.tensor_tensor(rot[:, :], ps[:, 1, :], at["sin"], ALU.mult).then_inc(early_chain.next(), 1)
                    dve.wait_ge(early_chain.sem, early_chain.so_far())
                    dve.wait_ge(cos_ready.sem, cos_ready.at(i, 1))
                    nc.vector.tensor_tensor(qk[:, :], qk[:, :], rot[:, :], ALU.add).then_inc(qk_ready.sem, 1)
                yield from skip(LO - ROT_READ)
                dve.wait_ge(hi_ready.sem, hi_ready.at(i, 1))
                dve.wait_ge(qk_ready.sem, qk_ready.at(i, 1))
                nc.vector.tensor_tensor(lo[:, :], qk[:, :], hi[:, :].bitcast(F32), ALU.subtract).then_inc(
                    lo_ready.sem, 1)
                early_chain.end()

            def front(i, p):
                dve.wait_ge(v_ps.sem, v_ps.at(i, 1))
                v_bank = ps[:, 0 if causal else 1, 0:SEQ].rearrange("p (t h d) -> p t h d", t=T, h=NH)
                dve.wait_ge(pv_done.sem, pv_done.at(i, NG, 2))
                for t in range(T):
                    if causal:
                        last = nc.vector.tensor_tensor(V[p][:, t, :, 0:D8], v_bank[:, t],
                                                       at["vb"].rearrange("p (h d) -> p h d", h=NH), ALU.add)
                    else:
                        last = nc.vector.tensor_copy(V[p][:, t, :, 0:D8], v_bank[:, t])
                last.then_inc(v_ready.sem, 1)
                yield from skip(HEAD)
                for j in range(NG):
                    if j == 0:
                        dve.wait_ge(max_ps.sem, max_ps.at(i, NG, 1))
                    for n in range(FILLS):
                        c = j * FILLS + n
                        dve.wait_ge(score_ps.sem, score_ps.at(i, c + 1))
                        bank = ps[:, 2 + c % 2, :]
                        if causal and n == 0:
                            o, src = rowmax[:, 0, 4 * j:4 * j + 4], bank.rearrange("p (h k) -> p h k", h=4)
                        else:
                            t, h = (1, 4 * j + 2 * (n - 1)) if causal else (n // 2, 4 * j + 2 * (n % 2))
                            o, src = rowmax[:, t, h:h + 2], bank.rearrange("p (h k) -> p h k", h=2)
                        nc.vector.reduce_max(o, src, AX).then_inc(rowmax_ready.sem, 1)
                        yield

            def finish(i):
                back_chain.begin(i)
                yield
                dve.wait_ge(picked.sem, picked.at(i, NG))
                c = ps[:, 7, 0:T * NH * DV].rearrange("p (t h d) -> p t h d", t=T, h=NH)
                nc.vector.reciprocal(recip[:, :, :], c[:, :, :, D8]).then_inc(back_chain.next(), 1)
                dve.wait_ge(back_chain.sem, back_chain.so_far())
                for t in range(T):
                    last = nc.vector.tensor_tensor(cx[:, t, :].rearrange("p (h d) -> p h d", h=NH), c[:, t, :, 0:D8],
                                                   recip[:, t, :].rearrange("p (h o) -> p h o", o=1).to_broadcast([P, NH, D8]), ALU.mult)
                last.then_inc(cx_ready.sem, 1)
                yield from skip(3)
                dve.wait_ge(out_ps.sem, out_ps.at(i, 1))
                for t in range(T):
                    last = nc.vector.tensor_tensor(f[:, t, :], ps[:, 6, SEQ + t * P:SEQ + (t + 1) * P], at["ob"], ALU.add)
                last.then_inc(f_ready.sem, 1)
                dve.wait_ge(f_ready.sem, f_ready.at(i, 1))
                norm_out.moments(nc, dve, back_chain, lambda j: f[:, j, :])
                yield
                yield
                add_normed(nc, dve, back_chain, norm_out, i, x, i * T, f)
                dve.wait_ge(back_chain.sem, back_chain.so_far())
                back_chain.end()

            pipeline_early(dve, early, front, nothing, finish)

        @block.scalar
        def _(act):
            nc.scalar.preload_act_table(ACT.Exp)
            for s in (yT_ready, hi_ready, stack_ready, mrow_ready, exp_done, raw_ready, cxT_ready):
                s.credit(act)

            def early(i, p):
                yield from skip(TO_SBUF)
                act.wait_ge(yT_ps.sem, yT_ps.at(i, 1))
                act.wait_ge(v_ps.sem, v_ps.at(i, 1, 1))
                nc.scalar.activation(yT[:, :], ps[:, 1, 0:SEQ], ACT.Copy).then_inc(yT_ready.sem, 1)
                yield from skip(HI - TO_SBUF)
                act.wait_ge(qk_ready.sem, qk_ready.at(i, 1))
                act.wait_ge(stack_ps.sem, stack_ps.at(i, 4, 1))
                nc.scalar.activation(hi[:, :], qk[:, :], ACT.Copy).then_inc(hi_ready.sem, 1)
                yield

            def front(i, p):
                yield
                act.wait_ge(sT_ps.sem, sT_ps.at(i, NG * FILLS, 2))
                for n in range(4):
                    act.wait_ge(stack_ps.sem, stack_ps.at(i, n + 1))
                    bank = ps[:, (1 if causal else 0) + (n % 2) * (-1 if causal else 1), :].rearrange(
                        "p (g t) -> p g t", g=2)
                    g2 = 2 * (n % 2)
                    if n < 2:
                        nc.scalar.activation(QT[p][:, g2:g2 + 2, :], bank, ACT.Copy).then_inc(stack_ready.sem, 1)
                    else:
                        nc.scalar.activation(KT[p][:, g2:g2 + 2, :], bank, ACT.Identity,
                                             bias=g.ones_rows[:, :]).then_inc(stack_ready.sem, 1)
                    if n % 2 == 1:
                        yield
                yield from skip(2)
                for j in range(NG):
                    yield from skip(FILLS)
                    act.wait_ge(max_ps.sem, max_ps.at(i, j + 1))
                    nc.scalar.activation(mrow[p][j][:, :], ps[0:NG, 0, 0:SEQ], ACT.Copy, scale=-1.0).then_inc(
                        mrow_ready.sem, 1)

            def to_sbuf(i, m):
                act.wait_ge(pv_done.sem, pv_done.at(i, m + 1))
                if m < 2:
                    act.wait_ge(picked.sem, picked.at(i, m + 3, 1))
                else:
                    act.wait_ge(picked.sem, picked.at(i, m - 1))
                nc.scalar.activation(raw[m % 2][:, :], ps[:, 6, 0:SEQ], ACT.Copy).then_inc(raw_ready.sem, 1)

            def back(i, p):
                for j in range(NG):
                    if j < 2:
                        act.wait_ge(pv_done.sem, pv_done.at(i, j + 3, 1))
                    else:
                        act.wait_ge(pv_done.sem, pv_done.at(i, j - 1))
                    for n in range(FILLS):
                        c = j * FILLS + n
                        act.wait_ge(sT_ps.sem, sT_ps.at(i, c + 1))
                        nc.scalar.activation(probs[j % 2][:, n, :], ps[:, 4 + c % 2, :], ACT.Exp,
                                             scale=SCALE).then_inc(exp_done.sem, 1)
                        if j > 0 and n == FILLS - 1:
                            to_sbuf(i, j - 1)
                        yield
                yield from skip(FILLS - 1)
                to_sbuf(i, NG - 1)
                yield

            def finish(i):
                yield from skip(3)
                act.wait_ge(cxT_ps.sem, cxT_ps.at(i, 1))
                nc.scalar.activation(cxT[:, :], ps[:, 6, 0:SEQ], ACT.Copy).then_inc(cxT_ready.sem, 1)
                yield

            pipeline_early(act, early, front, back, finish)

        @block.tensor
        def _(pe):
            mm = nc.tensor.matmul
            for s in (yT_ps, qk_ps, rot_ps, v_ps, stack_ps, score_ps, max_ps, sT_ps, pv_done, picked, cxT_ps, out_ps):
                s.credit(pe)
            pe.wait_ge(loaded, 16)
            pe.wait_ge(g.loaded["shared"], 48)
            pe.wait_ge(spread_ready, 1)
            pe.wait_ge(constants, 2)

            def early(i, p):
                yield from skip(TRANSPOSE)
                pe.wait_ge(y_ready.sem, y_ready.at(i, 1))
                pe.wait_ge(stack_ready.sem, stack_ready.at(i, 4, 1))
                for t in range(T):
                    last = nc.tensor.transpose(ps[:, 1, t * P:(t + 1) * P], y[:, t, :], g.ident[:, :])
                last.then_inc(yT_ps.sem, 1)
                yield from skip(QK - TRANSPOSE)
                pe.wait_ge(yT_ready.sem, yT_ready.at(i, 1))
                for k in range(2):
                    last = mm(ps[:, 1, k * SEQ:(k + 1) * SEQ], at["wqk"][:, k * P:(k + 1) * P], yT[:, :],
                              start=True, stop=True)
                last.then_inc(qk_ps.sem, 1)
                yield from skip(ROT - QK)
                if rope:
                    pe.wait_ge(cos_ready.sem, cos_ready.at(i, 1))
                    for k in range(2):
                        last = mm(ps[:, 1, k * SEQ:(k + 1) * SEQ], at["wrot"][:, k * P:(k + 1) * P], yT[:, :],
                                  start=True, stop=True)
                    last.then_inc(rot_ps.sem, 1)
                yield

            def front(i, p):
                pe.wait_ge(yT_ready.sem, yT_ready.at(i, 1))
                pe.wait_ge(mrow_ready.sem, mrow_ready.at(i, NG, 1))
                pe.wait_ge(qk_ready.sem, qk_ready.at(i, 1))
                vb = 0 if causal else 1
                for t in range(T):
                    last = mm(ps[:, vb, t * P:(t + 1) * P], yT[:, t * P:(t + 1) * P], at["wv"], start=True, stop=True)
                last.then_inc(v_ps.sem, 1)
                yield
                pe.wait_ge(hi_ready.sem, hi_ready.at(i, 1))
                pe.wait_ge(lo_ready.sem, lo_ready.at(i, 1))
                for n in range(4):
                    if n == 1:
                        pe.wait_ge(v_ready.sem, v_ready.at(i, 1))
                    elif n > 1:
                        pe.wait_ge(stack_ready.sem, stack_ready.at(i, n - 1))
                    bank = (1 if causal else 0) + (n % 2) * (-1 if causal else 1)
                    k, m_hi, m_lo = n // 2, (Q_HI, K_HI)[n // 2], (Q_LO, K_LO)[n // 2]
                    for gg in range(2):
                        blk = 2 * (n % 2) + gg
                        o = ps[:, bank, gg * SEQ:(gg + 1) * SEQ]
                        mm(o, spread[:, m_hi + blk, :], hi[:, k * SEQ:(k + 1) * SEQ], start=True, stop=False)
                        last = mm(o, spread[:, m_lo + blk, :], lo[:, k * SEQ:(k + 1) * SEQ], start=False, stop=True)
                    last.then_inc(stack_ps.sem, 1)
                    if n % 2 == 1:
                        yield
                pe.wait_ge(stack_ready.sem, stack_ready.at(i, 4))
                for j in range(NG + 1):
                    rows = slice(32 * j, 32 * j + ROWS)
                    for n in range(FILLS):
                        if j < NG:
                            c = j * FILLS + n
                            if c < 2:
                                pe.wait_ge(rowmax_ready.sem, rowmax_ready.at(i, NG * FILLS - 1 + c, 1))
                            else:
                                pe.wait_ge(rowmax_ready.sem, rowmax_ready.at(i, c - 1))
                            bank = ps[:, 2 + c % 2, :]
                            if causal:
                                mm(bank, ident16[:, :], masks[:, 0 if n == 0 else 1, :], start=True, stop=False)
                            if causal and n == 0:
                                for h in range(4):
                                    last = mm(bank[:, h * P:(h + 1) * P], QT[p][rows, h, 0:P], KT[p][rows, h, 0:P],
                                              start=False, stop=h == 3)
                            else:
                                t, h0 = (1, 2 * (n - 1)) if causal else (n // 2, 2 * (n % 2))
                                for h in range(2):
                                    last = mm(bank[:, h * SEQ:(h + 1) * SEQ], QT[p][rows, h0 + h, t * P:(t + 1) * P],
                                              KT[p][rows, h0 + h, :], start=not causal, stop=(not causal) or h == 1)
                            last.then_inc(score_ps.sem, 1)
                        if j > 0 and n == 1:
                            m = j - 1
                            pe.wait_ge(rowmax_ready.sem, rowmax_ready.at(i, j * FILLS))
                            if m >= 1:
                                pe.wait_ge(mrow_ready.sem, mrow_ready.at(i, m))
                            for t in range(T):
                                last = nc.tensor.transpose(ps[0:NG, 0, t * P:(t + 1) * P],
                                                           rowmax[:, t, 4 * m:4 * m + 4], g.ident[:, :])
                            last.then_inc(max_ps.sem, 1)
                        yield

            def transpose_group(i, m):
                pe.wait_ge(raw_ready.sem, raw_ready.at(i, m + 1))
                if m == 0:
                    pe.wait_ge(cx_ready.sem, cx_ready.at(i, 1, 1))
                for t in range(T):
                    o = (t * NH + HG * m) * DV
                    last = mm(ps[:, 7, o:o + HG * DV], raw[m % 2][:, t * P:(t + 1) * P], pick[:, :], start=True, stop=True)
                last.then_inc(picked.sem, 1)

            def values(i, p, m, kt):
                if kt == 0:
                    pe.wait_ge(exp_done.sem, exp_done.at(i, (m + 1) * FILLS))
                    if m == 0:
                        pe.wait_ge(f_ready.sem, f_ready.at(i, 1, 1))
                    else:
                        pe.wait_ge(raw_ready.sem, raw_ready.at(i, m))
                for h in range(HG):
                    o = ps[h * COLS:(h + 1) * COLS, 6, :]
                    v = V[p][:, kt, HG * m + h, :]
                    if causal and kt == 1:
                        last = mm(o[:, P:SEQ], v, probs[m % 2][:, 2, h * P:(h + 1) * P], start=False, stop=True)
                    else:
                        last = mm(o[:, 0:SEQ], v, probs[m % 2][:, 2 * kt + h // 2, (h % 2) * SEQ:(h % 2 + 1) * SEQ],
                                  start=kt == 0, stop=kt == T - 1)
                if kt == T - 1:
                    last.then_inc(pv_done.sem, 1)

            def back(i, p):
                for j in range(NG + 1):
                    rows = slice(32 * j, 32 * j + ROWS + 1)
                    for n in range(FILLS):
                        if j < NG:
                            if n == 0:
                                pe.wait_ge(mrow_placed[j], i * 16 + 16)
                            c = j * FILLS + n
                            if c < 2:
                                pe.wait_ge(exp_done.sem, exp_done.at(i, NG * FILLS - 1 + c, 1))
                            else:
                                pe.wait_ge(exp_done.sem, exp_done.at(i, c - 1))
                            bank = ps[:, 4 + c % 2, :]
                            if causal:
                                mm(bank, ident16[:, :], masks[:, 3 if n == 2 else 2, :], start=True, stop=False)
                            if causal and n == 2:
                                for h in range(4):
                                    last = mm(bank[:, h * P:(h + 1) * P], KT[p][rows, h, P:SEQ], QT[p][rows, h, P:SEQ],
                                              start=False, stop=h == 3)
                            else:
                                t, h0 = n // 2, 2 * (n % 2)
                                for h in range(2):
                                    last = mm(bank[:, h * SEQ:(h + 1) * SEQ], KT[p][rows, h0 + h, t * P:(t + 1) * P],
                                              QT[p][rows, h0 + h, :], start=not causal, stop=(not causal) or h == 1)
                            last.then_inc(sT_ps.sem, 1)
                        if n == 0 and j > 1:
                            transpose_group(i, j - 2)
                        if j > 0 and 1 <= n <= T:
                            values(i, p, j - 1, n - 1)
                        yield

            def finish(i):
                yield
                transpose_group(i, NG - 1)
                yield
                pe.wait_ge(cx_ready.sem, cx_ready.at(i, 1))
                for t in range(T):
                    last = nc.tensor.transpose(ps[:, 6, t * P:(t + 1) * P], cx[:, t, :], g.ident[:, :])
                last.then_inc(cxT_ps.sem, 1)
                yield from skip(2)
                pe.wait_ge(cxT_ready.sem, cxT_ready.at(i, 1))
                for t in range(T):
                    last = mm(ps[:, 6, SEQ + t * P:SEQ + (t + 1) * P], cxT[:, t * P:(t + 1) * P], at["wo"],
                              start=True, stop=True)
                last.then_inc(out_ps.sem, 1)
                yield

            pipeline_early(pe, early, front, back, finish)



def load_experts(eng, layer, src_gu, src_down, raw):
    last_rows = F_EXP[layer] - (FC - 1) * P
    eng.dma_start(raw["gu"][:, :, :], src_gu.rearrange("e p f -> p e f")).then_inc(raw["loaded"], 16)
    for c in range(FC):
        r = P if c < FC - 1 else last_rows
        eng.dma_start(raw["down"][0:r, :, c, :],
                      src_down[:, c * P:c * P + r, :].rearrange("e p d -> p e d")).then_inc(raw["loaded"], 16)


def split_experts(nc, g, layer, raw, w):
    last_rows = F_EXP[layer] - (FC - 1) * P
    with ExitStack() as ctx:
        st = Stage(nc, ctx, f"w{layer}")
        hi_ready = st.sig("hi_ready", 1)
        block = ctx.enter_context(nc.Block())

        def parts(e):
            yield raw["gu"][:, e, :], w["gu_hi"][:, e, :], w["gu_lo"][:, e, :]
            for rows, c in ((slice(0, P), slice(0, FC - 1)), (slice(0, last_rows), slice(FC - 1, FC))):
                yield raw["down"][rows, e, c, :], w["down_hi"][rows, e, c, :], w["down_lo"][rows, e, c, :]

        @block.scalar
        def _(act):
            hi_ready.credit(act)
            act.wait_ge(raw["loaded"], 16 + 16 * FC)
            with act.Fori(0, NE) as e:
                for r, hi, lo in parts(e):
                    last = nc.scalar.activation(hi, r, ACT.Copy)
                last.then_inc(hi_ready.sem, 1)

        @block.vector
        def _(dve):
            with dve.Fori(0, NE) as e:
                dve.wait_ge(hi_ready.sem, hi_ready.at(e, 1))
                for r, hi, lo in parts(e):
                    nc.vector.tensor_tensor(lo, r, hi.bitcast(F32), ALU.subtract)


MOE = {
    0: [("router", NE), ("logit_bias", NE), ("iota", NE), ("pick_expert", NE * P)],
    3: [("router", NE), ("iota", NE), ("pick_expert", NE * P), ("gate_b", NE * FC), ("up_b", NE * FC), ("down_b", P)],
}


def experts(nc, g, layer, key, w):
    width = F_EXP[layer]
    by_distance = layer == 3
    rows_of = [P, P, width - 2 * P]
    N = NE * FC
    RING = 4
    LOW = 32
    WROWS = LOW + NE
    x = g.x
    with ExitStack() as ctx:
        st = Stage(nc, ctx, f"m{layer}")
        ps = st.ps
        wb = g.w[key]
        at = columns(wb, MOE[layer])
        y = st.sb("y", [P, RT, P])
        yT = st.sb("yT", [P, RUN])
        y_hi, y_lo = st.sb("y_hi", [P, RUN], F32R), st.sb("y_lo", [P, RUN], F32R)
        gate = [st.sb(f"gate{k}", [P, RUN]) for k in range(2)]
        gated = [st.sb(f"gated{k}", [P, RUN]) for k in range(2)]
        weights = [st.sb(f"weights{k}", [P, RUN]) for k in range(2)]
        h = [st.sb(f"h{k}", [P, RUN]) for k in range(2)]
        h_hi = st.sb("h_hi", [P, RING, RUN], F32R)
        h_lo = st.sb("h_lo", [P, RING, RUN], F32R)
        accT = st.sb("accT", [P, RUN])
        f = st.sb("f", [P, RT, P])
        score = st.sb("score", [P, RT, NE])
        top = st.sb("top", [P, RT, 8])
        top_at = st.sb("top_at", [P, RT, 8], U32)
        top_atf = st.sb("top_atf", [P, RT, 2])
        gap, th = st.sb("gap", [P, RT]), st.sb("th", [P, RT])
        share = st.sb("share", [P, RT, 2])
        one_hot = st.sb("one_hot", [P, RT, 2, NE])
        we = st.sb("we", [P, RT, NE])
        we_parts = st.sb("we_parts", [P, RT, WROWS])
        we_hi = st.sb("we_hi", [P, RT, NE], F32R)
        weT = st.sb("weT", [WROWS, RUN], F32R)
        pick_expert = st.sb("pick_expert", [WROWS, NE * P], F32R)
        norm_in, norm_out = Norm(st, "in", RT), Norm(st, "out", RT)
        best = top
        if by_distance:
            down_b_hi, down_b_lo = st.sb("down_b_hi", [WROWS, P], F32R), st.sb("down_b_lo", [WROWS, P], F32R)
            dist = best = st.sb("dist", [P, RT, 2])
            sq_y = st.sb("sq_y", [P, RT])
            square = st.sb("square", [P, RT, P])
            ones = st.sb("ones", [P, P])
            c2 = st.sb("c2", [P, 3 * NE])
            sq_ready, d2_ready, dist_ready = (st.sig("sq_ready", 1), st.sig("d2_ready", 1), st.sig("dist_ready", 1))
            c2_sq, c2_ps, ones_ready = st.sem("c2_sq"), st.sem("c2_ps"), st.sem("ones_ready")
        loaded, constants = g.loaded[key], st.sem("constants_ready")
        y_ready, yT_ps, yT_ready = st.sig("y_ready", 1), st.sig("yT_ps", 1), st.sig("yT_ready", 1)
        y_hi_ready, y_lo_ready = st.sig("y_hi_ready", 1), st.sig("y_lo_ready", 1)
        router_ps, gap_ready, th_ready = st.sig("router_ps", 1), st.sig("gap_ready", 1), st.sig("th_ready", 1)
        we_ready, weT_ps, weT_ready = st.sig("we_ready", 1), st.sig("weT_ps", 1), st.sig("weT_ready", 1)
        weights_ps, weights_ready = st.sig("weights_ps", NE), st.sig("weights_ready", NE)
        gate_ps, up_ps = st.sig("gate_ps", N), st.sig("up_ps", N)
        silu_done, gated_done, h_done = st.sig("silu_done", N), st.sig("gated_done", N), st.sig("h_done", N)
        hi_done, lo_done, down_done = st.sig("h_hi_done", N), st.sig("h_lo_done", N), st.sig("down_done", N)
        accT_ready, f_ps, f_ready = st.sig("accT_ready", 1), st.sig("f_ps", 1), st.sig("f_ready", 1)
        front_chain = Chain(st.sem("dve_front"), Norm.CHAIN + 9)
        back_chain = Chain(st.sem("dve_back"), Norm.CHAIN + 2)
        block = ctx.enter_context(nc.Block())

        def run_pipeline(eng, front, back, finish):
            issue(front(0))
            merge(back(0), front(1))
            with eng.Fori(1, RUNS - 1) as t:
                merge(finish(t - 1), back(t), front(t + 1))
            merge(finish(RUNS - 2), back(RUNS - 1))
            issue(finish(RUNS - 1))

        @block.gpsimd
        def _(pool):
            for s in [norm_in.rstd_ready, norm_out.rstd_ready, gated_done] + ([dist_ready] if by_distance else []):
                s.credit(pool)

            def front(k):
                yield from skip(6)
                norm_in.power(nc, pool, k, g.minus_half)
                yield from skip(9)
                if by_distance:
                    pool.wait_ge(d2_ready.sem, d2_ready.at(k, 1))
                    nc.gpsimd.tensor_tensor(dist[:, :, :], top[:, :, 0:2],
                                            g.plus_half[:, 0:2 * RT].rearrange("p (t c) -> p t c", t=RT),
                                            ALU.pow).then_inc(dist_ready.sem, 1)

            def back(i):
                for n in range(N):
                    e, r = n // FC, rows_of[n % FC]
                    if n % FC == 0:
                        pool.wait_ge(weights_ready.sem, weights_ready.at(i, e + 1))
                    pool.wait_ge(silu_done.sem, silu_done.at(i, n + 1))
                    if n < 2:
                        pool.wait_ge(h_done.sem, h_done.at(i, N - 1 + n, 1))
                    else:
                        pool.wait_ge(h_done.sem, h_done.at(i, n - 1))
                    nc.gpsimd.tensor_tensor(gated[n % 2][0:r, :], gate[n % 2][0:r, :], weights[e % 2][0:r, :],
                                            ALU.mult).then_inc(gated_done.sem, 1)
                    yield

            def finish(i):
                yield from skip(7)
                norm_out.power(nc, pool, i, g.minus_half)
                yield

            run_pipeline(pool, front, back, finish)

        @block.vector
        def _(dve):
            sigs = [norm_in.var_ready, norm_out.var_ready, y_ready, y_lo_ready, gap_ready, h_done, lo_done,
                    front_chain.sig, back_chain.sig, we_ready]
            if by_distance:
                sigs += [d2_ready]
            for s in sigs:
                s.credit(dve)
            dve.wait_ge(loaded, 16)
            nc.vector.memset(we_parts[:, :, :], 0.0)
            nc.vector.tensor_copy(pick_expert[:, :], at["pick_expert"][0:WROWS, :]).then_inc(constants, 1)
            if by_distance:
                nc.vector.tensor_copy(down_b_hi[:, :], at["down_b"][0:WROWS, :]).then_inc(constants, 1)
                dve.wait_ge(constants, 2)
                nc.vector.tensor_tensor(down_b_lo[:, :], at["down_b"][0:WROWS, :], down_b_hi[:, :].bitcast(F32),
                                        ALU.subtract).then_inc(constants, 1)
                nc.vector.memset(ones[:, :], 1.0).then_inc(ones_ready, 1)
                nc.vector.tensor_tensor(c2[:, 0:NE], at["router"], at["router"], ALU.mult).then_inc(c2_sq, 1)
                dve.wait_ge(c2_sq, 1)
                nc.vector.tensor_scalar(c2[:, 2 * NE:3 * NE], at["router"], -2.0, None, ALU.mult).then_inc(c2_sq, 1)
                dve.wait_ge(c2_ps, 1)
                nc.vector.tensor_copy(c2[:, NE:2 * NE], ps[:, 7, 0:NE]).then_inc(constants, 1)
                dve.wait_ge(constants, 4)
                bias = c2[:, NE:2 * NE]
            else:
                bias = at["logit_bias"]
                dve.wait_ge(constants, 1)

            def hidden(i, n):
                r = rows_of[n % FC]
                dve.wait_ge(up_ps.sem, up_ps.at(i, n + 1))
                dve.wait_ge(gated_done.sem, gated_done.at(i, n + 1))
                if n < 2:
                    dve.wait_ge(lo_done.sem, lo_done.at(i, N - 1 + n, 1))
                else:
                    dve.wait_ge(lo_done.sem, lo_done.at(i, n - 1))
                up = ps[0:r, 2 + n % 3, :]
                if by_distance:
                    last = nc.vector.scalar_tensor_tensor(h[n % 2][0:r, :], up, at["up_b"][0:r, n:n + 1],
                                                          gated[n % 2][0:r, :], ALU.add, ALU.mult)
                else:
                    last = nc.vector.tensor_tensor(h[n % 2][0:r, :], up, gated[n % 2][0:r, :], ALU.mult)
                last.then_inc(h_done.sem, 1)

            def low_part(i, n):
                r = rows_of[n % FC]
                dve.wait_ge(h_done.sem, h_done.at(i, n + 1))
                dve.wait_ge(hi_done.sem, hi_done.at(i, n + 1))
                nc.vector.tensor_tensor(h_lo[0:r, n % RING, :], h[n % 2][0:r, :],
                                        h_hi[0:r, n % RING, :].bitcast(F32), ALU.subtract).then_inc(lo_done.sem, 1)

            def front(k):
                front_chain.begin(k)
                yield from skip(5)
                norm_in.moments(nc, dve, front_chain, lambda j: x[:, k * RT + j, :])
                yield from skip(2)
                dve.wait_ge(norm_in.rstd_ready.sem, norm_in.rstd_ready.at(k, 1))
                dve.wait_ge(yT_ps.sem, yT_ps.at(k, 1, 1))
                if by_distance:
                    dve.wait_ge(sq_ready.sem, sq_ready.at(k, 1, 1))
                for j in range(RT):
                    last = norm_in.apply(nc, j, y[:, j, :], x[:, k * RT + j, :])
                last.then_inc(y_ready.sem, 1)
                yield from skip(6)
                dve.wait_ge(router_ps.sem, router_ps.at(k, 1))
                bc = bias.rearrange("p (o e) -> p o e", o=1).to_broadcast([P, RT, NE])
                nc.vector.tensor_tensor(score[:, :, :], ps[:, 6, 0:RT * NE].rearrange("p (t e) -> p t e", t=RT), bc,
                                        ALU.add).then_inc(front_chain.next(), 1)
                dve.wait_ge(front_chain.sem, front_chain.so_far())
                if by_distance:
                    dve.wait_ge(sq_ready.sem, sq_ready.at(k, 1))
                    nc.vector.tensor_tensor(
                        score[:, :, :], score[:, :, :],
                        sq_y[:, :].rearrange("p (t o) -> p t o", o=1).to_broadcast([P, RT, NE]),
                        ALU.add).then_inc(front_chain.next(), 1)
                    dve.wait_ge(front_chain.sem, front_chain.so_far())
                    nc.vector.tensor_scalar(score[:, :, :], score[:, :, :], 1e-12, None, ALU.max).then_inc(
                        front_chain.next(), 1)
                    dve.wait_ge(front_chain.sem, front_chain.so_far())
                yield from skip(2)
                if by_distance:
                    dve.wait_ge(dist_ready.sem, dist_ready.at(k, 1, 1))
                    own_wait(dve, st.dve_waited)
                for t in range(RT):
                    last = nc.vector.max(top[:, t, :], score[:, t, :])
                last.then_inc(d2_ready.sem if by_distance else front_chain.next(), 1)
                if by_distance:
                    dve.wait_ge(d2_ready.sem, d2_ready.at(k, 1))
                else:
                    dve.wait_ge(front_chain.sem, front_chain.so_far())
                own_wait(dve, st.dve_waited)
                for t in range(RT):
                    last = nc.vector.max_index(top_at[:, t, :], top[:, t, :], score[:, t, :])
                last.then_inc(front_chain.next(), 1)
                dve.wait_ge(front_chain.sem, front_chain.so_far())
                nc.vector.tensor_copy(top_atf[:, :, :], top_at[:, :, 0:2]).then_inc(front_chain.next(), 1)
                yield
                if by_distance:
                    dve.wait_ge(dist_ready.sem, dist_ready.at(k, 1))
                nc.vector.tensor_tensor(gap[:, :], best[:, :, 1], best[:, :, 0], ALU.subtract).then_inc(
                    gap_ready.sem, 1)
                yield
                dve.wait_ge(front_chain.sem, front_chain.so_far())
                dve.wait_ge(th_ready.sem, th_ready.at(k, 1))
                nc.vector.tensor_scalar(share[:, :, 0], th[:, :], -0.5, 0.5, ALU.mult, ALU.add)
                nc.vector.tensor_scalar(share[:, :, 1], th[:, :], 0.5, 0.5, ALU.mult, ALU.add)
                io = at["iota"].rearrange("p (o e) -> p o e", o=1).to_broadcast([P, RT, NE])
                for c in range(2):
                    last = nc.vector.tensor_tensor(one_hot[:, :, c, :], io,
                                                   top_atf[:, :, c:c + 1].to_broadcast([P, RT, NE]), ALU.is_equal)
                last.then_inc(front_chain.next(), 1)
                dve.wait_ge(front_chain.sem, front_chain.so_far())
                for c in range(2):
                    last = nc.vector.tensor_tensor(one_hot[:, :, c, :], one_hot[:, :, c, :],
                                                   share[:, :, c:c + 1].to_broadcast([P, RT, NE]), ALU.mult)
                last.then_inc(front_chain.next(), 1)
                dve.wait_ge(front_chain.sem, front_chain.so_far())
                yield
                nc.vector.tensor_tensor(we[:, :, :], one_hot[:, :, 0, :], one_hot[:, :, 1, :], ALU.add).then_inc(
                    front_chain.next(), 1)
                dve.wait_ge(front_chain.sem, front_chain.so_far())
                if not by_distance:
                    nc.vector.memset(we[:, :, NE - 1:NE], 1.0).then_inc(front_chain.next(), 1)
                    dve.wait_ge(front_chain.sem, front_chain.so_far())
                nc.vector.tensor_copy(we_hi[:, :, :], we[:, :, :]).then_inc(front_chain.next(), 1)
                dve.wait_ge(front_chain.sem, front_chain.so_far())
                dve.wait_ge(weT_ps.sem, weT_ps.at(k, 1, 1))
                nc.vector.tensor_copy(we_parts[:, :, 0:NE], we_hi[:, :, :].bitcast(F32))
                nc.vector.tensor_tensor(we_parts[:, :, LOW:WROWS], we[:, :, :], we_hi[:, :, :].bitcast(F32),
                                        ALU.subtract).then_inc(we_ready.sem, 1)
                dve.wait_ge(we_ready.sem, we_ready.at(k, 1))
                yield from skip(N - 18)
                dve.wait_ge(y_hi_ready.sem, y_hi_ready.at(k, 1))
                nc.vector.tensor_tensor(y_lo[:, :], yT[:, :], y_hi[:, :].bitcast(F32), ALU.subtract).then_inc(
                    y_lo_ready.sem, 1)
                front_chain.end()

            def back(i):
                for n in range(N):
                    if n >= 1:
                        hidden(i, n - 1)
                    if n >= 2:
                        low_part(i, n - 2)
                    yield

            def finish(i):
                back_chain.begin(i)
                hidden(i, N - 1)
                low_part(i, N - 2)
                yield
                low_part(i, N - 1)
                yield from skip(5)
                dve.wait_ge(f_ready.sem, f_ready.at(i, 1))
                norm_out.moments(nc, dve, back_chain, lambda j: f[:, j, :])
                yield from skip(2)
                add_normed(nc, dve, back_chain, norm_out, i, x, i * RT, f)
                dve.wait_ge(back_chain.sem, back_chain.so_far())
                back_chain.end()

            run_pipeline(dve, front, back, finish)

        @block.scalar
        def _(act):
            nc.scalar.preload_act_table(ACT.Silu)
            sigs = [yT_ready, y_hi_ready, th_ready, weT_ready, weights_ready, silu_done, hi_done, accT_ready, f_ready]
            if by_distance:
                sigs += [sq_ready]
            for s in sigs:
                s.credit(act)
            act.wait_ge(loaded, 16)

            def expert_weights_row(i, e):
                act.wait_ge(weights_ps.sem, weights_ps.at(i, e + 1))
                if e < 2:
                    act.wait_ge(gated_done.sem, gated_done.at(i, N + FC * (e - 1), 1))
                else:
                    act.wait_ge(gated_done.sem, gated_done.at(i, FC * (e - 1)))
                nc.scalar.activation(weights[e % 2][:, :], ps[:, 7, :], ACT.Copy).then_inc(weights_ready.sem, 1)

            def high_part(i, n):
                r = rows_of[n % FC]
                act.wait_ge(h_done.sem, h_done.at(i, n + 1))
                if n < RING:
                    act.wait_ge(down_done.sem, down_done.at(i, N - RING + 1 + n, 1))
                else:
                    act.wait_ge(down_done.sem, down_done.at(i, n - RING + 1))
                nc.scalar.activation(h_hi[0:r, n % RING, :], h[n % 2][0:r, :], ACT.Copy).then_inc(hi_done.sem, 1)

            def front(k):
                yield from skip(10)
                act.wait_ge(yT_ps.sem, yT_ps.at(k, 1))
                act.wait_ge(y_lo_ready.sem, y_lo_ready.at(k, 1, 1))
                nc.scalar.activation(yT[:, :], ps[:, 6, :], ACT.Copy).then_inc(yT_ready.sem, 1)
                if by_distance:
                    act.wait_ge(y_ready.sem, y_ready.at(k, 1))
                    act.wait_ge(d2_ready.sem, d2_ready.at(k, 1, 1))
                    for t in range(RT):
                        last = nc.scalar.activation(square[:, t, :], y[:, t, :], ACT.Square, accum_out=sq_y[:, t:t + 1])
                    last.then_inc(sq_ready.sem, 1)
                yield from skip(7)
                act.wait_ge(gap_ready.sem, gap_ready.at(k, 1))
                nc.scalar.activation(th[:, :], gap[:, :], ACT.Tanh, scale=0.5).then_inc(th_ready.sem, 1)
                yield from skip(5)
                act.wait_ge(weT_ps.sem, weT_ps.at(k, 1))
                nc.scalar.activation(weT[:, :], ps[0:WROWS, 6, :], ACT.Copy).then_inc(weT_ready.sem, 1)
                yield from skip(N - 22)
                act.wait_ge(yT_ready.sem, yT_ready.at(k, 1))
                act.wait_ge(up_ps.sem, up_ps.at(k, N, 1))
                nc.scalar.activation(y_hi[:, :], yT[:, :], ACT.Copy).then_inc(y_hi_ready.sem, 1)

            def back(i):
                for n in range(N):
                    r = rows_of[n % FC]
                    if n == 0:
                        expert_weights_row(i, 0)
                    act.wait_ge(gate_ps.sem, gate_ps.at(i, n + 1))
                    if n < 2:
                        act.wait_ge(gated_done.sem, gated_done.at(i, N - 1 + n, 1))
                    else:
                        act.wait_ge(gated_done.sem, gated_done.at(i, n - 1))
                    bias = at["gate_b"][0:r, n:n + 1] if by_distance else 0.0
                    nc.scalar.activation(gate[n % 2][0:r, :], ps[0:r, n % 2, :], ACT.Silu, bias=bias).then_inc(
                        silu_done.sem, 1)
                    if n >= 2:
                        high_part(i, n - 2)
                    if n % FC == FC - 1 and n < N - 1:
                        expert_weights_row(i, n // FC + 1)
                    yield

            def finish(i):
                high_part(i, N - 2)
                yield
                high_part(i, N - 1)
                yield from skip(2)
                act.wait_ge(down_done.sem, down_done.at(i, N))
                act.wait_ge(f_ps.sem, f_ps.at(i, 1, 1))
                nc.scalar.activation(accT[:, :], ps[:, 5, :], ACT.Copy).then_inc(accT_ready.sem, 1)
                yield from skip(2)
                act.wait_ge(f_ps.sem, f_ps.at(i, 1))
                act.wait_ge(back_chain.sem, back_chain.sig.at(i, back_chain.per, 1))
                nc.scalar.activation(f[:, :, :], ps[:, 6, :].rearrange("p (t d) -> p t d", t=RT), ACT.Copy).then_inc(
                    f_ready.sem, 1)
                yield

            run_pipeline(act, front, back, finish)

        @block.tensor
        def _(pe):
            mm = nc.tensor.matmul
            for s in (yT_ps, router_ps, weT_ps, weights_ps, gate_ps, up_ps, down_done, f_ps):
                s.credit(pe)
            pe.wait_ge(loaded, 16)
            if by_distance:
                pe.wait_ge(ones_ready, 1)
                pe.wait_ge(c2_sq, 1)
                mm(ps[:, 7, 0:NE], ones[:, :], c2[:, 0:NE], start=True, stop=True).then_inc(c2_ps, 1)
            pe.wait_ge(constants, 4 if by_distance else 1)
            router = c2[:, 2 * NE:3 * NE] if by_distance else at["router"]

            def front(k):
                yield from skip(9)
                pe.wait_ge(y_ready.sem, y_ready.at(k, 1))
                pe.wait_ge(f_ready.sem, f_ready.at(k, 1, 2))
                for t in range(RT):
                    last = nc.tensor.transpose(ps[:, 6, t * P:(t + 1) * P], y[:, t, :], g.ident[:, :])
                last.then_inc(yT_ps.sem, 1)
                yield from skip(3)
                pe.wait_ge(yT_ready.sem, yT_ready.at(k, 1))
                for t in range(RT):
                    last = mm(ps[:, 6, t * NE:(t + 1) * NE], yT[:, t * P:(t + 1) * P], router, start=True, stop=True)
                last.then_inc(router_ps.sem, 1)
                yield from skip(9)
                pe.wait_ge(we_ready.sem, we_ready.at(k, 1))
                for t in range(RT):
                    last = mm(ps[0:WROWS, 6, t * P:(t + 1) * P], we_parts[:, t, :], g.ident[:, :], start=True, stop=True)
                last.then_inc(weT_ps.sem, 1)
                yield

            def down(i, n):
                e, c, r = n // FC, n % FC, rows_of[n % FC]
                if n == 0:
                    pe.wait_ge(accT_ready.sem, accT_ready.at(i, 1, 1))
                    if by_distance:
                        mm(ps[:, 5, :], down_b_hi[:, :], weT[:, :], start=True, stop=False)
                        mm(ps[:, 5, :], down_b_lo[:, :], weT[:, :], start=False, stop=False)
                pe.wait_ge(lo_done.sem, lo_done.at(i, n + 1))
                hi, lo = w["down_hi"][0:r, e, c, :], w["down_lo"][0:r, e, c, :]
                mm(ps[:, 5, :], hi, h_hi[0:r, n % RING, :], start=n == 0 and not by_distance, stop=False)
                mm(ps[:, 5, :], lo, h_hi[0:r, n % RING, :], start=False, stop=False)
                mm(ps[:, 5, :], hi, h_lo[0:r, n % RING, :], start=False, stop=n == N - 1).then_inc(down_done.sem, 1)

            def weights_of(i, e):
                if e == 0:
                    pe.wait_ge(weT_ready.sem, weT_ready.at(i, 1))
                    pe.wait_ge(weights_ready.sem, weights_ready.at(i, NE, 1))
                else:
                    pe.wait_ge(weights_ready.sem, weights_ready.at(i, e))
                mm(ps[:, 7, :], pick_expert[:, e * P:(e + 1) * P], weT[:, :], start=True, stop=True).then_inc(
                    weights_ps.sem, 1)

            def back(i):
                for n in range(N):
                    e, c, r = n // FC, n % FC, rows_of[n % FC]
                    if n == 0:
                        weights_of(i, 0)
                        pe.wait_ge(y_hi_ready.sem, y_hi_ready.at(i, 1))
                        pe.wait_ge(y_lo_ready.sem, y_lo_ready.at(i, 1))
                    for k, (bank, done) in enumerate(((n % 2, gate_ps), (2 + n % 3, up_ps))):
                        if k == 0 and n < 2:
                            pe.wait_ge(silu_done.sem, silu_done.at(i, N - 1 + n, 1))
                        elif k == 0:
                            pe.wait_ge(silu_done.sem, silu_done.at(i, n - 1))
                        elif n < 3:
                            pe.wait_ge(h_done.sem, h_done.at(i, N - 2 + n, 1))
                        else:
                            pe.wait_ge(h_done.sem, h_done.at(i, n - 2))
                        s = slice(k * width + c * P, k * width + c * P + r)
                        o = ps[0:r, bank, :]
                        mm(o, w["gu_hi"][:, e, s], y_hi[:, :], start=True, stop=False)
                        mm(o, w["gu_hi"][:, e, s], y_lo[:, :], start=False, stop=False)
                        mm(o, w["gu_lo"][:, e, s], y_hi[:, :], start=False, stop=True).then_inc(done.sem, 1)
                    if c == 1 and e + 1 < NE:
                        weights_of(i, e + 1)
                    if n == 4:
                        down(i, 0)
                    if n >= 4:
                        down(i, n - 3)
                    yield

            def finish(i):
                for n in range(N - 3, N):
                    down(i, n)
                    yield
                yield
                pe.wait_ge(accT_ready.sem, accT_ready.at(i, 1))
                for t in range(RT):
                    last = nc.tensor.transpose(ps[:, 6, t * P:(t + 1) * P], accT[:, t * P:(t + 1) * P], g.ident[:, :])
                last.then_inc(f_ps.sem, 1)
                yield

            run_pipeline(pe, front, back, finish)



F_SEL = 2 * P
SEL = [("nav_w", P), ("nav_b", 1), ("choose_w", NE), ("choose_b", NE), ("wo", P), ("bo", P)]
SEL_EXPERT = [("w1", F_SEL), ("w2", F_SEL), ("b1", F_SEL // P), ("b2", 1)]


def columns(tensor, names):
    at, off = {}, 0
    for name, width in names:
        at[name] = tensor[:, off:off + width]
        off += width
    assert off == tensor.shape[1]
    return at


def selected_ffn(nc, g, layer, key, experts_dram, prefetch=None):
    x = g.x
    with ExitStack() as ctx:
        st = Stage(nc, ctx, f"f{layer}")
        ps = st.ps
        wb = g.w[key]
        at = columns(wb, SEL)
        expert = [st.sb(f"expert{k}", [P, experts_dram.shape[2]]) for k in range(2)]
        ex = [columns(e, SEL_EXPERT) for e in expert]
        y = [st.sb(f"y{k}", [P, T, P]) for k in range(2)]
        yT = [st.sb(f"yT{k}", [P, SEQ]) for k in range(2)]
        nav = st.sb("nav", [P, 1])
        logits, best = st.sb("logits", [1, NE]), st.sb("best", [1, 8])
        chosen = [st.sb(f"chosen{k}", [1, 8], U32) for k in range(2)]
        hT = st.sb("hT", [P, 2, SEQ])
        rT = st.sb("rT", [P, SEQ])
        f = st.sb("f", [P, T, P])
        bo = st.sb("bo", [P, P])
        norm_in, norm_out = Norm(st, "in", T), Norm(st, "out", T)
        loaded, bo_ready = g.loaded[key], st.sem("bo_ready")
        y_ready, yT_ps, yT_ready = st.sig("y_ready", 1), st.sig("yT_ps", 1), st.sig("yT_ready", 1)
        nav_ps, nav_ready = st.sig("nav_ps", 1), st.sig("nav_ready", 1)
        logit_ps, chosen_ready = st.sig("logit_ps", 1), st.sig("chosen_ready", 1)
        expert_loaded = [st.sem(f"expert_loaded{k}") for k in range(2)]
        h_ps, h_ready = st.sig("h_ps", 2), st.sig("h_ready", 2)
        r_ps, r_ready = st.sig("r_ps", 1), st.sig("r_ready", 1)
        out_ps, f_ready = st.sig("out_ps", 1), st.sig("f_ready", 1)
        early_chain, front_chain = Chain(st.sem("dve_early"), Norm.CHAIN), Chain(st.sem("dve_front"), 2)
        back_chain, finish_chain = Chain(st.sem("dve_back"), Norm.CHAIN + 1), Chain(st.sem("dve_finish"), 2)
        block = ctx.enter_context(nc.Block())

        @block.sync
        def _(sp):
            def front(i, p):
                yield
                yield
                yield
                sp.wait_ge(chosen_ready.sem, chosen_ready.at(i, 1))
                own_wait(sp, st.sp_waited)
                sp.wait_ge(f_ready.sem, f_ready.at(i, 1, 2))
                own_wait(sp, st.sp_waited)
                e = sp.value_load(chosen[p][0:1, 0:1], min_val=0, max_val=NE - 1)
                sp.dma_start(expert[p][:, :], experts_dram[e, :, :]).then_inc(expert_loaded[p], 16)
                yield

            pipeline_early(sp, nothing, front, nothing, nothing)

        @block.gpsimd
        def _(pool):
            norm_in.rstd_ready.credit(pool)
            norm_out.rstd_ready.credit(pool)
            if prefetch:
                prefetch(pool)

            def early(i, p):
                yield
                norm_in.power(nc, pool, i, g.minus_half)
                yield

            def back(i, p):
                yield
                yield
                norm_out.power(nc, pool, i, g.minus_half)
                yield

            pipeline_early(pool, early, nothing, back, nothing)

        @block.vector
        def _(dve):
            for s in (norm_in.var_ready, norm_out.var_ready, y_ready, chosen_ready, f_ready, front_chain.sig,
                      back_chain.sig, early_chain.sig, finish_chain.sig):
                s.credit(dve)
            dve.wait_ge(loaded, 16)
            nc.vector.tensor_scalar(bo[:, :], at["bo"], 0.3, None, ALU.mult).then_inc(bo_ready, 1)
            dve.wait_ge(bo_ready, 1)

            def early(i, p):
                early_chain.begin(i)
                yield
                norm_in.moments(nc, dve, early_chain, lambda j: x[:, i * T + j, :])
                early_chain.end()
                yield
                yield
                dve.wait_ge(norm_in.rstd_ready.sem, norm_in.rstd_ready.at(i, 1))
                dve.wait_ge(f_ready.sem, f_ready.at(i, 1, 2))
                for j in range(T):
                    last = norm_in.apply(nc, j, y[p][:, j, :], x[:, i * T + j, :])
                last.then_inc(y_ready.sem, 1)
                yield

            def front(i, p):
                front_chain.begin(i)
                yield
                yield
                yield
                dve.wait_ge(logit_ps.sem, logit_ps.at(i, 1))
                nc.vector.tensor_tensor(logits[:, :], ps[0:1, 0, 0:NE], at["choose_b"][0:1, :], ALU.add).then_inc(front_chain.next(), 1)
                dve.wait_ge(front_chain.sem, front_chain.so_far())
                own_wait(dve, st.dve_waited)
                nc.vector.max(best[:, :], logits[:, :]).then_inc(front_chain.next(), 1)
                dve.wait_ge(front_chain.sem, front_chain.so_far())
                own_wait(dve, st.dve_waited)
                nc.vector.max_index(chosen[p][:, :], best[:, :], logits[:, :]).then_inc(chosen_ready.sem, 1)
                dve.wait_ge(chosen_ready.sem, chosen_ready.at(i, 1))
                yield
                front_chain.end()

            def back(i, p):
                back_chain.begin(i)
                yield
                yield
                dve.wait_ge(y_ready.sem, y_ready.at(i, 1))
                for t in range(T):
                    last = nc.vector.tensor_tensor(y[p][:, t, :], y[p][:, t, :], bo[:, :], ALU.add)
                last.then_inc(back_chain.next(), 1)
                dve.wait_ge(back_chain.sem, back_chain.so_far())
                dve.wait_ge(out_ps.sem, out_ps.at(i, 1))
                nc.vector.scalar_tensor_tensor(f[:, :, :], ps[:, 5, 0:SEQ].rearrange("p (t d) -> p t d", t=T), 0.3,
                                               y[p][:, :, :], ALU.mult, ALU.add).then_inc(f_ready.sem, 1)
                dve.wait_ge(f_ready.sem, f_ready.at(i, 1))
                norm_out.moments(nc, dve, back_chain, lambda j: f[:, j, :])
                back_chain.end()
                yield

            def finish(i):
                finish_chain.begin(i)
                yield
                add_normed(nc, dve, finish_chain, norm_out, i, x, i * T, f)
                dve.wait_ge(finish_chain.sem, finish_chain.so_far())
                finish_chain.end()
                yield

            pipeline_early(dve, early, front, back, finish)

        @block.scalar
        def _(act):
            nc.scalar.preload_act_table(ACT.Gelu)
            for s in (yT_ready, nav_ready, h_ready, r_ready):
                s.credit(act)
            act.wait_ge(loaded, 16)

            def front(i, p):
                yield
                act.wait_ge(yT_ps.sem, yT_ps.at(i, 1))
                act.wait_ge(h_ps.sem, h_ps.at(i, 2, 2))
                nc.scalar.activation(yT[p][:, :], ps[:, 0, 0:SEQ], ACT.Copy).then_inc(yT_ready.sem, 1)
                yield
                act.wait_ge(nav_ps.sem, nav_ps.at(i, 1))
                nc.scalar.activation(nav[:, :], ps[:, 1, 0:1], ACT.Gelu, bias=at["nav_b"]).then_inc(nav_ready.sem, 1)
                yield

            def back(i, p):
                act.wait_ge(expert_loaded[p], (i - p) * 8 + 16)
                for c in range(2):
                    act.wait_ge(h_ps.sem, h_ps.at(i, c + 1))
                    nc.scalar.activation(hT[:, c, :], ps[:, 2 + c, 0:SEQ], ACT.Gelu, bias=ex[p]["b1"][:, c:c + 1]).then_inc(
                        h_ready.sem, 1)
                yield
                act.wait_ge(r_ps.sem, r_ps.at(i, 1))
                nc.scalar.activation(rT[:, :], ps[:, 4, 0:SEQ], ACT.Identity, bias=ex[p]["b2"]).then_inc(r_ready.sem, 1)
                yield

            pipeline_early(act, nothing, front, back, nothing)

        @block.tensor
        def _(pe):
            mm = nc.tensor.matmul
            for s in (yT_ps, nav_ps, logit_ps, h_ps, r_ps, out_ps):
                s.credit(pe)
            pe.wait_ge(loaded, 16)

            def front(i, p):
                yield
                pe.wait_ge(y_ready.sem, y_ready.at(i, 1))
                pe.wait_ge(chosen_ready.sem, chosen_ready.at(i, 1, 1))
                for t in range(T):
                    last = nc.tensor.transpose(ps[:, 0, t * P:(t + 1) * P], y[p][:, t, :], g.ident[:, :])
                last.then_inc(yT_ps.sem, 1)
                yield
                pe.wait_ge(yT_ready.sem, yT_ready.at(i, 1))
                pe.wait_ge(nav_ready.sem, nav_ready.at(i, 1, 1))
                mm(ps[:, 1, 0:1], at["nav_w"], yT[p][:, SEQ - 1:SEQ], start=True, stop=True).then_inc(nav_ps.sem, 1)
                yield
                pe.wait_ge(nav_ready.sem, nav_ready.at(i, 1))
                mm(ps[0:1, 0, 0:NE], nav[:, :], at["choose_w"], start=True, stop=True).then_inc(logit_ps.sem, 1)
                yield

            def back(i, p):
                pe.wait_ge(expert_loaded[p], (i - p) * 8 + 16)
                for c in range(2):
                    pe.wait_ge(h_ready.sem, h_ready.at(i, c + 1, 1))
                    mm(ps[:, 2 + c, 0:SEQ], ex[p]["w1"][:, c * P:(c + 1) * P], yT[p][:, :], start=True,
                       stop=True).then_inc(h_ps.sem, 1)
                yield
                pe.wait_ge(r_ready.sem, r_ready.at(i, 1, 1))
                for c in range(2):
                    pe.wait_ge(h_ready.sem, h_ready.at(i, c + 1))
                    last = mm(ps[:, 4, 0:SEQ], ex[p]["w2"][:, c * P:(c + 1) * P], hT[:, c, :], start=c == 0, stop=c == 1)
                last.then_inc(r_ps.sem, 1)
                yield
                pe.wait_ge(r_ready.sem, r_ready.at(i, 1))
                pe.wait_ge(f_ready.sem, f_ready.at(i, 1, 1))
                for t in range(T):
                    last = mm(ps[:, 5, t * P:(t + 1) * P], rT[:, t * P:(t + 1) * P], at["wo"], start=True, stop=True)
                last.then_inc(out_ps.sem, 1)
                yield

            pipeline_early(pe, nothing, front, back, nothing)



MIX = [("wqk", 2 * P), ("wv", P), ("wo", P), ("blocks", P)]


def channel_attention(nc, g, key):
    SCALE = float(D8) ** -0.5
    x = g.x
    with ExitStack() as ctx:
        st = Stage(nc, ctx, "a3")
        ps = st.ps
        wb = g.w[key]
        at = columns(wb, MIX)
        y = st.sb("y", [P, T, P])
        yT = st.sb("yT", [P, SEQ])
        qk = [st.sb(f"qk{k}", [P, T, 2 * P]) for k in range(2)]
        vT = [st.sb(f"vT{k}", [P, SEQ]) for k in range(2)]
        z, z_exp, zn = st.sb("z", [P, P]), st.sb("z_exp", [P, P]), st.sb("zn", [P, P])
        top, neg_top, total, recip = (st.sb(n, [P, 1]) for n in ("top", "neg_top", "total", "recip"))
        cxT = st.sb("cxT", [P, SEQ])
        f = st.sb("f", [P, T, P])
        norm_in, norm_out = Norm(st, "in", T), Norm(st, "out", T)
        loaded = g.loaded[key]
        y_ready, yT_ps, yT_ready = st.sig("y_ready", 1), st.sig("yT_ps", 1), st.sig("yT_ready", 1)
        qk_ps, qk_ready, v_ps, v_ready = (st.sig(n, 1) for n in ("qk_ps", "qk_ready", "v_ps", "v_ready"))
        z_ps, top_ready, exp_ready, zn_ready = (st.sig(n, 1) for n in ("z_ps", "top_ready", "exp_ready", "zn_ready"))
        cxT_ps, cxT_ready, out_ps, f_ready = (st.sig(n, 1) for n in ("cxT_ps", "cxT_ready", "out_ps", "f_ready"))
        front_chain = Chain(st.sem("dve_front"), Norm.CHAIN)
        back_chain = Chain(st.sem("dve_back"), Norm.CHAIN + 3)
        finish_chain = Chain(st.sem("dve_finish"), 2)
        block = ctx.enter_context(nc.Block())

        @block.gpsimd
        def _(pool):
            norm_in.rstd_ready.credit(pool)
            norm_out.rstd_ready.credit(pool)

            def early(i, p):
                yield
                norm_in.power(nc, pool, i, g.minus_half)
                yield

            def back(i, p):
                yield
                yield
                yield
                norm_out.power(nc, pool, i, g.minus_half)
                yield

            pipeline_early(pool, early, nothing, back, nothing)

        @block.vector
        def _(dve):
            for s in (norm_in.var_ready, norm_out.var_ready, y_ready, top_ready, zn_ready, f_ready, front_chain.sig,
                      back_chain.sig, finish_chain.sig):
                s.credit(dve)
            dve.wait_ge(loaded, 16)

            def early(i, p):
                front_chain.begin(i)
                yield
                norm_in.moments(nc, dve, front_chain, lambda j: x[:, i * T + j, :])
                yield
                dve.wait_ge(norm_in.rstd_ready.sem, norm_in.rstd_ready.at(i, 1))
                dve.wait_ge(yT_ps.sem, yT_ps.at(i, 1, 1))
                for j in range(T):
                    last = norm_in.apply(nc, j, y[:, j, :], x[:, i * T + j, :])
                last.then_inc(y_ready.sem, 1)
                yield
                front_chain.end()

            def back(i, p):
                back_chain.begin(i)
                dve.wait_ge(z_ps.sem, z_ps.at(i, 1))
                nc.vector.tensor_tensor(z[:, :], ps[:, 2, 0:P], at["blocks"], ALU.add).then_inc(back_chain.next(), 1)
                dve.wait_ge(back_chain.sem, back_chain.so_far())
                nc.vector.reduce_max(top[:, :], z[:, :], AX).then_inc(back_chain.next(), 1)
                dve.wait_ge(back_chain.sem, back_chain.so_far())
                nc.vector.tensor_scalar(neg_top[:, :], top[:, :], -SCALE, None, ALU.mult).then_inc(top_ready.sem, 1)
                yield
                dve.wait_ge(exp_ready.sem, exp_ready.at(i, 1))
                nc.vector.reciprocal(recip[:, :], total[:, :]).then_inc(back_chain.next(), 1)
                dve.wait_ge(back_chain.sem, back_chain.so_far())
                nc.vector.tensor_scalar(zn[:, :], z_exp[:, :], recip[:, 0:1], None, ALU.mult).then_inc(zn_ready.sem, 1)
                yield
                yield
                dve.wait_ge(out_ps.sem, out_ps.at(i, 1))
                nc.vector.tensor_copy(f[:, :, :], ps[:, 4, 0:SEQ].rearrange("p (t d) -> p t d", t=T)).then_inc(
                    f_ready.sem, 1)
                dve.wait_ge(f_ready.sem, f_ready.at(i, 1))
                norm_out.moments(nc, dve, back_chain, lambda j: f[:, j, :])
                back_chain.end()
                yield

            def finish(i):
                finish_chain.begin(i)
                yield
                add_normed(nc, dve, finish_chain, norm_out, i, x, i * T, f)
                dve.wait_ge(finish_chain.sem, finish_chain.so_far())
                finish_chain.end()
                yield

            pipeline_early(dve, early, nothing, back, finish)

        @block.scalar
        def _(act):
            nc.scalar.preload_act_table(ACT.Exp)
            for s in (yT_ready, qk_ready, v_ready, exp_ready, cxT_ready):
                s.credit(act)

            def front(i, p):
                yield
                act.wait_ge(yT_ps.sem, yT_ps.at(i, 1))
                nc.scalar.activation(yT[:, :], ps[:, 0, 0:SEQ], ACT.Copy).then_inc(yT_ready.sem, 1)
                yield
                act.wait_ge(qk_ps.sem, qk_ps.at(i, 1))
                nc.scalar.activation(qk[p][:, :, :], ps[:, 1, :].rearrange("p (t d) -> p t d", t=T), ACT.Copy).then_inc(
                    qk_ready.sem, 1)
                act.wait_ge(v_ps.sem, v_ps.at(i, 1))
                nc.scalar.activation(vT[p][:, :], ps[:, 0, 0:SEQ], ACT.Copy).then_inc(v_ready.sem, 1)
                yield

            def back(i, p):
                act.wait_ge(top_ready.sem, top_ready.at(i, 1))
                act.wait_ge(zn_ready.sem, zn_ready.at(i, 1, 1))
                nc.scalar.activation(z_exp[:, :], z[:, :], ACT.Exp, bias=neg_top[:, :], scale=SCALE,
                                     accum_out=total[:, :]).then_inc(exp_ready.sem, 1)
                yield
                yield
                act.wait_ge(cxT_ps.sem, cxT_ps.at(i, 1))
                nc.scalar.activation(cxT[:, :], ps[:, 3, 0:SEQ], ACT.Copy).then_inc(cxT_ready.sem, 1)
                yield

            pipeline_early(act, nothing, front, back, nothing)

        @block.tensor
        def _(pe):
            mm = nc.tensor.matmul
            for s in (yT_ps, qk_ps, v_ps, z_ps, cxT_ps, out_ps):
                s.credit(pe)
            pe.wait_ge(loaded, 16)

            def front(i, p):
                yield
                pe.wait_ge(y_ready.sem, y_ready.at(i, 1))
                pe.wait_ge(v_ready.sem, v_ready.at(i, 1, 1))
                for t in range(T):
                    last = nc.tensor.transpose(ps[:, 0, t * P:(t + 1) * P], y[:, t, :], g.ident[:, :])
                last.then_inc(yT_ps.sem, 1)
                yield
                pe.wait_ge(yT_ready.sem, yT_ready.at(i, 1))
                pe.wait_ge(qk_ready.sem, qk_ready.at(i, 1, 1))
                for t in range(T):
                    last = mm(ps[:, 1, t * 2 * P:(t + 1) * 2 * P], yT[:, t * P:(t + 1) * P], at["wqk"], start=True,
                              stop=True)
                last.then_inc(qk_ps.sem, 1)
                mm(ps[:, 0, 0:SEQ], at["wv"], yT[:, :], start=True, stop=True).then_inc(v_ps.sem, 1)
                yield

            def back(i, p):
                pe.wait_ge(qk_ready.sem, qk_ready.at(i, 1))
                pe.wait_ge(top_ready.sem, top_ready.at(i, 1, 1))
                for t in range(T):
                    last = mm(ps[:, 2, 0:P], qk[p][:, t, P:2 * P], qk[p][:, t, 0:P], start=t == 0, stop=t == T - 1)
                last.then_inc(z_ps.sem, 1)
                yield
                yield
                pe.wait_ge(zn_ready.sem, zn_ready.at(i, 1))
                pe.wait_ge(v_ready.sem, v_ready.at(i, 1))
                pe.wait_ge(cxT_ready.sem, cxT_ready.at(i, 1, 1))
                mm(ps[:, 3, 0:SEQ], zn[:, :], vT[p][:, :], start=True, stop=True).then_inc(cxT_ps.sem, 1)
                yield
                pe.wait_ge(cxT_ready.sem, cxT_ready.at(i, 1))
                pe.wait_ge(f_ready.sem, f_ready.at(i, 1, 1))
                for t in range(T):
                    last = mm(ps[:, 4, t * P:(t + 1) * P], cxT[:, t * P:(t + 1) * P], at["wo"], start=True, stop=True)
                last.then_inc(out_ps.sem, 1)
                yield

            pipeline_early(pe, nothing, front, back, nothing)



GQA = [("wq", NH * D64), ("wk", NG * P), ("wv", NG * D64), ("wpost", NH * D64),
       ("spread_sums", NH // 2 * P)]


def grouped_attention(nc, g, key):
    SCALE = float(D64) ** -0.5
    COLS = 32
    PAIRS = NH // 2
    x = g.x
    with ExitStack() as ctx:
        st = Stage(nc, ctx, "a2")
        ps = st.ps
        wb = g.w[key]
        at = columns(wb, GQA)
        y = [st.sb(f"y{k}", [P, T, P]) for k in range(2)]
        f = st.sb("f", [P, T, P])
        yT = st.sb("yT", [P, SEQ])
        Q = {part: [st.sb(f"q_{part}{k}", [P, PAIRS, SEQ], F32R) for k in range(2)] for part in ("hi", "lo")}
        K = {part: [st.sb(f"k_{part}{k}", [P, 2, NG, SEQ], F32R) for k in range(2)] for part in ("hi", "lo")}
        V = [st.sb(f"V{k}", [P, T, NG, D64]) for k in range(2)]
        sum_cols = st.sb("sum_cols", [P, NG, COLS])
        rowmax = st.sb("rowmax", [P, T, NH])
        mrow = [st.sb(f"mrow{k}", [NG, SEQ], F32R) for k in range(NG)]
        maxima = st.sb("maxima", [P, NG, HG * SEQ], F32R)
        ones_row = st.sb("ones_row", [P, P], F32R)
        ones_raw = st.sb("ones_raw", [P, P])
        probs = [st.sb(f"probs{k}", [P, 4, BANK]) for k in range(2)]
        recip = st.sb("recip", [P, SEQ])
        skip_y = st.sb("skip_y", [P, T, P])
        craw = st.sb("craw", [P, PAIRS, SEQ])
        cxT = st.sb("cxT", [P, PAIRS, SEQ])
        norm_in, norm_out = Norm(st, "in", T), Norm(st, "out", T)
        loaded, constants = g.loaded[key], st.sem("constants_ready")
        y_ready, yT_ps, yT_ready = st.sig("y_ready", 1), st.sig("yT_ps", 1), st.sig("yT_ready", 1)
        q_ps, q_hi_ready, q_lo_ready = st.sig("q_ps", NG), st.sig("q_hi_ready", NG), st.sig("q_lo_ready", NG)
        k_ps, k_hi_ready, k_lo_ready = st.sig("k_ps", 2), st.sig("k_hi_ready", 2), st.sig("k_lo_ready", 2)
        v_ps, v_ready = st.sig("v_ps", 1), st.sig("v_ready", 1)
        FILLS = 4
        score_ps, rowmax_ready = st.sig("score_ps", NG * FILLS), st.sig("rowmax_ready", NG * FILLS)
        max_ps, mrow_ready = st.sig("max_ps", NG), st.sig("mrow_ready", NG)
        mrow_placed = [st.sem(f"mrow_placed{j}") for j in range(NG)]
        sT_ps, exp_done = st.sig("sT_ps", NG * FILLS), st.sig("exp_done", NG * FILLS)
        pv_done, craw_ready = st.sig("pv_done", NG), st.sig("craw_ready", NG)
        recip_ready, recip_ps, cxT_ready = st.sig("recip_ready", 1), st.sig("recip_ps", NG), st.sig("cxT_ready", NG)
        skip_ready, maxima_clear = st.sig("skip_ready", 1), st.sem("maxima_clear")
        out_ps, f_ready = st.sig("out_ps", 1), st.sig("f_ready", 1)
        front_chain = Chain(st.sem("dve_front"), Norm.CHAIN)
        back_chain = Chain(st.sem("dve_back"), Norm.CHAIN + 2)
        HEAD = 5
        FINISH = 8
        block = ctx.enter_context(nc.Block())

        @block.sync
        def _(sp):
            def front(i, p):
                yield from skip(HEAD + FILLS + 2)
                for j in range(NG):
                    sp.wait_ge(mrow_ready.sem, mrow_ready.at(i, j + 1))
                    own_wait(sp, st.sp_waited)
                    sp.wait_ge(sT_ps.sem, sT_ps.at(i, (j + 1) * FILLS, 1))
                    sp.dma_start(maxima[0:1, j, :].rearrange("p (h q) -> p h q", h=HG).bitcast(F32),
                                 mrow[j][:, :].bitcast(F32)).then_inc(mrow_placed[j], 16)
                    yield from skip(FILLS)

            pipeline3(sp, front, nothing, nothing)

        @block.gpsimd
        def _(pool):
            norm_in.rstd_ready.credit(pool)
            norm_out.rstd_ready.credit(pool)
            nc.gpsimd.memset(maxima[:, :, :].bitcast(F32), 0.0).then_inc(maxima_clear, 1)
            def front(i, p):
                norm_in.power(nc, pool, i, g.minus_half)
                yield

            def finish(i):
                yield from skip(7)
                norm_out.power(nc, pool, i, g.minus_half)
                yield

            pipeline3(pool, front, nothing, finish)

        @block.vector
        def _(dve):
            for s in (norm_in.var_ready, norm_out.var_ready, y_ready, q_lo_ready, k_lo_ready, v_ready,
                      rowmax_ready, recip_ready, cxT_ready, skip_ready, f_ready, front_chain.sig, back_chain.sig):
                s.credit(dve)
            for k in range(2):
                for part in ("hi", "lo"):
                    nc.vector.memset(K[part][k][D64:P, 0, :, :].bitcast(F32), 0.0)
                    nc.vector.memset(K[part][k][0:D64, 1, :, :].bitcast(F32), 0.0)
            nc.vector.memset(sum_cols[:, :, :], 0.0)
            nc.vector.memset(ones_raw[:, :], 0.0).then_inc(constants, 1)
            dve.wait_ge(constants, 1)
            for j in range(NG):
                nc.vector.memset(sum_cols[:, j, :].rearrange("p (c r) -> p c r", r=NG)[:, :, j:j + 1], 1.0)
            nc.vector.memset(ones_raw[0:1, :], 1.0).then_inc(constants, 1)
            dve.wait_ge(constants, 2)
            nc.vector.tensor_copy(ones_row[:, :], ones_raw[:, :]).then_inc(constants, 1)
            dve.wait_ge(constants, 3)

            def front(i, p):
                front_chain.begin(i)
                norm_in.moments(nc, dve, front_chain, lambda j: x[:, i * T + j, :])
                dve.wait_ge(norm_in.rstd_ready.sem, norm_in.rstd_ready.at(i, 1))
                dve.wait_ge(skip_ready.sem, skip_ready.at(i, 1, 2))
                for j in range(T):
                    last = norm_in.apply(nc, j, y[p][:, j, :], x[:, i * T + j, :])
                last.then_inc(y_ready.sem, 1)
                yield
                yield
                for j in range(NG):
                    dve.wait_ge(q_hi_ready.sem, q_hi_ready.at(i, j + 1))
                    nc.vector.tensor_tensor(Q["lo"][p][:, 2 * j:2 * j + 2, :],
                                            ps[:, (j + 1) % 2, :].rearrange("p (h t) -> p h t", h=2),
                                            Q["hi"][p][:, 2 * j:2 * j + 2, :].bitcast(F32), ALU.subtract).then_inc(
                        q_lo_ready.sem, 1)
                    if j == 1:
                        yield
                for n in range(2):
                    dve.wait_ge(k_hi_ready.sem, k_hi_ready.at(i, n + 1))
                    bank = ps[:, (n + 1) % 2, :].rearrange("p (g t) -> p g t", g=2)
                    for half, rows in enumerate((slice(0, D64), slice(D64, P))):
                        last = nc.vector.tensor_tensor(K["lo"][p][rows, half, 2 * n:2 * n + 2, :], bank[rows],
                                                       K["hi"][p][rows, half, 2 * n:2 * n + 2, :].bitcast(F32),
                                                       ALU.subtract)
                    last.then_inc(k_lo_ready.sem, 1)
                dve.wait_ge(v_ps.sem, v_ps.at(i, 1))
                dve.wait_ge(pv_done.sem, pv_done.at(i, NG, 2))
                nc.vector.tensor_copy(V[p][:, :, :, :],
                                      ps[:, 1, :].rearrange("p (t g d) -> p t g d", t=T, g=NG)).then_inc(v_ready.sem, 1)
                yield from skip(HEAD - 3)
                for j in range(NG):
                    if j == 0:
                        dve.wait_ge(max_ps.sem, max_ps.at(i, NG, 1))
                    for n in range(FILLS):
                        c = j * FILLS + n
                        dve.wait_ge(score_ps.sem, score_ps.at(i, c + 1))
                        t, h = n // 2, 4 * j + 2 * (n % 2)
                        nc.vector.reduce_max(rowmax[:, t, h:h + 2], ps[:, 2 + c % 2, :].rearrange("p (h k) -> p h k", h=2),
                                             AX).then_inc(rowmax_ready.sem, 1)
                        yield
                front_chain.end()

            def back(i, p):
                yield from skip(FINISH)
                dve.wait_ge(y_ready.sem, y_ready.at(i, 1))
                nc.vector.tensor_copy(skip_y[:, :, :], y[p][:, :, :]).then_inc(skip_ready.sem, 1)
                yield

            def finish(i):
                back_chain.begin(i)
                dve.wait_ge(pv_done.sem, pv_done.at(i, NG))
                nc.vector.reciprocal(recip[:, :], ps[:, 7, 0:SEQ]).then_inc(recip_ready.sem, 1)
                yield
                for j in range(NG):
                    dve.wait_ge(recip_ps.sem, recip_ps.at(i, j + 1))
                    dve.wait_ge(craw_ready.sem, craw_ready.at(i, j + 1))
                    nc.vector.tensor_tensor(cxT[:, 2 * j:2 * j + 2, :], ps[:, 6, :].rearrange("p (h t) -> p h t", h=2),
                                            craw[:, 2 * j:2 * j + 2, :], ALU.mult).then_inc(cxT_ready.sem, 1)
                    yield
                dve.wait_ge(out_ps.sem, out_ps.at(i, 1))
                nc.vector.tensor_copy(f[:, :, :], ps[:, 7, SEQ:2 * SEQ].rearrange("p (t d) -> p t d", t=T)).then_inc(
                    f_ready.sem, 1)
                yield
                dve.wait_ge(f_ready.sem, f_ready.at(i, 1))
                norm_out.moments(nc, dve, back_chain, lambda j: f[:, j, :])
                yield from skip(2)
                add_normed(nc, dve, back_chain, norm_out, i, x, i * T, f)
                dve.wait_ge(back_chain.sem, back_chain.so_far())
                back_chain.end()

            pipeline3(dve, front, back, finish)

        @block.scalar
        def _(act):
            nc.scalar.preload_act_table(ACT.Exp)
            for s in (yT_ready, q_hi_ready, k_hi_ready, mrow_ready, exp_done, craw_ready):
                s.credit(act)
            act.wait_ge(constants, 3)

            def front(i, p):
                yield
                act.wait_ge(yT_ps.sem, yT_ps.at(i, 1))
                nc.scalar.activation(yT[:, :], ps[:, 0, 0:SEQ], ACT.Copy).then_inc(yT_ready.sem, 1)
                yield
                act.wait_ge(sT_ps.sem, sT_ps.at(i, NG * FILLS, 2))
                for j in range(NG):
                    act.wait_ge(q_ps.sem, q_ps.at(i, j + 1))
                    nc.scalar.activation(Q["hi"][p][:, 2 * j:2 * j + 2, :],
                                         ps[:, (j + 1) % 2, :].rearrange("p (h t) -> p h t", h=2), ACT.Copy).then_inc(
                        q_hi_ready.sem, 1)
                    if j == 1:
                        yield
                for n in range(2):
                    act.wait_ge(k_ps.sem, k_ps.at(i, n + 1))
                    bank = ps[:, (n + 1) % 2, :].rearrange("p (g t) -> p g t", g=2)
                    for half, rows in enumerate((slice(0, D64), slice(D64, P))):
                        last = nc.scalar.activation(K["hi"][p][rows, half, 2 * n:2 * n + 2, :], bank[rows], ACT.Copy)
                    last.then_inc(k_hi_ready.sem, 1)
                yield from skip(HEAD - 1)
                for j in range(NG):
                    yield from skip(FILLS)
                    act.wait_ge(max_ps.sem, max_ps.at(i, j + 1))
                    pe_bank = j % 2
                    act.wait_ge(sT_ps.sem, sT_ps.at(i, (j + 1) * FILLS, 1))
                    nc.scalar.activation(mrow[j][:, :], ps[0:NG, pe_bank, 0:SEQ], ACT.Copy, scale=-1.0).then_inc(
                        mrow_ready.sem, 1)

            def back(i, p):
                for j in range(NG + 1):
                    for n in range(FILLS):
                        if n == 0 and j > 1:
                            to_sbuf(i, j - 2)
                        if j < NG:
                            if n == 0 and j < 2:
                                act.wait_ge(pv_done.sem, pv_done.at(i, j + 3, 1))
                            elif n == 0:
                                act.wait_ge(pv_done.sem, pv_done.at(i, j - 1))
                            c = j * FILLS + n
                            act.wait_ge(sT_ps.sem, sT_ps.at(i, c + 1))
                            nc.scalar.activation(probs[j % 2][:, n, :], ps[:, 4 + c % 2, :], ACT.Exp,
                                                 scale=SCALE).then_inc(exp_done.sem, 1)
                        yield
                to_sbuf(i, NG - 1)
                yield

            def to_sbuf(i, m):
                act.wait_ge(pv_done.sem, pv_done.at(i, m + 1))
                act.wait_ge(cxT_ready.sem, cxT_ready.at(i, m + 1, 1))
                nc.scalar.activation(craw[:, 2 * m:2 * m + 2, :], ps[:, 6, :].rearrange("p (h t) -> p h t", h=2),
                                     ACT.Copy).then_inc(craw_ready.sem, 1)

            pipeline3(act, front, back, nothing)

        @block.tensor
        def _(pe):
            mm = nc.tensor.matmul
            for s in (yT_ps, q_ps, k_ps, v_ps, score_ps, max_ps, sT_ps, pv_done, recip_ps, out_ps):
                s.credit(pe)
            pe.wait_ge(loaded, 16)
            pe.wait_ge(constants, 3)
            pe.wait_ge(maxima_clear, 1)

            def front(i, p):
                yield
                pe.wait_ge(y_ready.sem, y_ready.at(i, 1))
                pe.wait_ge(mrow_ready.sem, mrow_ready.at(i, NG, 1))
                for t in range(T):
                    last = nc.tensor.transpose(ps[:, 0, t * P:(t + 1) * P], y[p][:, t, :], g.ident[:, :])
                last.then_inc(yT_ps.sem, 1)
                yield
                pe.wait_ge(yT_ready.sem, yT_ready.at(i, 1))
                for j in range(NG):
                    if j >= 2:
                        pe.wait_ge(q_lo_ready.sem, q_lo_ready.at(i, j - 1))
                    for h in range(2):
                        o = 2 * j + h
                        last = mm(ps[:, (j + 1) % 2, h * SEQ:(h + 1) * SEQ], at["wq"][:, o * P:(o + 1) * P], yT[:, :],
                                  start=True, stop=True)
                    last.then_inc(q_ps.sem, 1)
                    if j == 1:
                        yield
                for n in range(2):
                    pe.wait_ge(q_lo_ready.sem, q_lo_ready.at(i, n + 3))
                    for h in range(2):
                        o = 2 * n + h
                        last = mm(ps[:, (n + 1) % 2, h * SEQ:(h + 1) * SEQ], at["wk"][:, o * P:(o + 1) * P], yT[:, :],
                                  start=True, stop=True)
                    last.then_inc(k_ps.sem, 1)
                pe.wait_ge(k_lo_ready.sem, k_lo_ready.at(i, 1))
                for t in range(T):
                    last = mm(ps[:, 1, t * SEQ:(t + 1) * SEQ], yT[:, t * P:(t + 1) * P], at["wv"], start=True, stop=True)
                last.then_inc(v_ps.sem, 1)
                yield from skip(HEAD - 3)
                pe.wait_ge(k_lo_ready.sem, k_lo_ready.at(i, 2))
                for j in range(NG + 1):
                    for n in range(FILLS):
                        if j < NG:
                            c = j * FILLS + n
                            if c < 2:
                                pe.wait_ge(rowmax_ready.sem, rowmax_ready.at(i, NG * FILLS - 1 + c, 1))
                            else:
                                pe.wait_ge(rowmax_ready.sem, rowmax_ready.at(i, c - 1))
                            t, pair = n // 2, 2 * j + n % 2
                            for h in range(2):
                                last = mm(ps[:, 2 + c % 2, h * SEQ:(h + 1) * SEQ], Q["hi"][p][:, pair, t * P:(t + 1) * P],
                                          K["hi"][p][:, h, j, :], start=True, stop=True)
                            last.then_inc(score_ps.sem, 1)
                        if j > 0 and n == 1:
                            m = j - 1
                            pe.wait_ge(rowmax_ready.sem, rowmax_ready.at(i, j * FILLS))
                            if m == 0:
                                pe.wait_ge(k_lo_ready.sem, k_lo_ready.at(i, 2))
                            elif m == 1:
                                pe.wait_ge(v_ready.sem, v_ready.at(i, 1))
                            else:
                                pe.wait_ge(mrow_ready.sem, mrow_ready.at(i, m - 1))
                            for t in range(T):
                                last = nc.tensor.transpose(ps[0:NG, m % 2, t * P:(t + 1) * P], rowmax[:, t, 4 * m:4 * m + 4],
                                                           g.ident[:, :])
                            last.then_inc(max_ps.sem, 1)
                        yield

            def scores(i, p, j, n):
                c = j * FILLS + n
                if c < 2:
                    pe.wait_ge(exp_done.sem, exp_done.at(i, NG * FILLS - 1 + c, 1))
                else:
                    pe.wait_ge(exp_done.sem, exp_done.at(i, c - 1))
                t, pair = n // 2, 2 * j + n % 2
                keys = slice(t * P, (t + 1) * P)
                bank = ps[:, 4 + c % 2, :]
                mm(bank, ones_row[:, :], maxima[:, j, (n % 2) * BANK:(n % 2 + 1) * BANK], start=True, stop=False)
                for h in range(2):
                    o = bank[:, h * SEQ:(h + 1) * SEQ]
                    mm(o, K["hi"][p][:, h, j, keys], Q["hi"][p][:, pair, :], start=False, stop=False)
                    mm(o, K["hi"][p][:, h, j, keys], Q["lo"][p][:, pair, :], start=False, stop=False)
                    last = mm(o, K["lo"][p][:, h, j, keys], Q["hi"][p][:, pair, :], start=False, stop=h == 1)
                last.then_inc(sT_ps.sem, 1)

            def values(i, p, m, u):
                if u == 0:
                    pe.wait_ge(exp_done.sem, exp_done.at(i, (m + 1) * FILLS))
                    if m == 0:
                        pe.wait_ge(cxT_ready.sem, cxT_ready.at(i, NG, 1))
                    else:
                        pe.wait_ge(craw_ready.sem, craw_ready.at(i, m))
                for kt in range(T):
                    for h in range(2):
                        mm(ps[h * D64:(h + 1) * D64, 6, u * SEQ:(u + 1) * SEQ], V[p][:, kt, m, :],
                           probs[m % 2][:, 2 * kt + u, h * SEQ:(h + 1) * SEQ], start=kt == 0, stop=kt == T - 1)
                if u == 1:
                    if m == 0:
                        pe.wait_ge(f_ready.sem, f_ready.at(i, 1, 1))
                    for kt in range(T):
                        for h in range(HG):
                            last = mm(ps[h * COLS:(h + 1) * COLS, 7, 0:SEQ], sum_cols[:, m, :],
                                      probs[m % 2][:, 2 * kt + h // 2, (h % 2) * SEQ:(h % 2 + 1) * SEQ],
                                      start=m == 0 and kt == 0, stop=m == NG - 1 and kt == T - 1)
                    last.then_inc(pv_done.sem, 1)

            def back(i, p):
                for j in range(NG + 1):
                    for n in range(FILLS):
                        if j < NG:
                            if n == 0:
                                pe.wait_ge(mrow_placed[j], i * 16 + 16)
                            scores(i, p, j, n)
                        if j > 0 and n >= 2:
                            values(i, p, j - 1, n - 2)
                        yield

            def finish(i):
                yield
                for j in range(NG + 1):
                    if j < NG:
                        pe.wait_ge(recip_ready.sem, recip_ready.at(i, 1))
                        if j == 0:
                            pe.wait_ge(craw_ready.sem, craw_ready.at(i, NG))
                        else:
                            pe.wait_ge(cxT_ready.sem, cxT_ready.at(i, j))
                        for u in range(2):
                            last = mm(ps[:, 6, u * SEQ:(u + 1) * SEQ], at["spread_sums"][:, (2 * j + u) * P:(2 * j + u + 1) * P],
                                      recip[:, :], start=True, stop=True)
                        last.then_inc(recip_ps.sem, 1)
                    if j > 0:
                        if j == 1:
                            pe.wait_ge(skip_ready.sem, skip_ready.at(i, 1))
                            mm(ps[:, 7, SEQ:2 * SEQ], g.ident[:, :], skip_y[:, :, :].rearrange("p t d -> p (t d)"),
                               start=True, stop=False)
                        pe.wait_ge(cxT_ready.sem, cxT_ready.at(i, j))
                        for pair in (2 * j - 2, 2 * j - 1):
                            for t in range(T):
                                last = mm(ps[:, 7, SEQ + t * P:SEQ + (t + 1) * P], cxT[:, pair, t * P:(t + 1) * P],
                                          at["wpost"][:, pair * P:(pair + 1) * P], start=False,
                                          stop=pair == PAIRS - 1 and t == T - 1)
                        if j == NG:
                            last.then_inc(out_ps.sem, 1)
                    yield

            pipeline3(pe, front, back, finish)


ATT8 = {
    0: [("wqk", 2 * P), ("wv", P), ("wo", P), ("vb", P), ("ob", P), ("qkb", 2)],
    1: [("wqk", 2 * P), ("wrot", 2 * P), ("wv", P), ("wo", P), ("ob", P), ("cos", 2 * SEQ), ("sin", 2 * SEQ)],
}


class Globals:
    pass


def expert_shapes(layer):
    return ("gu", [P, NE, 2 * F_EXP[layer]]), ("down", [P, NE, FC, P])


def expert_raw(nc, ctx, layer):
    raw = {k: ctx.enter_context(nc.sbuf_tensor(f"e{layer}_{k}_raw", shape, F32)) for k, shape in expert_shapes(layer)}
    raw["loaded"] = ctx.enter_context(nc.semaphore(f"e{layer}_loaded"))
    return raw


def expert_weights(nc, ctx, layer):
    return {f"{k}_{part}": ctx.enter_context(nc.sbuf_tensor(f"e{layer}_{k}_{part}", shape, F32R))
            for part in ("hi", "lo") for k, shape in expert_shapes(layer)}


def program(nc, a, out_dram, only=None):
    g = Globals()
    with ExitStack() as ctx:
        def sb(name, shape, dt=F32):
            return ctx.enter_context(nc.sbuf_tensor(name, shape, dt))

        g.x = sb("x", [P, TILES, P])
        g.ident = sb("ident", [P, P])
        g.minus_half = sb("minus_half", [P, 8])
        g.plus_half = sb("plus_half", [P, 32])
        g.ones_rows = sb("ones_rows", [P, 1])
        g.spread, g.masks, g.pick = sb("spread", a["spread"].shape), sb("masks", a["masks"].shape), sb("pick", a["pick"].shape)
        early, late = ("att0", "moe0", "att1", "ffn1"), ("att2", "ffn2", "att3", "moe3")
        g.w = {k: sb(f"w_{k}", a[k].shape) for k in early}
        g.loaded = {k: ctx.enter_context(nc.semaphore(f"loaded_{k}")) for k in early + late + ("shared",)}
        first = ctx.enter_context(ExitStack())
        raw = expert_raw(nc, first, 0)

        def load_small(sp, names):
            for k in names:
                sp.dma_start(g.w[k][:, :], a[k]).then_inc(g.loaded[k], 16)

        with nc.semaphore("x_loaded") as x_loaded, nc.Block() as block:
            @block.sync
            def _(sp):
                sp.dma_start(g.x[:, :, :], a["x"].rearrange("b (t p) d -> p (b t) d", p=P)).then_inc(x_loaded, 16)
                sp.dma_start(g.ident[:, :], a["ident"]).then_inc(x_loaded, 16)
                sp.dma_start(g.ones_rows[:, :], a["ones_rows"]).then_inc(x_loaded, 16)
                sp.dma_start(g.w["att0"][:, :], a["att0"]).then_inc(g.loaded["att0"], 16)
                sp.dma_start(g.spread[:, :, :], a["spread"]).then_inc(g.loaded["shared"], 16)
                sp.dma_start(g.masks[:, :, :], a["masks"]).then_inc(g.loaded["shared"], 16)
                sp.dma_start(g.pick[:, :], a["pick"]).then_inc(g.loaded["shared"], 16)
                load_small(sp, early[1:])
                load_experts(sp, 0, a["gu0"], a["down0"], raw)
                sp.wait_ge(x_loaded, 48)

            @block.vector
            def _(dve):
                nc.vector.memset(g.minus_half[:, :], -0.5)
                nc.vector.memset(g.plus_half[:, :], 0.5)

        n = 99 if only is None else only
        if n > 0:
            attention8(nc, g, 0, "att0")
        if n > 1:
            w0 = expert_weights(nc, first, 0)
            split_experts(nc, g, 0, raw, w0)
            experts(nc, g, 0, "moe0", w0)
        first.close()
        g.w |= {k: sb(f"w_{k}", a[k].shape) for k in late}
        if n > 2:
            attention8(nc, g, 1, "att1", prefetch=lambda sp: load_small(sp, late))
        if n > 3:
            selected_ffn(nc, g, 1, "ffn1", a["experts1"])
        if n > 4:
            grouped_attention(nc, g, "att2")
        w3 = expert_weights(nc, ctx, 3)
        second = ctx.enter_context(ExitStack())
        raw3 = expert_raw(nc, second, 3)
        if n > 5:
            selected_ffn(nc, g, 2, "ffn2", a["experts2"],
                         prefetch=lambda pool: load_experts(pool, 3, a["gu3"], a["down3"], raw3))
        if n > 6:
            channel_attention(nc, g, "att3")
        if n > 7:
            split_experts(nc, g, 3, raw3, w3)
            second.close()
            experts(nc, g, 3, "moe3", w3)

        with nc.semaphore("x_stored") as x_stored, nc.Block() as block:
            @block.sync
            def _(sp):
                sp.dma_start(out_dram.rearrange("b (t p) d -> p (b t) d", p=P), g.x[:, :, :]).then_inc(x_stored, 16)
                sp.wait_ge(x_stored, 16)


def packed(inputs):
    f32 = lambda k: np.asarray(inputs[k], np.float32)
    rows = lambda v: np.broadcast_to(v, (P, v.shape[-1]))
    cols = lambda v: v.reshape(-1, P).T
    a = {"x": f32("L0_attn_x"), "ident": np.eye(P, dtype=np.float32)}
    spread = np.zeros((P, 16, P), np.float32)
    ones = np.zeros((P, 1), np.float32)
    parts = [(0, (0, 16)), (4, (8,)), (8, (0, 8)), (12, (16,))]
    for first, places in parts:
        for blk in range(NG):
            for j in range(NG):
                for d in range(D8):
                    for at in places:
                        spread[(4 * j + blk) * D8 + d, first + blk, 32 * j + at + d] = 1.0
    for j in range(NG):
        ones[32 * j + ROWS, 0] = 1.0
    a["spread"], a["ones_rows"] = spread, ones
    pick = np.zeros((HG, 32, HG, D8 + 1), np.float32)
    for h in range(HG):
        pick[h, 0:D8 + 1, h] = np.eye(D8 + 1)
    a["pick"] = pick.reshape(P, HG * (D8 + 1))
    r = np.arange(P)
    m = np.where(r[None, :] > r[:, None], MASKED, 0.0)
    z = np.zeros((P, P))
    a["masks"] = np.stack([np.hstack(v) for v in ([m] * 4, [z, m, z, m], [m.T, z, m.T, z], [m.T] * 4)],
                          axis=1).astype(np.float32)
    a["att0"] = np.hstack([f32("L0_attn_qkv_w"), f32("L0_attn_out_w"), rows(f32("L0_attn_qkv_b")[2 * P:]),
                           rows(f32("L0_attn_out_b")), cols(f32("L0_attn_qkv_b")[:2 * P])])
    qkv1 = f32("L1_attn_w_qkv")
    theta = (1.0 / 10000.0 ** (np.arange(0, D8, 2, dtype=np.float32) / D8)).astype(np.float32)
    angles = np.outer(np.arange(SEQ, dtype=np.float32), theta).astype(np.float32).T
    sign = np.repeat(np.array([-1.0, 1.0], np.float32), D8 // 2)[:, None]
    cos = np.tile(np.cos(np.vstack([angles, angles])), (NH, 2)).astype(np.float32)
    sin = np.tile(sign * np.sin(np.vstack([angles, angles])), (NH, 2)).astype(np.float32)
    turned = qkv1[:, :2 * P].reshape(P, 2 * NH, 2, D8 // 2)[:, :, ::-1].reshape(P, 2 * P)
    a["att1"] = np.hstack([qkv1[:, :2 * P], turned, qkv1[:, 2 * P:], f32("L1_attn_w_out"), rows(f32("L1_attn_b_out")),
                           cos, sin])
    for k in (1, 2):
        c = lambda n: f32(f"L{k}_ffn_{n}")
        a[f"ffn{k}"] = np.hstack([c("Wp1"), cols(c("bp1")), c("Wp2"), rows(c("bp2")), c("Wo"), rows(c("bo"))])
        w2 = c("W2").reshape(NE, 2, P, P).transpose(0, 2, 1, 3).reshape(NE, P, 2 * P)
        a[f"experts{k}"] = np.concatenate([c("W1"), w2, c("b1").reshape(NE, 2, P).transpose(0, 2, 1),
                                           c("b2")[:, :, None]], axis=2)
    wk = f32("L2_attn_Wk").reshape(P, NG, 1, D64)
    post = f32("L2_attn_Wpost").reshape(NH // 2, P, P).transpose(1, 0, 2).reshape(P, NH * D64)
    spread_sums = np.zeros((P, NG, 2, 2, D64), np.float32)
    for j in range(NG):
        for h in range(HG):
            spread_sums[32 * h + j, j, h // 2, h % 2] = 1.0
    a["att2"] = np.hstack([f32("L2_attn_Wq"), np.broadcast_to(wk, (P, NG, 2, D64)).reshape(P, NG * P),
                           f32("L2_attn_Wv"), post, spread_sums.reshape(P, -1)])
    head = np.arange(P) // D8
    blocks = np.where(head[:, None] == head[None, :], 0.0, MASKED).astype(np.float32)
    a["att3"] = np.hstack([f32("L3_attn_Wq").T, f32("L3_attn_Wk").T, f32("L3_attn_Wv").T, f32("L3_attn_Wo").T, blocks])
    iota = rows(np.arange(NE, dtype=np.float32))
    t = lambda k: f32(k).T
    pad = lambda v, n: np.pad(v, [(0, n - v.shape[0])] + [(0, 0)] * (v.ndim - 1))
    gate0, up0, down0 = (np.concatenate([f32(f"L0_ffn_r{c}"), f32(f"L0_ffn_s{c}")[None]]) for c in "gud")
    a["gu0"] = np.concatenate([gate0.transpose(0, 2, 1), up0.transpose(0, 2, 1)], axis=2)
    a["down0"] = down0.transpose(0, 2, 1)
    logit_bias = np.full((NE,), MASKED, np.float32)
    logit_bias[:NE - 1] = f32("L0_ffn_rb")
    twice = lambda v: pad(np.concatenate([pad(v, 32), v]), P)
    pick_expert = twice(np.repeat(np.eye(NE, dtype=np.float32), P, axis=1))
    a["moe0"] = np.hstack([pad(f32("L0_ffn_wr"), NE).T, rows(logit_bias), iota, pick_expert])
    a["gu3"] = np.concatenate([f32("L3_ffn_Wg"), f32("L3_ffn_W1")], axis=2)
    a["down3"] = f32("L3_ffn_W2")

    def chunks(b):
        b = np.pad(b, ((0, 0), (0, FC * P - b.shape[1])))
        return b.reshape(NE * FC, P).T

    a["moe3"] = np.hstack([t("L3_ffn_centroid"), iota, pick_expert, chunks(f32("L3_ffn_bg")), chunks(f32("L3_ffn_b1")),
                           twice(f32("L3_ffn_b2"))])
    return a


def kernel(**inputs):
    import concourse.bacc as bacc
    from concourse.bass_utils import run_bass_kernel_spmd

    nc = bacc.Bacc("TRN2", target_bir_lowering=False, num_devices=1)
    a = {k: np.ascontiguousarray(v) for k, v in packed(inputs).items()}
    shape = (SEQS, SEQ, P)
    aps = {k: nc.dram_tensor(f"in_{k}", v.shape, mybir.dt.from_np(v.dtype), kind="ExternalInput").ap() for k, v in a.items()}
    out = nc.dram_tensor("out", shape, F32, kind="ExternalOutput").ap()
    program(nc, aps, out)
    r = run_bass_kernel_spmd(nc, [{f"in_{k}": v for k, v in a.items()}], core_ids=[0])
    return r.results[0]["out"]
```
